# Optimizing a Trainium2 kernel written in Bass

```python
import numpy as np
import jax
import jax.numpy as jnp

def _softmax(x, axis=-1):
    return jax.nn.softmax(x, axis=axis)

def _gelu(x):
    return jax.nn.gelu(x, approximate=True)

def _silu(x):
    return jax.nn.silu(x)

def _sigmoid(x):
    return jax.nn.sigmoid(x)

def _layernorm(x, axis=-1, eps=1e-05):
    m = jnp.mean(x, axis=axis, keepdims=True)
    v = jnp.var(x, axis=axis, keepdims=True)
    return (x - m) / jnp.sqrt(v + eps)

def _scatter_add(tgt, idx, src, axis=0):
    return tgt.at[idx].add(src)

def _segment_sum(src, seg, n):
    return jax.ops.segment_sum(src, seg, n)
kernel_name = 'mk_seq_postln_d1_jaxref_r8_ed64c2'

def setup_inputs(seed: int=0):
    np.random.seed(seed)
    _w = jnp.asarray

    def _L0_attn_setup():
        import jax, jax.numpy as jnp
        import numpy as np
        from jax import lax
        HID = 128
        NH = 16
        NKV = 4
        HD = 64
        SPLIT = 64
        KS = 3

        def _dynamic_conv(x, w_kgen, b_kgen, w_conv, b_conv):
            context = x.mean(axis=1)
            dyn = context @ w_kgen.T + b_kgen
            gate = jax.nn.sigmoid(dyn).mean(axis=1)
            x_t = x.transpose(0, 2, 1)
            y = lax.conv_general_dilated(x_t, w_conv, window_strides=(1,), padding=[(KS // 2, KS // 2)], feature_group_count=HID, dimension_numbers=('NCH', 'OIH', 'NCH'))
            y = (y + b_conv[None, :, None]) * gate[:, None, None]
            return y.transpose(0, 2, 1)

        def _fixed_split_attention(x, w_q, w_k, w_v, w_o):
            B, S, _ = x.shape
            q = (x @ w_q.T).reshape(B, S, NH, HD).transpose(0, 2, 1, 3)
            k = (x @ w_k.T).reshape(B, S, NKV, HD).transpose(0, 2, 1, 3)
            v = (x @ w_v.T).reshape(B, S, NKV, HD).transpose(0, 2, 1, 3)
            n_rep = NH // NKV
            k = jnp.repeat(k, n_rep, axis=1)
            v = jnp.repeat(v, n_rep, axis=1)
            C = S // SPLIT
            kc = k.reshape(B, NH, C, SPLIT, HD)
            vc = v.reshape(B, NH, C, SPLIT, HD)
            scale = HD ** (-0.5)
            scores = jnp.einsum('bhqd,bhckd->bhcqk', q, kc) * scale
            w = jax.nn.softmax(scores.astype(jnp.float32), axis=-1).astype(q.dtype)
            chunk_out = jnp.einsum('bhcqk,bhckd->bhcqd', w, vc)
            sum_w = w.sum(axis=-1, keepdims=True)
            combined = (chunk_out * sum_w).sum(axis=2)
            total = sum_w.sum(axis=2)
            out = combined / (total + 1e-09)
            out = out.transpose(0, 2, 1, 3).reshape(B, S, NH * HD)
            return out @ w_o.T
        key = jax.random.key(seed)
        ks = jax.random.split(key, 9)
        s = 0.02
        return {'hidden_states': jax.random.normal(ks[0], (2, 256, HID), jnp.float32), 'w_q': jax.random.normal(ks[1], (NH * HD, HID), jnp.float32) * s, 'w_k': jax.random.normal(ks[2], (NKV * HD, HID), jnp.float32) * s, 'w_v': jax.random.normal(ks[3], (NKV * HD, HID), jnp.float32) * s, 'w_o': jax.random.normal(ks[4], (HID, NH * HD), jnp.float32) * s, 'w_kgen': jax.random.normal(ks[5], (KS, HID), jnp.float32) * s, 'b_kgen': jnp.zeros((KS,), jnp.float32), 'w_conv': jax.random.normal(ks[6], (HID, 1, KS), jnp.float32) * s, 'b_conv': jnp.zeros((HID,), jnp.float32)}
    _L0_attn_in = _L0_attn_setup()

    def _L0_ffn_setup():
        import jax, jax.numpy as jnp
        import numpy as np
        DIM = 128
        DEPTH = 2
        HEADS = 8
        DIM_HEAD = 64
        WINDOW = 64
        INNER = HEADS * DIM_HEAD
        HID = int(DIM * 4 * 2 / 3)
        B, N = (2, 1024)
        QK_SCALE = 8.0

        def shift_token(t):
            t1, t2 = jnp.split(t, 2, axis=-1)
            t2 = jnp.pad(t2, ((0, 0), (1, 0), (0, 0)))[:, :-1]
            return jnp.concatenate([t1, t2], axis=-1)

        def l2norm(t):
            return t / jnp.clip(jnp.linalg.norm(t, axis=-1, keepdims=True), 1e-12)

        def rotate_half(x):
            x1, x2 = jnp.split(x, 2, axis=-1)
            return jnp.concatenate([-x2, x1], axis=-1)

        def rotary_xpos(q, k):
            n = q.shape[-2]
            half_idx = jnp.arange(0, DIM_HEAD, 2, dtype=jnp.float32)
            inv_freq = 1.0 / 10000.0 ** (half_idx / DIM_HEAD)
            t = jnp.arange(n, dtype=jnp.float32)
            freqs = t[:, None] * inv_freq[None, :]
            freqs = jnp.concatenate([freqs, freqs], axis=-1)
            base = (half_idx + 0.4 * DIM_HEAD) / (1.4 * DIM_HEAD)
            power = (t - n // 2) / float(WINDOW // 2)
            scale = base[None, :] ** power[:, None]
            scale = jnp.concatenate([scale, scale], axis=-1)
            cos, sin = (jnp.cos(freqs), jnp.sin(freqs))
            q = q * cos * scale + rotate_half(q) * sin * scale
            k = k * cos / scale + rotate_half(k) * sin / scale
            return (q, k)

        def local_attention(q, k, v):
            b, h, n, d = q.shape
            w = n // WINDOW
            bq = q.reshape(b, h, w, WINDOW, d) * QK_SCALE
            bk = k.reshape(b, h, w, WINDOW, d)
            bv = v.reshape(b, h, w, WINDOW, d)

            def look_around(t):
                p = jnp.pad(t, ((0, 0), (0, 0), (1, 0), (0, 0), (0, 0)))
                return jnp.concatenate([p[:, :, :w], p[:, :, 1:]], axis=3)
            bk, bv = (look_around(bk), look_around(bv))
            bt = jnp.arange(n).reshape(w, WINDOW)
            btp = jnp.pad(bt, ((1, 0), (0, 0)), constant_values=-1)
            btk = jnp.concatenate([btp[:w], btp[1:]], axis=1)
            sim = jnp.einsum('bhwid,bhwjd->bhwij', bq, bk)
            i = bt[:, :, None]
            j = btk[:, None, :]
            mask = (i < j) | (i > j + WINDOW) | (j == -1)
            sim = jnp.where(mask, -jnp.finfo(sim.dtype).max, sim)
            attn = jax.nn.softmax(sim, axis=-1)
            out = jnp.einsum('bhwij,bhwjd->bhwid', attn, bv)
            return out.reshape(b, h, n, d)

        def _layer(x, wqkv, qs, ksc, wo, lg, lb, w1, b1, w2, b2):
            b, n, _ = x.shape
            h = shift_token(x)
            qkv = h @ wqkv
            q, k, v = jnp.split(qkv, 3, axis=-1)
            to_heads = lambda t: t.reshape(b, n, HEADS, DIM_HEAD).transpose(0, 2, 1, 3)
            q, k, v = (to_heads(q), to_heads(k), to_heads(v))
            q = l2norm(q) * qs
            k = l2norm(k) * ksc
            q, k = rotary_xpos(q, k)
            o = local_attention(q, k, v)
            o = o.transpose(0, 2, 1, 3).reshape(b, n, INNER)
            x = x + o @ wo
            h = shift_token(x)
            mu = h.mean(-1, keepdims=True)
            var = h.var(-1, keepdims=True)
            h = (h - mu) / jnp.sqrt(var + 1e-05) * lg + lb
            h = h @ w1 + b1
            a, g = jnp.split(h, 2, axis=-1)
            h = a * jax.nn.gelu(g, approximate=False)
            x = x + h @ w2 + b2
            return x
        key = jax.random.key(seed)
        ks = jax.random.split(key, 6)
        return {'x': jax.random.normal(ks[0], (B, N, DIM), jnp.float32), 'wqkv': jax.random.normal(ks[1], (DEPTH, DIM, 3 * INNER), jnp.float32) * 0.02, 'q_scale': jnp.ones((DEPTH, DIM_HEAD), jnp.float32), 'k_scale': jnp.ones((DEPTH, DIM_HEAD), jnp.float32), 'wo': jax.random.normal(ks[2], (DEPTH, INNER, DIM), jnp.float32) * 0.02, 'ln_g': jnp.ones((DEPTH, DIM), jnp.float32), 'ln_b': jnp.zeros((DEPTH, DIM), jnp.float32), 'w1': jax.random.normal(ks[3], (DEPTH, DIM, 2 * HID), jnp.float32) * 0.02, 'b1': jnp.zeros((DEPTH, 2 * HID), jnp.float32), 'w2': jax.random.normal(ks[4], (DEPTH, HID, DIM), jnp.float32) * 0.02, 'b2': jnp.zeros((DEPTH, DIM), jnp.float32)}
    _L0_ffn_in = _L0_ffn_setup()
    _d = {'L0_attn_hidden_states': _L0_attn_in['hidden_states'], 'L0_attn_w_q': _L0_attn_in['w_q'], 'L0_attn_w_k': _L0_attn_in['w_k'], 'L0_attn_w_v': _L0_attn_in['w_v'], 'L0_attn_w_o': _L0_attn_in['w_o'], 'L0_attn_w_kgen': _L0_attn_in['w_kgen'], 'L0_attn_b_kgen': _L0_attn_in['b_kgen'], 'L0_attn_w_conv': _L0_attn_in['w_conv'], 'L0_attn_b_conv': _L0_attn_in['b_conv'], 'L0_ffn_wqkv': _L0_ffn_in['wqkv'], 'L0_ffn_q_scale': _L0_ffn_in['q_scale'], 'L0_ffn_k_scale': _L0_ffn_in['k_scale'], 'L0_ffn_wo': _L0_ffn_in['wo'], 'L0_ffn_ln_g': _L0_ffn_in['ln_g'], 'L0_ffn_ln_b': _L0_ffn_in['ln_b'], 'L0_ffn_w1': _L0_ffn_in['w1'], 'L0_ffn_b1': _L0_ffn_in['b1'], 'L0_ffn_w2': _L0_ffn_in['w2'], 'L0_ffn_b2': _L0_ffn_in['b2']}
    _x0 = _d['L0_attn_hidden_states']
    _d['L0_attn_hidden_states'] = jax.random.normal(jax.random.fold_in(jax.random.key(seed), 1), (16, 256, 128), dtype=_x0.dtype)
    del _x0
    return _d

def reference(L0_attn_hidden_states, L0_attn_w_q, L0_attn_w_k, L0_attn_w_v, L0_attn_w_o, L0_attn_w_kgen, L0_attn_b_kgen, L0_attn_w_conv, L0_attn_b_conv, L0_ffn_wqkv, L0_ffn_q_scale, L0_ffn_k_scale, L0_ffn_wo, L0_ffn_ln_g, L0_ffn_ln_b, L0_ffn_w1, L0_ffn_b1, L0_ffn_w2, L0_ffn_b2):

    def _L0_attn_ref(hidden_states, w_q, w_k, w_v, w_o, w_kgen, b_kgen, w_conv, b_conv):
        import jax, jax.numpy as jnp
        import numpy as np
        from jax import lax
        HID = 128
        NH = 16
        NKV = 4
        HD = 64
        SPLIT = 64
        KS = 3

        def _dynamic_conv(x, w_kgen, b_kgen, w_conv, b_conv):
            context = x.mean(axis=1)
            dyn = context @ w_kgen.T + b_kgen
            gate = jax.nn.sigmoid(dyn).mean(axis=1)
            x_t = x.transpose(0, 2, 1)
            y = lax.conv_general_dilated(x_t, w_conv, window_strides=(1,), padding=[(KS // 2, KS // 2)], feature_group_count=HID, dimension_numbers=('NCH', 'OIH', 'NCH'))
            y = (y + b_conv[None, :, None]) * gate[:, None, None]
            return y.transpose(0, 2, 1)

        def _fixed_split_attention(x, w_q, w_k, w_v, w_o):
            B, S, _ = x.shape
            q = (x @ w_q.T).reshape(B, S, NH, HD).transpose(0, 2, 1, 3)
            k = (x @ w_k.T).reshape(B, S, NKV, HD).transpose(0, 2, 1, 3)
            v = (x @ w_v.T).reshape(B, S, NKV, HD).transpose(0, 2, 1, 3)
            n_rep = NH // NKV
            k = jnp.repeat(k, n_rep, axis=1)
            v = jnp.repeat(v, n_rep, axis=1)
            C = S // SPLIT
            kc = k.reshape(B, NH, C, SPLIT, HD)
            vc = v.reshape(B, NH, C, SPLIT, HD)
            scale = HD ** (-0.5)
            scores = jnp.einsum('bhqd,bhckd->bhcqk', q, kc) * scale
            w = jax.nn.softmax(scores.astype(jnp.float32), axis=-1).astype(q.dtype)
            chunk_out = jnp.einsum('bhcqk,bhckd->bhcqd', w, vc)
            sum_w = w.sum(axis=-1, keepdims=True)
            combined = (chunk_out * sum_w).sum(axis=2)
            total = sum_w.sum(axis=2)
            out = combined / (total + 1e-09)
            out = out.transpose(0, 2, 1, 3).reshape(B, S, NH * HD)
            return out @ w_o.T
        h = _dynamic_conv(hidden_states, w_kgen, b_kgen, w_conv, b_conv)
        return _fixed_split_attention(h, w_q, w_k, w_v, w_o)

    def _L0_ffn_ref(x, wqkv, q_scale, k_scale, wo, ln_g, ln_b, w1, b1, w2, b2):
        import jax, jax.numpy as jnp
        import numpy as np
        DIM = 128
        DEPTH = 2
        HEADS = 8
        DIM_HEAD = 64
        WINDOW = 64
        INNER = HEADS * DIM_HEAD
        HID = int(DIM * 4 * 2 / 3)
        B, N = (2, 1024)
        QK_SCALE = 8.0

        def shift_token(t):
            t1, t2 = jnp.split(t, 2, axis=-1)
            t2 = jnp.pad(t2, ((0, 0), (1, 0), (0, 0)))[:, :-1]
            return jnp.concatenate([t1, t2], axis=-1)

        def l2norm(t):
            return t / jnp.clip(jnp.linalg.norm(t, axis=-1, keepdims=True), 1e-12)

        def rotate_half(x):
            x1, x2 = jnp.split(x, 2, axis=-1)
            return jnp.concatenate([-x2, x1], axis=-1)

        def rotary_xpos(q, k):
            n = q.shape[-2]
            half_idx = jnp.arange(0, DIM_HEAD, 2, dtype=jnp.float32)
            inv_freq = 1.0 / 10000.0 ** (half_idx / DIM_HEAD)
            t = jnp.arange(n, dtype=jnp.float32)
            freqs = t[:, None] * inv_freq[None, :]
            freqs = jnp.concatenate([freqs, freqs], axis=-1)
            base = (half_idx + 0.4 * DIM_HEAD) / (1.4 * DIM_HEAD)
            power = (t - n // 2) / float(WINDOW // 2)
            scale = base[None, :] ** power[:, None]
            scale = jnp.concatenate([scale, scale], axis=-1)
            cos, sin = (jnp.cos(freqs), jnp.sin(freqs))
            q = q * cos * scale + rotate_half(q) * sin * scale
            k = k * cos / scale + rotate_half(k) * sin / scale
            return (q, k)

        def local_attention(q, k, v):
            b, h, n, d = q.shape
            w = n // WINDOW
            bq = q.reshape(b, h, w, WINDOW, d) * QK_SCALE
            bk = k.reshape(b, h, w, WINDOW, d)
            bv = v.reshape(b, h, w, WINDOW, d)

            def look_around(t):
                p = jnp.pad(t, ((0, 0), (0, 0), (1, 0), (0, 0), (0, 0)))
                return jnp.concatenate([p[:, :, :w], p[:, :, 1:]], axis=3)
            bk, bv = (look_around(bk), look_around(bv))
            bt = jnp.arange(n).reshape(w, WINDOW)
            btp = jnp.pad(bt, ((1, 0), (0, 0)), constant_values=-1)
            btk = jnp.concatenate([btp[:w], btp[1:]], axis=1)
            sim = jnp.einsum('bhwid,bhwjd->bhwij', bq, bk)
            i = bt[:, :, None]
            j = btk[:, None, :]
            mask = (i < j) | (i > j + WINDOW) | (j == -1)
            sim = jnp.where(mask, -jnp.finfo(sim.dtype).max, sim)
            attn = jax.nn.softmax(sim, axis=-1)
            out = jnp.einsum('bhwij,bhwjd->bhwid', attn, bv)
            return out.reshape(b, h, n, d)

        def _layer(x, wqkv, qs, ksc, wo, lg, lb, w1, b1, w2, b2):
            b, n, _ = x.shape
            h = shift_token(x)
            qkv = h @ wqkv
            q, k, v = jnp.split(qkv, 3, axis=-1)
            to_heads = lambda t: t.reshape(b, n, HEADS, DIM_HEAD).transpose(0, 2, 1, 3)
            q, k, v = (to_heads(q), to_heads(k), to_heads(v))
            q = l2norm(q) * qs
            k = l2norm(k) * ksc
            q, k = rotary_xpos(q, k)
            o = local_attention(q, k, v)
            o = o.transpose(0, 2, 1, 3).reshape(b, n, INNER)
            x = x + o @ wo
            h = shift_token(x)
            mu = h.mean(-1, keepdims=True)
            var = h.var(-1, keepdims=True)
            h = (h - mu) / jnp.sqrt(var + 1e-05) * lg + lb
            h = h @ w1 + b1
            a, g = jnp.split(h, 2, axis=-1)
            h = a * jax.nn.gelu(g, approximate=False)
            x = x + h @ w2 + b2
            return x
        for l in range(DEPTH):
            x = _layer(x, wqkv[l], q_scale[l], k_scale[l], wo[l], ln_g[l], ln_b[l], w1[l], b1[l], w2[l], b2[l])
        return x
    x = L0_attn_hidden_states
    x = _layernorm(x + _L0_attn_ref(x, L0_attn_w_q, L0_attn_w_k, L0_attn_w_v, L0_attn_w_o, L0_attn_w_kgen, L0_attn_b_kgen, L0_attn_w_conv, L0_attn_b_conv), axis=-1)
    x = _layernorm(x + _L0_ffn_ref(x, L0_ffn_wqkv, L0_ffn_q_scale, L0_ffn_k_scale, L0_ffn_wo, L0_ffn_ln_g, L0_ffn_ln_b, L0_ffn_w1, L0_ffn_b1, L0_ffn_w2, L0_ffn_b2), axis=-1)
    return x

_drawn_inputs = setup_inputs


def setup_inputs(seed=0):
    import zlib

    import numpy as np

    out = dict(_drawn_inputs(seed))
    spreads = {'L0_attn_b_kgen': (0.0, 0.8),
     'L0_attn_b_conv': (0.0, 0.8),
     'L0_ffn_q_scale': (1.0, 0.6),
     'L0_ffn_k_scale': (1.0, 0.6),
     'L0_ffn_ln_g': (1.0, 0.6),
     'L0_ffn_ln_b': (0.0, 0.8),
     'L0_ffn_b1': (0.0, 0.8),
     'L0_ffn_b2': (0.0, 0.8)}
    factors = {'L0_attn_w_q': 8.0,
     'L0_attn_w_k': 24.86,
     'L0_attn_w_v': 8.0,
     'L0_attn_w_o': 7.907,
     'L0_attn_w_kgen': 64.0,
     'L0_attn_w_conv': 8.0,
     'L0_ffn_wqkv': 3.406,
     'L0_ffn_wo': 3.415,
     'L0_ffn_w1': 6.212,
     'L0_ffn_w2': 6.122}
    for name, (base, spread) in spreads.items():
        noise = np.random.default_rng([zlib.crc32(name.encode()), seed]).standard_normal(out[name].shape)
        drawn = base * np.exp(spread * noise) if base else spread * noise
        out[name] = jnp.asarray(drawn.astype(out[name].dtype))
    for name, factor in factors.items():
        out[name] = (out[name] * factor).astype(out[name].dtype)
    return out
```

```python
import concourse.bass as bass
from concourse import mybir
from contextlib import ExitStack
import math

import numpy as np

FP32 = mybir.dt.float32
BF16 = mybir.dt.bfloat16
ALU = mybir.AluOpType
ACT = mybir.ActivationFunctionType
AX = mybir.AxisListType

BATCH, SEQ, DIM = 16, 256, 128
P = 128
TILES = SEQ // P
A_HEADS, A_KV, A_HD = 16, 4, 64
A_REP = A_HEADS // A_KV
CHUNK = 64
CHUNKS = SEQ // CHUNK
KS = 3
LAYERS, F_HEADS, F_HD, WINDOW = 2, 8, 64, 64
INNER = F_HEADS * F_HD
F_HID = int(DIM * 4 * 2 / 3)
LN_EPS = 1e-5

PAIR = 2
TURNS = BATCH // PAIR
A_SLOTS = PAIR * TILES
A_STEPS = A_SLOTS * A_KV
E_RING = 8
EXP_LAG, SUM_LAG, NORM_LAG, PV_LAG, OUT_LAG, LN_LAG = 1, 2, 5, 7, 11, 14
F_GROUPS = 2
F_GH = F_HEADS // F_GROUPS
F_SLOTS = PAIR * TILES
F_STEPS = F_SLOTS * F_GROUPS
F_PV_LAG, F_OT_LAG, F_OUT_LAG = 3, 5, 6
F_KEYS = P + WINDOW
F_RING = 4
F_CHUNKS = -(-F_HID // P)
F_ROWS = [min(P, F_HID - P * c) for c in range(F_CHUNKS)]
QK_SCALE = 8.0
MASKED = -1e30


def wait(engine, sem, value):
    if isinstance(value, int) and value <= 0:
        return
    engine.wait_ge(sem, value)


class SharedBanks:

    BEFORE = {"drain": "last", "last": "middle", "middle": "middle", "first": "pre"}

    def __init__(self, order, pre, stride, late):
        assert len(order) % 2 == 0
        self.order, self.pre, self.stride, self.late = order, pre, stride, late

    def bank(self, kind, local, turn):
        if turn == "pre":
            return (self.pre.index((kind, local)) + len(self.pre)) % 2
        return self.order.index((kind, local)) % 2

    def left_out(self, turn, kind, local):
        if kind in self.late:
            return turn == "first" and local < 0 or turn == "drain" and local >= 0
        return turn == "drain" or turn == "last" and local // (self.stride[kind] // PAIR) >= PAIR

    def before(self, kind, local, turn):
        if turn == "pre":
            at = self.pre.index((kind, local)) - 2
            return (*self.pre[at], 0) if at >= 0 else None
        back, shift, at = self.order.index((kind, local)) - 2, 0, turn
        while True:
            if back < 0:
                at, shift, back = self.BEFORE[at], shift - 1, back + len(self.order)
                if at == "pre":
                    same = [f for f in self.pre if self.bank(*f, "pre") == back % 2]
                    return (*same[-1], 0)
            if not self.left_out(at, *self.order[back]):
                return (*self.order[back], shift)
            back -= 2


def stage_a_banks():
    order = []
    for s in range(A_STEPS):
        slot, g = divmod(s, A_KV)
        p, tile = divmod(slot, TILES)
        if tile == 0 and g == 0:
            order.append(("xT", p + 1))
        if tile == 0 and g == 2:
            order.append(("gate", p + 1))
        if tile == 1:
            order += [(k, per * (p + 1) + m) for k, per, m in A_PROJECTIONS[g]]
        order.append(("o", s - PV_LAG))
        if g == OUT_LAG % A_KV:
            order.append(("out", (s - OUT_LAG) // A_KV))
    pre = [("xT", 0), ("gate", 0)] + [(k, m) for g in range(A_KV) for k, per, m in A_PROJECTIONS[g]]
    stride = {"xT": PAIR, "gate": PAIR, "k": 2 * PAIR, "q": 4 * PAIR, "v": PAIR, "o": A_STEPS, "out": A_SLOTS}
    return SharedBanks(order, pre, stride, ("o", "out"))


A_PROJECTIONS = {0: [], 1: [("k", 2, 0), ("k", 2, 1), ("q", 4, 0)], 2: [("q", 4, 1), ("q", 4, 2)], 3: [("q", 4, 3), ("v", 1, 0)]}


def stage_f_banks():
    order = []
    for s in range(F_STEPS):
        p, at = divmod(s, TILES * F_GROUPS)
        for kind, per, m, ahead in F_FILLS[at]:
            if kind in ("oT", "out"):
                order.append((kind, (s - (F_OT_LAG if kind == "oT" else F_OUT_LAG)) // F_GROUPS))
            else:
                order.append((kind, per * (p + ahead) + m))
    prepared = [(k, per, m) for at in range(4) for k, per, m, ahead in F_FILLS[at] if ahead == 1]
    pre = [("hT", 0)] + [(k, m) for kind in ("qk", "v", "qkT") for k, per, m in prepared if k == kind] + [("hT", 1)]
    stride = {"hT": PAIR, "qk": 4 * PAIR, "v": 2 * PAIR, "qkT": 4 * PAIR, "oT": F_SLOTS, "out": F_SLOTS}
    return SharedBanks(order, pre, stride, ("oT", "out"))


F_FILLS = {
    0: [("out", 2, 0, 0), ("qk", 4, 0, 1)],
    1: [("qkT", 4, 2, 0), ("qkT", 4, 3, 0), ("oT", 2, 0, 0), ("qk", 4, 1, 1)],
    2: [("v", 2, 0, 1), ("v", 2, 1, 1), ("out", 2, 0, 0), ("qk", 4, 2, 1)],
    3: [("oT", 2, 0, 0), ("qkT", 4, 0, 1), ("qkT", 4, 1, 1), ("qk", 4, 3, 1), ("hT", 1, 0, 2)],
}


A_BANKS, F_BANKS = stage_a_banks(), stage_f_banks()


def build(nc, t):
    ctx = ExitStack()
    with ctx:
        def sb(name, shape, dt=FP32):
            return ctx.enter_context(nc.sbuf_tensor(name, shape, dt))

        def sem(name):
            return ctx.enter_context(nc.semaphore(name))

        banks = [ctx.enter_context(nc.psum_tensor(f"bank{i}", [P, 512], FP32)) for i in range(8)]
        x_in = t["x"].rearrange("b (t p) d -> p b t d", p=P)
        x1, x2, x3, x4, x_out = (t[k].rearrange("b (t p) d -> p b t d", p=P) for k in ("x1", "x2", "x3", "x4", "out"))

        ident = sb("ident", [P, P])
        ones = sb("ones", [P, P])
        halves = sb("halves", [P, 32])
        eps = sb("eps", [P, TILES])
        wq = sb("wq", [P, A_HEADS * A_HD])
        wk2 = sb("wk2", [P, A_KV, 2, A_HD])
        wv = sb("wv", [P, A_KV * A_HD])
        wo = sb("wo", [P, A_HEADS // 2, DIM])
        wkgen = sb("wkgen", [P, KS])
        bkgen = sb("bkgen", [P, KS])
        wconv = sb("wconv", [P, KS])
        bconv = sb("bconv", [P, 1])

        xn = [sb(f"xn{p}", [P, TILES, DIM]) for p in range(PAIR)]
        xr = [sb(f"xr{p}", [P, TILES, DIM]) for p in range(PAIR)]
        xT = sb("xT", [P, SEQ + 2])
        ctx_sum = sb("ctx_sum", [P, 1])
        wk_ctx = sb("wk_ctx", [P, KS])
        gate = sb("gate", [P, 4, KS])
        gate_sum = sb("gate_sum", [P, 1])
        conv = sb("conv", [P, 3, SEQ])
        hT = sb("hT", [P, SEQ])
        qT = [sb(f"qT{p}", [P, A_HEADS // 2, SEQ]) for p in range(PAIR)]
        kT = [sb(f"kT{p}", [P, A_KV, SEQ]) for p in range(PAIR)]
        v = [sb(f"v{p}", [P, TILES, A_KV * A_HD]) for p in range(PAIR)]
        probs = sb("probs", [P, E_RING, A_REP * SEQ])
        E = [probs[:, r, :].rearrange("p (h c k) -> p h c k", h=A_REP, c=CHUNKS) for r in range(E_RING)]
        mx = [sb(f"mx{r}", [P, A_REP, CHUNKS]) for r in range(2)]
        sums = [sb(f"sums{r}", [P, A_HEADS, CHUNKS]) for r in range(2)]
        coef = [sb(f"coef{r}", [P, 3, A_HEADS, CHUNKS]) for r in range(2)]
        total = [sb(f"total{r}", [P, 3, A_HEADS]) for r in range(2)]
        wT = [sb(f"wT{r}", [P, TILES, 2, P]) for r in range(2)]
        oT = [sb(f"oT{r}", [P, A_HEADS // 2, P]) for r in range(2)]
        y = [sb(f"y{r}", [P, DIM]) for r in range(2)]
        stat = [sb(f"stat{r}", [P, 6]) for r in range(2)]
        mv = [sb(f"mv{r}", [P, 2]) for r in range(2)]
        rstd = [sb(f"rstd{r}", [P, 2]) for r in range(2)]
        xo = [sb(f"xo{r}", [P, DIM]) for r in range(2)]

        wqkv = [sb(f"wqkv{l}", [P, 3 * INNER]) for l in range(LAYERS)]
        wof = [sb(f"wof{l}", [P, INNER // P, DIM]) for l in range(LAYERS)]
        w1 = [sb(f"w1_{l}", [P, 2 * F_HID]) for l in range(LAYERS)]
        w2 = [sb(f"w2_{l}", [P, F_CHUNKS, DIM]) for l in range(LAYERS)]
        b1 = [sb(f"b1_{l}", [P, 2, F_CHUNKS]) for l in range(LAYERS)]
        b2 = [sb(f"b2_{l}", [P, DIM]) for l in range(LAYERS)]
        ln_g = [sb(f"ln_g{l}", [P, 1]) for l in range(LAYERS)]
        ln_b = [sb(f"ln_b{l}", [P, 1]) for l in range(LAYERS)]
        rotary = sb("rotary", [P, TILES, 4, F_HD])
        qk_scale = [sb(f"qk_scale{l}", [P, 4, F_HD]) for l in range(LAYERS)]
        table = [sb(f"table{l}", [P, TILES, 4, F_HD]) for l in range(LAYERS)]
        mask32 = sb("mask32", [P, 2 * (P + F_KEYS)])
        mask = sb("mask", [P, 2 * (P + F_KEYS)], BF16)
        ident16 = sb("ident16", [P, P], BF16)

        hn = [sb(f"hn{p}", [P, TILES, DIM]) for p in range(PAIR)]
        fhT = sb("fhT", [P, SEQ])
        sq = [sb(f"sq{r}", [P, INNER]) for r in range(2)]
        on_self = [sb(f"on_self{r}", [P, F_HEADS, F_HD]) for r in range(2)]
        on_partner = [sb(f"on_partner{r}", [P, F_HEADS, F_HD]) for r in range(2)]
        qk = [sb(f"qk{m}", [P, F_HEADS, F_HD]) for m in range(4)]
        norm2 = sb("norm2", [P, 2, 4 * F_HEADS])
        rnorm = sb("rnorm", [P, 4 * F_HEADS])
        qkT = [probs[:, 2 * p:2 * p + 2, :].rearrange("p r (m q) -> p (r m) q", q=SEQ) for p in range(PAIR)]
        v1s = [sb(f"v1s{p}", [P, TILES, F_HEADS, F_HD + 1]) for p in range(PAIR)]
        fE = [probs[:, 4 + r, 0:F_GH * F_KEYS].rearrange("p (k a n) -> p k a n", k=2, a=2) for r in range(F_RING)]
        fmx = [sb(f"fmx{r}", [P, 2, 2]) for r in range(2)]
        eT = sb("eT", [P, F_GH, P])
        eT_back = sb("eT_back", [P, F_GH, P])
        f_rsum = sb("f_rsum", [P, F_GH])
        o_nat = [sb(f"o_nat{r}", [P, F_HEADS, F_HD]) for r in range(2)]
        foT = sb("foT", [P, INNER // P, P])

        hc = [sb(f"hc{p}", [P, TILES, DIM]) for p in range(PAIR)]
        hT2 = [sb(f"hT2_{p}", [P, SEQ]) for p in range(PAIR)]
        ge = [sb(f"ge{c}", [P, SEQ]) for c in range(F_CHUNKS)]
        uT = [sb(f"uT{p}", [P, F_CHUNKS, SEQ]) for p in range(PAIR)]
        res = [sb(f"res{p}", [P, TILES, DIM]) for p in range(PAIR)]
        res1 = [sb(f"res1_{p}", [P, TILES, DIM]) for p in range(PAIR)]
        resb = [sb(f"resb{p}", [P, 2, TILES, DIM]) for p in range(PAIR)]
        yo = [sb(f"yo{p}", [P, TILES, DIM]) for p in range(PAIR)]
        zo = [sb(f"zo{p}", [P, TILES, DIM]) for p in range(PAIR)]
        mstat = [sb(f"mstat{p}", [P, TILES, 6]) for p in range(PAIR)]
        mmv = [sb(f"mmv{p}", [P, TILES, 2]) for p in range(PAIR)]
        mrstd = [sb(f"mrstd{p}", [P, 2, TILES]) for p in range(PAIR)]
        zstat = [sb(f"zstat{p}", [P, TILES, 6]) for p in range(PAIR)]
        zmv = [sb(f"zmv{p}", [P, TILES, 2]) for p in range(PAIR)]
        zrstd = [sb(f"zrstd{p}", [P, 2, TILES]) for p in range(PAIR)]

        weights_in = sem("weights_in")
        ident_step, consts_set, pool_const = sem("ident_step"), sem("consts_set"), sem("pool_const")
        xn_in = [sem(f"xn{p}_in") for p in range(PAIR)]
        xr_in = [sem(f"xr{p}_in") for p in range(PAIR)]
        xo_out = [sem(f"xo{r}_out") for r in range(2)]
        made = {k: sem(f"{k}_made") for k in A_BANKS.stride}
        read = {k: sem(f"{k}_read") for k in A_BANKS.stride}
        wk_ctx_set, gate_exp, gate_step, conv_step, hT_set = (
            sem(n) for n in ("wk_ctx_set", "gate_exp", "gate_step", "conv_step", "hT_set"))
        scored, max_set, sub_done, exp_done, sum_done, coef_step, normed = (
            sem(n) for n in ("scored", "max_set", "sub_done", "exp_done", "sum_done", "coef_step", "normed"))
        wT_made, wT_read, pv_done = sem("wT_made"), sem("wT_read"), sem("pv_done")
        stats_waited, y_step, eps_added, rstd_set, xo_set = sem("stats_waited"), sem("y_step"), sem("eps_added"), sem("rstd_set"), sem("xo_set")

        f_made = {k: sem(f"f_{k}_made") for k in F_BANKS.stride}
        f_read = {k: sem(f"f_{k}_read") for k in F_BANKS.stride}
        f_o_made, f_o_read = sem("f_o_made"), sem("f_o_read")
        hn_in = [sem(f"hn{p}_in") for p in range(PAIR)]
        res_in = [sem(f"res{p}_in") for p in range(PAIR)]
        res1_in = [sem(f"res1_{p}_in") for p in range(PAIR)]
        f_out = [sem(f"f_out{r}") for r in range(2)]
        m_out = [sem(f"m_out{p}") for p in range(PAIR)]
        tables_set, f_consts = sem("tables_set"), sem("f_consts")
        squared, norm_step, guarded, added, rnorm_set, qk_normed = (
            sem(n) for n in ("squared", "norm_step", "guarded", "added", "rnorm_set", "qk_normed"))
        f_scored, f_max, f_sub, f_exp, eT_made, eT_read, back_read, f_rsum_set, f_x_set = (
            sem(n) for n in ("f_scored", "f_max", "f_sub", "f_exp", "eT_made", "eT_read", "back_read", "f_rsum_set", "f_x_set"))
        m_bn, m_stats, m_eps, m_rstd, hc_set, hT2_made, hT2_read = (
            sem(n) for n in ("m_bn", "m_stats", "m_eps", "m_rstd", "hc_set", "hT2_made", "hT2_read"))
        up_made, gelu_done, u_done, down_made, down_read, resb_step = (
            sem(n) for n in ("up_made", "gelu_done", "u_done", "down_made", "down_read", "resb_step"))
        z_bn, z_stats, z_eps, z_rstd, z_set = (sem(n) for n in ("z_bn", "z_stats", "z_eps", "z_rstd", "z_set"))

        block = ctx.enter_context(nc.Block())
        COEF_STEPS = 7
        N_WEIGHTS, N_CONSTS, N_F_CONSTS = 12 + LAYERS * (6 + 3 * F_CHUNKS + 6), 5, 7
        GATE_STEPS = 3

        def stage_a(engine, body, pre=None):
            if pre:
                pre()
            body(0, "first")
            with engine.Fori(1, TURNS - 1) as i:
                body(i, "middle")
            body(TURNS - 1, "last")
            body(TURNS, "drain")

        def f_steps(turn):
            for s in range(F_STEPS if turn != "drain" else F_OUT_LAG):
                slot, g = divmod(s, F_GROUPS)
                yield (s, slot, *divmod(slot, TILES), g)

        def f_fills(turn, s):
            p, at = divmod(s, TILES * F_GROUPS)
            for kind, per, m, ahead in F_FILLS[at]:
                if kind in ("oT", "out"):
                    lag = F_OT_LAG if kind == "oT" else F_OUT_LAG
                    if exists(turn, s, lag):
                        yield kind, (s - lag) // F_GROUPS, m, ahead
                elif prepares(turn, p, ahead):
                    yield kind, per * (p + ahead) + m, m, ahead

        def over_turns(engine, layer, body, pre=None):
            if pre:
                pre()
            first = TURNS * layer
            body(0, first, "first")
            with engine.Fori(1, TURNS - 1) as i:
                body(i, first + i, "middle")
            body(TURNS - 1, first + TURNS - 1, "last")
            body(TURNS, first + TURNS, "drain")

        def keys(tile):
            return (P, 0) if tile == 0 else (F_KEYS, P - WINDOW)

        def steps(i, turn):
            for s in range(A_STEPS if turn != "drain" else LN_LAG):
                slot, g = divmod(s, A_KV)
                p, tile = divmod(slot, TILES)
                yield s, slot, p, tile, g

        def exists(turn, s, lag=0):
            return not (turn == "first" and s < lag) and not (turn == "drain" and s >= lag)

        def prepares(turn, p, ahead=1):
            return turn != "drain" and not (turn == "last" and p + ahead >= PAIR)

        def bank_free(pe, shared, read, kind, local, i, turn):
            last = shared.before(kind, local, turn)
            if last:
                wait(pe, read[last[0]], shared.stride[last[0]] * (i + last[2]) + last[1] + 1)

        def layer_weights(l):
            half = F_HD // 2
            yield wqkv[l][:, :], t["wqkv"][l]
            yield wof[l][:, :, :], t["wof"][l].rearrange("(m p) n -> p m n", p=P)
            yield w1[l][:, :], t["w1"][l]
            yield b2[l][:, :], t["b2"][l].partition_broadcast(P)
            yield ln_g[l][:, :], t["ln_g"][l].rearrange("(p a) -> p a", a=1)
            yield ln_b[l][:, :], t["ln_b"][l].rearrange("(p a) -> p a", a=1)
            for c, rows in enumerate(F_ROWS):
                yield w2[l][0:rows, c, :], t["w2"][l, P * c:P * c + rows, :]
                for a in range(2):
                    at = F_HID * a + P * c
                    yield b1[l][0:rows, a, c:c + 1], t["b1"][l, at:at + rows].rearrange("(p a) -> p a", a=1)
            for a, name in enumerate(("q_scale", "k_scale")):
                yield qk_scale[l][:, 2 * a, :], t[name][l].partition_broadcast(P)
                yield qk_scale[l][:, 2 * a + 1, 0:half], t[name][l, half:].partition_broadcast(P)
                yield qk_scale[l][:, 2 * a + 1, half:], t[name][l, 0:half].partition_broadcast(P)

        @block.sync
        def _(sp):
            for dst, src in (
                (wq[:, :], t["wqT"]), (wv[:, :], t["wvT"]),
                (wk2[:, :, 0, :], t["wkT"].rearrange("c (g d) -> c g d", g=A_KV)),
                (wk2[:, :, 1, :], t["wkT"].rearrange("c (g d) -> c g d", g=A_KV)),
                (wo[:, :, :], t["woT"].rearrange("(m p) n -> p m n", p=P)),
                (wkgen[:, :], t["wkgenT"]),
                (bkgen[:, :], t["bkgen"].partition_broadcast(P)),
                (wconv[:, :], t["wconv"]), (bconv[:, :], t["bconv"].rearrange("(p a) -> p a", a=1)),
                (ident[:, :], t["eye"]), (rotary[:, :, :, :], t["rotary"].rearrange("(t p) a d -> p t a d", p=P)),
                (mask32[:, :], t["mask"]),
                *[pair for l in range(LAYERS) for pair in layer_weights(l)],
            ):
                sp.dma_start(dst, src).then_inc(weights_in, 16)

            def load(dst, b, done, x_in=x_in):
                sp.dma_start(dst[:, :, :], x_in[:, bass.ds(b, 1), :, :]).then_inc(done, 16)

            def pre():
                load(xn[0], 0, xn_in[0])
                load(xn[1], 1, xn_in[1])

            def body(i, turn):
                for p in range(PAIR):
                    b = PAIR * i + p
                    if turn in ("first", "middle"):
                        wait(sp, made["xT"], b + 1)
                        load(xn[p], b + 2, xn_in[p])
                    if turn != "drain":
                        wait(sp, read["out"], TILES * (b - 1))
                        load(xr[p], b, xr_in[p])
                    for tile in range(TILES):
                        at = TILES * p + tile - 3
                        j = A_SLOTS * i + at
                        if (turn == "first" and at < 0) or (turn == "drain" and at >= 0):
                            continue
                        wait(sp, xo_set, j + 1)
                        r = at % 2
                        jb, jt = (at // TILES), at % TILES
                        sp.dma_start(x1[:, bass.ds(PAIR * i + jb, 1), jt, :], xo[r][:, :]).then_inc(xo_out[r], 16)

            stage_a(sp, body, pre)
            for r in range(2):
                sp.wait_ge(xo_out[r], 16 * BATCH * TILES // 2)

            HALF = DIM // 2

            def load_shifted(dst, b, done, src):
                x = src[:, bass.ds(b, 1), :, :]
                sp.dma_start(dst[:, :, 0:HALF], x[:, :, :, 0:HALF]).then_inc(done, 16)
                sp.dma_start(dst[1:P, 0, HALF:DIM], x[0:P - 1, :, 0, HALF:DIM]).then_inc(done, 16)
                sp.dma_start(dst[0:1, 1, HALF:DIM], x[P - 1:P, :, 0, HALF:DIM]).then_inc(done, 16)
                sp.dma_start(dst[1:P, 1, HALF:DIM], x[0:P - 1, :, 1, HALF:DIM]).then_inc(done, 16)

            def attention(layer):
                src, dst = (x1, x2) if layer == 0 else (x3, x4)

                def pre():
                    for p in range(PAIR):
                        load_shifted(hn[p], p, hn_in[p], src)

                def body(i, it, turn):
                    for p in range(PAIR):
                        b, bb = PAIR * i + p, PAIR * it + p
                        if prepares(turn, p, 2):
                            wait(sp, f_made["hT"], bb + 1)
                            load_shifted(hn[p], b + 2, hn_in[p], src)
                        if turn != "drain":
                            wait(sp, f_read["out"], TILES * (bb - 1))
                            load(res[p], b, res_in[p], src)
                        for tile in range(TILES):
                            at = TILES * p + tile - 4
                            if (turn == "first" and at < 0) or (turn == "drain" and at >= 0):
                                continue
                            wait(sp, f_read["out"], F_SLOTS * it + at + 1)
                            sp.dma_start(dst[:, bass.ds(PAIR * i + at // TILES, 1), at % TILES, :],
                                         xo[at % 2][:, :]).then_inc(f_out[at % 2], 16)

                over_turns(sp, layer, body, pre)
                for r in range(2):
                    sp.wait_ge(f_out[r], 16 * (layer + 1) * BATCH * TILES // 2)

            def mlp(layer):
                src, dst = (x2, x3) if layer == 0 else (x4, x_out)
                at_start = PAIR * TURNS * layer

                def pre():
                    for p in range(PAIR):
                        load_shifted(hn[p], p, hn_in[p], src)

                def body(i, it, turn):
                    for p in range(PAIR):
                        b, bb = PAIR * i + p, PAIR * it + p
                        if turn != "drain":
                            wait(sp, down_read, bb - 1)
                            load(res[p], b, res_in[p], src)
                            if layer == LAYERS - 1:
                                load(res1[p], b, res1_in[p], x1)
                        if prepares(turn, p, 2):
                            wait(sp, hc_set, bb + 1)
                            load_shifted(hn[p], b + 2, hn_in[p], src)
                        lag = 2 if layer == LAYERS - 1 else 1
                        if not (turn == "first" and p < lag) and not (turn == "drain" and p >= lag):
                            r = (p - lag) % PAIR
                            if layer == LAYERS - 1:
                                wait(sp, z_set, PAIR * i + p - lag + 1)
                                data = zo[r]
                            else:
                                wait(sp, down_read, bb - lag + 1)
                                data = yo[r]
                            sp.dma_start(dst[:, bass.ds(b - lag, 1), :, :], data[:, :, :]).then_inc(m_out[r], 16)

                over_turns(sp, layer, body, pre)
                for r in range(PAIR):
                    sp.wait_ge(m_out[r], 16 * (layer + 1) * TURNS)

            for layer in range(LAYERS):
                attention(layer)
                mlp(layer)

        @block.gpsimd
        def _(pool):
            pool.memset(ones[:, :], 1.0).then_inc(consts_set, 1)
            pool.memset(halves[:, :], -0.5).then_inc(consts_set, 1)
            pool.memset(eps[:, :], LN_EPS).then_inc(consts_set, 1)
            pool.memset(xT[:, 0:1], 0.0).then_inc(consts_set, 1)
            pool.memset(xT[:, SEQ + 1:SEQ + 2], 0.0).then_inc(consts_set, 1)
            for p in range(PAIR):
                pool.memset(hn[p][0:1, 0, DIM // 2:DIM], 0.0).then_inc(f_consts, 1)
                pool.memset(v1s[p][:, :, :, F_HD:F_HD + 1], 1.0).then_inc(f_consts, 1)
            pool.memset(eT_back[0:WINDOW, :, :], 0.0).then_inc(f_consts, 1)
            pool.wait_ge(consts_set, N_CONSTS)
            pool.wait_ge(weights_in, 16 * N_WEIGHTS)
            for l in range(LAYERS):
                for tile in range(TILES):
                    nc.gpsimd.tensor_tensor(out=table[l][:, tile, :, :], in0=rotary[:, tile, :, :], in1=qk_scale[l][:, :, :],
                                            op=ALU.mult).then_inc(tables_set, 1)

            def body(i, turn):
                for s, slot, p, tile, g in steps(i, turn):
                    if exists(turn, s, NORM_LAG):
                        at, ng = divmod(s - NORM_LAG, A_KV)
                        r = at % 2
                        wait(pool, coef_step, COEF_STEPS * (A_SLOTS * i + at + 1))
                        e = E[(s - NORM_LAG) % E_RING]
                        nc.gpsimd.tensor_tensor(
                            out=e[:, :, :, :], in0=e[:, :, :, :],
                            in1=coef[r][:, 2, A_REP * ng:A_REP * (ng + 1), :].unsqueeze(3).broadcast_to([P, A_REP, CHUNKS, CHUNK]),
                            op=ALU.mult).then_inc(normed, 1)
                    if g == (OUT_LAG + 1) % A_KV and exists(turn, s, OUT_LAG + 1):
                        at = (s - OUT_LAG - 1) // A_KV
                        j = A_SLOTS * i + at
                        r = at % 2
                        wait(pool, y_step, 2 * j + 2)
                        nc.gpsimd.tensor_tensor(out=rstd[r][:, 0:1], in0=mv[r][:, 1:2], in1=eps[:, 0:1], op=ALU.add).then_inc(eps_added, 1)
                        wait(pool, eps_added, j + 1)
                        wait(pool, xo_set, j - 1)
                        nc.gpsimd.tensor_tensor(out=rstd[r][:, 1:2], in0=rstd[r][:, 0:1], in1=halves[:, 0:1],
                                                op=ALU.pow).then_inc(rstd_set, 1)

            stage_a(pool, body)

            def attention(layer):
                def sums(it, local, m):
                    index = F_BANKS.stride["qk"] * it + local
                    pool.wait_ge(f_read["qk"], index + 1)
                    wait(pool, f_made["qkT"], index - 3)
                    nc.gpsimd.tensor_tensor(out=qk[m][:, :, :], in0=on_self[m % 2][:, :, :], in1=on_partner[m % 2][:, :, :],
                                            op=ALU.add).then_inc(added, 1)

                def inverse_norms(bb, tile):
                    pool.wait_ge(guarded, TILES * bb + tile + 1)
                    wait(pool, qk_normed, 4 * (bb - 1) + 2 * tile + 2)
                    at = slice(2 * F_HEADS * tile, 2 * F_HEADS * (tile + 1))
                    nc.gpsimd.tensor_tensor(out=rnorm[:, at], in0=norm2[:, 1, at], in1=halves[:, 0:2 * F_HEADS],
                                            op=ALU.pow).then_inc(rnorm_set, 1)
                    pool.wait_ge(rnorm_set, TILES * bb + tile + 1)

                def normalise(bb, m):
                    wait(pool, added, 4 * bb + m + 1)
                    nc.gpsimd.tensor_tensor(
                        out=qk[m][:, :, :], in0=qk[m][:, :, :],
                        in1=rnorm[:, F_HEADS * m:F_HEADS * (m + 1)].unsqueeze(2).broadcast_to([P, F_HEADS, F_HD]),
                        op=ALU.mult).then_inc(qk_normed, 1)

                def prepare(bb, it, m, ahead_local):
                    sums(it, ahead_local + m, m)
                    if m % 2 == 1:
                        inverse_norms(bb, m // 2)
                        normalise(bb, m - 1)
                        normalise(bb, m)

                def pre():
                    for m in range(4):
                        prepare(PAIR * TURNS * layer, TURNS * layer, m, 0)

                def body(i, it, turn):
                    for s, slot, p, tile, g in f_steps(turn):
                        if prepares(turn, p):
                            prepare(PAIR * it + p + 1, it, F_GROUPS * tile + g, 4 * (p + 1))

                over_turns(pool, layer, body, pre)

            def mlp(layer):
                def rstd_of(mv2, out, step, done, stats, bb):
                    pool.wait_ge(stats, 2 * bb + 2)
                    nc.gpsimd.tensor_tensor(out=out[:, 0, :], in0=mv2[:, :, 1], in1=eps[:, 0:TILES], op=ALU.add).then_inc(step, 1)
                    pool.wait_ge(step, bb + 1)
                    nc.gpsimd.tensor_tensor(out=out[:, 1, :], in0=out[:, 0, :], in1=halves[:, 0:TILES], op=ALU.pow).then_inc(done, 1)

                def pre():
                    for p in range(PAIR):
                        rstd_of(mmv[p], mrstd[p], m_eps, m_rstd, m_stats, PAIR * TURNS * layer + p)

                def body(i, it, turn):
                    for p in range(PAIR):
                        b, bb = PAIR * i + p, PAIR * it + p
                        if turn != "drain":
                            pool.wait_ge(res_in[p], 16 * ((2 * layer + 1) * TURNS + i + 1))
                            wait(pool, down_read, bb - 1)
                            nc.gpsimd.tensor_tensor(out=resb[p][:, 0, :, :], in0=res[p][:, :, :],
                                                    in1=b2[layer][:, :].unsqueeze(1).broadcast_to([P, TILES, DIM]),
                                                    op=ALU.add).then_inc(resb_step, 1)
                            if layer == LAYERS - 1:
                                pool.wait_ge(res1_in[p], 16 * (i + 1))
                                wait(pool, resb_step, BATCH * layer + 2 * b + 1)
                                nc.gpsimd.tensor_tensor(out=resb[p][:, 1, :, :], in0=resb[p][:, 0, :, :], in1=res1[p][:, :, :],
                                                        op=ALU.add).then_inc(resb_step, 1)
                        if layer == LAYERS - 1 and not (turn == "first" and p < 1) and not (turn == "drain" and p >= 1):
                            rstd_of(zmv[(p - 1) % PAIR], zrstd[(p - 1) % PAIR], z_eps, z_rstd, z_stats, b - 1)
                        if prepares(turn, p, 2):
                            rstd_of(mmv[p], mrstd[p], m_eps, m_rstd, m_stats, bb + 2)

                over_turns(pool, layer, body, pre)

            for layer in range(LAYERS):
                attention(layer)
                mlp(layer)

        @block.scalar
        def _(act):
            def x_transposed(i, local, turn, b):
                act.wait_ge(made["xT"], b + 1)
                wait(act, hT_set, b)
                wait(act, wk_ctx_set, b)
                nc.scalar.activation(xT[:, 1:SEQ + 1], banks[6 + A_BANKS.bank("xT", local, turn)][:, 0:SEQ], ACT.Copy,
                                     accum_out=ctx_sum[:, :]).then_inc(read["xT"], 1)

            def gate_exponential(b):
                act.wait_ge(read["gate"], b + 1)
                nc.scalar.activation(gate[:, 1, :], gate[:, 0, :], ACT.Exp, scale=-1.0).then_inc(gate_exp, 1)

            def projected(kind, i, local, turn, m, pb):
                index = A_BANKS.stride[kind] * i + local
                act.wait_ge(made[kind], index + 1)
                bank = banks[6 + A_BANKS.bank(kind, local, turn)]
                if kind == "q":
                    nc.scalar.activation(qT[pb][:, 2 * m:2 * m + 2, :], bank[:, :], ACT.Copy, scale=A_HD ** -0.5).then_inc(read[kind], 1)
                elif kind == "k":
                    nc.scalar.activation(kT[pb][:, 2 * m:2 * m + 2, :], bank[:, :], ACT.Copy).then_inc(read[kind], 1)
                else:
                    nc.scalar.activation(v[pb][:, :, :], bank[:, :], ACT.Copy).then_inc(read[kind], 1)

            def pre():
                act.wait_ge(consts_set, N_CONSTS)
                x_transposed(0, 0, "pre", 0)
                gate_exponential(0)
                for kind, local in A_BANKS.pre[2:]:
                    projected(kind, 0, local, "pre", local, 0)

            def body(i, turn):
                for s, slot, p, tile, g in steps(i, turn):
                    if exists(turn, s, PV_LAG):
                        n = A_STEPS * i + s - PV_LAG
                        for hp in range(2):
                            act.wait_ge(wT_made, 2 * n + hp + 1)
                            wait(act, pv_done, 2 * (n - 1) + hp + 1)
                            nc.scalar.activation(wT[hp][:, :, :, :], banks[4 + hp][:, :], ACT.Copy).then_inc(wT_read, 1)
                    if exists(turn, s, EXP_LAG):
                        n = A_STEPS * i + s - EXP_LAG
                        act.wait_ge(sub_done, n + 1)
                        e = E[(s - EXP_LAG) % E_RING]
                        nc.scalar.activation(e[:, :, :, :], e[:, :, :, :], ACT.Exp).then_inc(exp_done, 1)
                    if prepares(turn, p) and tile == 0:
                        if g == 0:
                            x_transposed(i, p + 1, turn, PAIR * i + p + 1)
                        if g == 3:
                            gate_exponential(PAIR * i + p + 1)
                    if prepares(turn, p) and tile == 1:
                        for kind, per, m in A_PROJECTIONS[g]:
                            projected(kind, i, per * (p + 1) + m, turn, m, (p + 1) % 2)
                    if exists(turn, s, PV_LAG):
                        n = A_STEPS * i + s - PV_LAG
                        at, og = divmod(s - PV_LAG, A_KV)
                        act.wait_ge(pv_done, 2 * n + 2)
                        wait(act, made["out"], A_SLOTS * i + at - 1)
                        nc.scalar.activation(oT[at % 2][:, 2 * og:2 * og + 2, :],
                                             banks[6 + A_BANKS.bank("o", s - PV_LAG, "middle")][:, 0:2 * P], ACT.Copy).then_inc(read["o"], 1)

            stage_a(act, body, pre)

            def attention(layer):
                def prepare(it, kind, local, m, batch, turn):
                    act.wait_ge(f_made[kind], F_BANKS.stride[kind] * it + local + 1)
                    bank = banks[6 + F_BANKS.bank(kind, local, turn)]
                    par = (local // (F_BANKS.stride[kind] // PAIR)) % PAIR
                    if kind == "hT":
                        nc.scalar.activation(fhT[:, :], bank[:, 0:SEQ], ACT.Copy).then_inc(f_read[kind], 1)
                    elif kind == "qk":
                        wait(act, norm_step, 4 * batch + m - 1)
                        nc.scalar.activation(sq[m % 2][:, :], bank[:, :], ACT.Square).then_inc(squared, 1)
                    elif kind == "v":
                        wait(act, f_o_made, 4 * (batch - 1))
                        nc.scalar.activation(v1s[par][:, m, :, 0:F_HD], bank[:, :].rearrange("p (h d) -> p h d", h=F_HEADS),
                                             ACT.Copy).then_inc(f_read[kind], 1)
                    else:
                        tile, half = divmod(m, 2)
                        nc.scalar.activation(qkT[par][:, 4 * half:4 * half + 4, P * tile:P * (tile + 1)],
                                             bank[:, :].rearrange("p (m q) -> p m q", m=4), ACT.Copy).then_inc(f_read[kind], 1)

                def pre():
                    if layer == 0:
                        act.wait_ge(f_consts, N_F_CONSTS)
                    for kind, local in F_BANKS.pre:
                        per = F_BANKS.stride[kind] // PAIR
                        prepare(TURNS * layer, kind, local, local % per, PAIR * TURNS * layer + local // per, "pre")

                def body(i, it, turn):
                    for s, slot, p, tile, g in f_steps(turn):
                        n = F_STEPS * it + s
                        if exists(turn, s, F_PV_LAG):
                            act.wait_ge(eT_made, n - F_PV_LAG + 1)
                            wait(act, f_o_made, n - F_PV_LAG)
                            nc.scalar.activation(eT[:, :, :], banks[4][:, :], ACT.Copy).then_inc(eT_read, 1)
                            if (s - F_PV_LAG) // F_GROUPS % TILES == 1:
                                nc.scalar.activation(eT_back[WINDOW:P, :, :], banks[5][0:WINDOW, :], ACT.Copy).then_inc(back_read, 1)

                        def exponentials():
                            n_keys, _ = keys(tile)
                            e = fE[s % F_RING]
                            act.wait_ge(f_sub, n + 1)
                            nc.scalar.activation(e[:, :, :, 0:n_keys], e[:, :, :, 0:n_keys], ACT.Exp).then_inc(f_exp, 1)

                        for kind, local, m, ahead in f_fills(turn, s):
                            if kind == "qk":
                                exponentials()
                            if kind == "oT":
                                j = F_SLOTS * it + local
                                act.wait_ge(f_made["oT"], j + 1)
                                wait(act, f_made["out"], j)
                                nc.scalar.activation(foT[:, :, :], banks[6 + F_BANKS.bank("oT", local, "middle")][:, :],
                                                     ACT.Copy).then_inc(f_read["oT"], 1)
                            elif kind != "out":
                                prepare(it, kind, local, m, PAIR * it + p + ahead, turn)
                        if exists(turn, s) and not prepares(turn, p):
                            exponentials()

                over_turns(act, layer, body, pre)

            def mlp(layer):
                def body(i, it, turn):
                    if turn == "drain":
                        return
                    for p in range(PAIR):
                        bb = PAIR * it + p
                        for c, rows in enumerate(F_ROWS):
                            act.wait_ge(up_made, 3 * bb + c + 1)
                            wait(act, u_done, 3 * (bb - 1) + c + 1)
                            nc.scalar.activation(ge[c][0:rows, :], banks[3 * p + c][0:rows, SEQ:2 * SEQ], ACT.Gelu,
                                                 bias=b1[layer][0:rows, 1, c:c + 1]).then_inc(gelu_done, 1)

                over_turns(act, layer, body)

            for layer in range(LAYERS):
                attention(layer)
                mlp(layer)

        @block.vector
        def _(dve):
            def gate_weights(b):
                dve.wait_ge(read["xT"], b + 1)
                wait(dve, made["gate"], b)
                nc.vector.tensor_scalar(wk_ctx[:, :], wkgen[:, :], ctx_sum[:, 0:1], None, ALU.mult).then_inc(wk_ctx_set, 1)

            def gate_logit(b, local, turn):
                dve.wait_ge(made["gate"], b + 1)
                wait(dve, gate_step, GATE_STEPS * b)
                wait(dve, gate_exp, b)
                nc.vector.scalar_tensor_tensor(gate[:, 0, :], banks[6 + A_BANKS.bank("gate", local, turn)][:, 0:KS], 1.0 / SEQ,
                                               bkgen[:, :], ALU.mult, ALU.add).then_inc(read["gate"], 1)

            def convolution(b):
                nc.vector.tensor_scalar(conv[:, 0, :], xT[:, 1:SEQ + 1], wconv[:, 1:2], bconv[:, 0:1],
                                        ALU.mult, ALU.add).then_inc(conv_step, 1)
                dve.wait_ge(conv_step, 3 * b + 1)
                nc.vector.scalar_tensor_tensor(conv[:, 1, :], xT[:, 0:SEQ], wconv[:, 0:1], conv[:, 0, :],
                                               ALU.mult, ALU.add).then_inc(conv_step, 1)
                dve.wait_ge(conv_step, 3 * b + 2)
                nc.vector.scalar_tensor_tensor(conv[:, 2, :], xT[:, 2:SEQ + 2], wconv[:, 2:3], conv[:, 1, :],
                                               ALU.mult, ALU.add).then_inc(conv_step, 1)

            def gated(b):
                dve.wait_ge(gate_exp, b + 1)
                nc.vector.tensor_scalar_add(gate[:, 2, :], gate[:, 1, :], 1.0).then_inc(gate_step, 1)
                dve.wait_ge(gate_step, GATE_STEPS * b + 1)
                nc.vector.reciprocal(gate[:, 3, :], gate[:, 2, :]).then_inc(gate_step, 1)
                dve.wait_ge(gate_step, GATE_STEPS * b + 2)
                nc.vector.tensor_reduce(gate_sum[:, :], gate[:, 3, :], AX.X, ALU.add).then_inc(gate_step, 1)
                dve.wait_ge(gate_step, GATE_STEPS * b + 3)
                dve.wait_ge(conv_step, 3 * b + 3)
                wait(dve, made["v"], b)
                nc.vector.tensor_scalar(hT[:, :], conv[:, 2, :], gate_sum[:, 0:1], 1.0 / KS,
                                        ALU.mult, ALU.mult).then_inc(hT_set, 1)

            def pre():
                dve.wait_ge(weights_in, 16 * N_WEIGHTS)
                dve.wait_ge(consts_set, N_CONSTS)
                gate_weights(0)
                gate_logit(0, 0, "pre")
                convolution(0)
                gated(0)

            def factors(j, r):
                c, tt = coef[r], total[r]
                k = COEF_STEPS * j

                def link(ins, at):
                    ins.then_inc(coef_step, 1)
                    if at < COEF_STEPS:
                        dve.wait_ge(coef_step, k + at)
                dve.wait_ge(sum_done, A_KV * (j + 1))
                wait(dve, normed, A_KV * (j - 1))
                link(nc.vector.reciprocal(c[:, 0, :, :], sums[r][:, :, :]), 1)
                link(nc.vector.tensor_tensor(c[:, 1, :, :], sums[r][:, :, :], c[:, 0, :, :], ALU.mult), 2)
                link(nc.vector.tensor_reduce(tt[:, 0, :], c[:, 1, :, :], AX.X, ALU.add), 3)
                link(nc.vector.tensor_scalar_add(tt[:, 1, :], tt[:, 0, :], 1e-9), 4)
                link(nc.vector.reciprocal(tt[:, 2, :], tt[:, 1, :]), 5)
                link(nc.vector.tensor_tensor(c[:, 1, :, :], c[:, 1, :, :],
                                             tt[:, 2, :].unsqueeze(2).broadcast_to([P, A_HEADS, CHUNKS]), ALU.mult), 6)
                link(nc.vector.tensor_tensor(c[:, 2, :, :], c[:, 0, :, :], c[:, 1, :, :], ALU.mult), 7)

            def summed(i, turn, s):
                if exists(turn, s, SUM_LAG):
                    n = A_STEPS * i + s - SUM_LAG
                    at, gg = divmod(s - SUM_LAG, A_KV)
                    dve.wait_ge(exp_done, n + 1)
                    nc.vector.tensor_reduce(sums[at % 2][:, A_REP * gg:A_REP * (gg + 1), :], E[(s - SUM_LAG) % E_RING][:, :, :, :],
                                            AX.X, ALU.add).then_inc(sum_done, 1)
                    if gg == A_KV - 1:
                        factors(A_SLOTS * i + at, at % 2)

            def body(i, turn):
                for s, slot, p, tile, g in steps(i, turn):
                    if tile == 0 and g == 1 and prepares(turn, p):
                        gate_weights(PAIR * i + p + 1)
                    if tile == 1 and g == 0 and prepares(turn, p):
                        gated(PAIR * i + p + 1)
                    if g == 1:
                        summed(i, turn, s)
                    if exists(turn, s):
                        n = A_STEPS * i + s
                        e, m = E[s % E_RING], mx[s % 2]
                        both = [banks[2 * (s % 2) + k] for k in range(2)]
                        dve.wait_ge(scored, n + 1)
                        for k in range(2):
                            ins = nc.vector.tensor_reduce(m[:, 2 * k:2 * k + 2, :], both[k][:, :].rearrange("p (h c k) -> p h c k", h=2, c=CHUNKS),
                                                          AX.X, ALU.max)
                            ins.then_inc(max_set, 1)
                        wait(dve, wT_made, 2 * (n - E_RING) + 2)
                        for k in range(2):
                            dve.wait_ge(max_set, 2 * n + k + 1)
                            ins = nc.vector.tensor_tensor(
                                e[:, 2 * k:2 * k + 2, :, :], both[k][:, :].rearrange("p (h c k) -> p h c k", h=2, c=CHUNKS),
                                m[:, 2 * k:2 * k + 2, :].unsqueeze(3).broadcast_to([P, 2, CHUNKS, CHUNK]), ALU.subtract)
                        ins.then_inc(sub_done, 1)
                    if tile == 0 and g == 2 and prepares(turn, p):
                        gate_logit(PAIR * i + p + 1, p + 1, turn)
                    if g != 1:
                        summed(i, turn, s)
                    if prepares(turn, p):
                        b = PAIR * i + p + 1
                        if tile == 0 and g == 2:
                            convolution(b)
                    if g == OUT_LAG % A_KV and exists(turn, s, OUT_LAG):
                        at = (s - OUT_LAG) // A_KV
                        j, r = A_SLOTS * i + at, at % 2
                        dve.wait_ge(made["out"], j + 1)
                        dve.wait_ge(xr_in[(at // TILES) % 2], 16 * (i + at // TILES // PAIR + 1))
                        nc.vector.tensor_tensor(y[r][:, :], banks[6 + A_BANKS.bank("out", at, "middle")][:, 0:DIM],
                                                xr[(at // TILES) % 2][:, at % TILES, :], ALU.add).then_inc(read["out"], 1)
                        dve.wait_ge(read["out"], j + 1)
                        nc.vector.bn_stats(stat[r][:, :], y[r][:, :]).then_inc(y_step, 1)
                        dve.wait_ge(y_step, 2 * j + 1)
                        dve.sem_inc(stats_waited, 1)
                        nc.vector.bn_aggr(mv[r][:, :], stat[r][:, :]).then_inc(y_step, 1)
                    if g == LN_LAG % A_KV and exists(turn, s, LN_LAG):
                        at = (s - LN_LAG) // A_KV
                        j, r = A_SLOTS * i + at, at % 2
                        dve.wait_ge(rstd_set, j + 1)
                        wait(dve, xo_out[r], 16 * (2 * i + at // 2))
                        nc.vector.tensor_scalar(xo[r][:, :], y[r][:, :], mv[r][:, 0:1], rstd[r][:, 1:2],
                                                ALU.subtract, ALU.mult).then_inc(xo_set, 1)

            stage_a(dve, body, pre)

            dve.wait_ge(tables_set, LAYERS * TILES)
            nc.vector.tensor_copy(mask[:, :], mask32[:, :]).then_inc(f_consts, 1)
            nc.vector.tensor_copy(ident16[:, :], ident[:, :]).then_inc(f_consts, 1)

            def attention(layer):
                HALF = F_HD // 2

                def rotate(it, local, m, turn):
                    index = F_BANKS.stride["qk"] * it + local
                    bank = banks[6 + F_BANKS.bank("qk", local, turn)][:, :].rearrange("p (h d) -> p h d", h=F_HEADS)
                    tile, kind = divmod(m, 2)

                    def tab(k, lo, hi):
                        return table[layer][:, tile, 2 * kind + k, lo:hi].unsqueeze(1).broadcast_to([P, F_HEADS, hi - lo])

                    dve.wait_ge(squared, index + 1)
                    wait(dve, added, index - 1)
                    nc.vector.tensor_tensor(on_self[m % 2][:, :, :], bank, tab(0, 0, F_HD), ALU.mult)
                    nc.vector.tensor_tensor(on_partner[m % 2][:, :, 0:HALF], bank[:, :, HALF:F_HD], tab(1, 0, HALF), ALU.mult)
                    nc.vector.tensor_tensor(on_partner[m % 2][:, :, HALF:F_HD], bank[:, :, 0:HALF], tab(1, HALF, F_HD),
                                            ALU.mult).then_inc(f_read["qk"], 1)
                    nc.vector.tensor_reduce(norm2[:, 0, F_HEADS * m:F_HEADS * (m + 1)],
                                            sq[m % 2][:, :].rearrange("p (h d) -> p h d", h=F_HEADS), AX.X, ALU.add).then_inc(norm_step, 1)
                    if m % 2 == 1:
                        dve.wait_ge(norm_step, index + 1)
                        wait(dve, rnorm_set, TILES * (PAIR * it + local // 4 - 1) + tile + 1)
                        at = slice(F_HEADS * (m - 1), F_HEADS * (m + 1))
                        nc.vector.tensor_scalar_max(norm2[:, 1, at], norm2[:, 0, at], 1e-24).then_inc(guarded, 1)

                def pre():
                    for m in range(4):
                        rotate(TURNS * layer, m, m, "pre")

                def body(i, it, turn):
                    for s, slot, p, tile, g in f_steps(turn):
                        n = F_STEPS * it + s
                        if exists(turn, s):
                            n_keys, _ = keys(tile)
                            e, m = fE[s % F_RING], fmx[s % 2]
                            both = [banks[2 * (s % 2) + k][:, 0:2 * n_keys].rearrange("p (a k) -> p a k", a=2) for k in range(2)]
                            dve.wait_ge(f_scored, n + 1)
                            for k in range(2):
                                nc.vector.tensor_reduce(m[:, k, :], both[k], AX.X, ALU.max).then_inc(f_max, 1)
                            wait(dve, eT_made, n - F_RING + 1)
                            for k in range(2):
                                dve.wait_ge(f_max, 2 * n + k + 1)
                                ins = nc.vector.tensor_tensor(e[:, k, :, 0:n_keys], both[k],
                                                              m[:, k, :].unsqueeze(2).broadcast_to([P, 2, n_keys]), ALU.subtract)
                            ins.then_inc(f_sub, 1)
                        if exists(turn, s, F_PV_LAG):
                            at, og = divmod(s - F_PV_LAG, F_GROUPS)
                            j = F_SLOTS * it + at
                            view = banks[5][:, 0:F_GH * (F_HD + 1)].rearrange("p (h d) -> p h d", h=F_GH)
                            dve.wait_ge(f_o_made, n - F_PV_LAG + 1)
                            nc.vector.reciprocal(f_rsum[:, :].unsqueeze(2), view[:, :, F_HD:F_HD + 1]).then_inc(f_rsum_set, 1)
                            dve.wait_ge(f_rsum_set, n - F_PV_LAG + 1)
                            wait(dve, f_made["oT"], j - 1)
                            nc.vector.tensor_tensor(o_nat[at % 2][:, F_GH * og:F_GH * (og + 1), :], view[:, :, 0:F_HD],
                                                    f_rsum[:, :].unsqueeze(2).broadcast_to([P, F_GH, F_HD]), ALU.mult).then_inc(f_o_read, 1)
                        for kind, local, m, ahead in f_fills(turn, s):
                            if kind == "qk":
                                rotate(it, local, m, turn)
                            if kind == "out":
                                at = local
                                j, r = F_SLOTS * it + at, at % 2
                                dve.wait_ge(f_made["out"], j + 1)
                                dve.wait_ge(res_in[(at // TILES) % PAIR], 16 * (2 * layer * TURNS + i + at // TILES // PAIR + 1))
                                wait(dve, f_out[r], 16 * (2 * it + at // 2))
                                nc.vector.tensor_tensor(xo[r][:, :], banks[6 + F_BANKS.bank("out", at, "middle")][:, 0:DIM],
                                                        res[(at // TILES) % PAIR][:, at % TILES, :], ALU.add).then_inc(f_read["out"], 1)

                over_turns(dve, layer, body, pre)

            def mlp(layer):
                last_layer = layer == LAYERS - 1

                def stats(x, st, out, bn, done, count):
                    for tile in range(TILES):
                        nc.vector.bn_stats(st[:, tile, :], x[:, tile, :]).then_inc(bn, 1)
                    dve.wait_ge(bn, TILES * (count + 1))
                    dve.sem_inc(stats_waited, 1)
                    for tile in range(TILES):
                        nc.vector.bn_aggr(out[:, tile, :], st[:, tile, :]).then_inc(done, 1)

                def loaded(par, i_of):
                    dve.wait_ge(hn_in[par], 64 * ((2 * layer + 1) * TURNS + i_of + 1))

                def normalised(par, bb):
                    dve.wait_ge(m_rstd, bb + 1)
                    for tile in range(TILES):
                        ins = nc.vector.tensor_scalar(hc[par][:, tile, :], hn[par][:, tile, :], mmv[par][:, tile, 0:1],
                                                      mrstd[par][:, 1, tile:tile + 1], ALU.subtract, ALU.mult)
                    ins.then_inc(hc_set, 1)

                def gain_and_bias(par, bb):
                    dve.wait_ge(hT2_made, bb + 1)
                    nc.vector.tensor_scalar(hT2[par][:, :], banks[6][:, 0:SEQ], ln_g[layer][:, 0:1], ln_b[layer][:, 0:1],
                                            ALU.mult, ALU.add).then_inc(hT2_read, 1)

                def pre():
                    bb = PAIR * TURNS * layer
                    for p in range(PAIR):
                        loaded(p, 0)
                        stats(hn[p], mstat[p], mmv[p], m_bn, m_stats, bb + p)
                    normalised(0, bb)
                    gain_and_bias(0, bb)

                def body(i, it, turn):
                    for p in range(PAIR):
                        b, bb, other = PAIR * i + p, PAIR * it + p, 1 - p
                        if prepares(turn, p):
                            normalised(other, bb + 1)
                        if turn != "drain":
                            for c, rows in enumerate(F_ROWS):
                                dve.wait_ge(gelu_done, 3 * bb + c + 1)
                                nc.vector.scalar_tensor_tensor(uT[p][0:rows, c, :], banks[3 * p + c][0:rows, 0:SEQ],
                                                               b1[layer][0:rows, 0, c:c + 1], ge[c][0:rows, :],
                                                               ALU.add, ALU.mult).then_inc(u_done, 1)
                        if prepares(turn, p):
                            gain_and_bias(other, bb + 1)
                        if not (turn == "first" and p == 0) and not (turn == "drain" and p >= 1):
                            dve.wait_ge(down_made, bb)
                            dve.wait_ge(resb_step, BATCH * layer + 2 * b if last_layer else bb)
                            if last_layer:
                                wait(dve, z_set, b - 2)
                            wait(dve, m_out[other], 16 * (it + p - 1)) if not last_layer else None
                            nc.vector.tensor_tensor(yo[other][:, :, :], banks[7][:, 0:TILES * DIM].rearrange("p (t d) -> p t d", t=TILES),
                                                    resb[other][:, 1 if last_layer else 0, :, :], ALU.add).then_inc(down_read, 1)
                            if last_layer:
                                dve.wait_ge(down_read, bb)
                                stats(yo[other], zstat[other], zmv[other], z_bn, z_stats, b - 1)
                        if last_layer and not (turn == "first") and not (turn == "drain" and p >= 2):
                            dve.wait_ge(z_rstd, b - 1)
                            wait(dve, m_out[p], 16 * (TURNS * layer + i - 1))
                            for tile in range(TILES):
                                ins = nc.vector.tensor_scalar(zo[p][:, tile, :], yo[p][:, tile, :], zmv[p][:, tile, 0:1],
                                                              zrstd[p][:, 1, tile:tile + 1], ALU.subtract, ALU.mult)
                            ins.then_inc(z_set, 1)
                        if prepares(turn, p, 2):
                            loaded(p, i + 1)
                            stats(hn[p], mstat[p], mmv[p], m_bn, m_stats, bb + 2)

                over_turns(dve, layer, body, pre)

            for layer in range(LAYERS):
                attention(layer)
                mlp(layer)

        @block.tensor
        def _(pe):
            def transpose_x(i, local, turn, b):
                bank_free(pe, A_BANKS, read, "xT", local, i, turn)
                pe.wait_ge(xn_in[local % 2], 16 * (i + local // 2 + 1))
                bank = banks[6 + A_BANKS.bank("xT", local, turn)]
                for tt in range(TILES):
                    ins = nc.tensor.transpose(bank[:, P * tt:P * (tt + 1)], xn[local % 2][:, tt, :], ident[:, :])
                ins.then_inc(made["xT"], 1)

            def gate_matmul(i, local, turn, b):
                bank_free(pe, A_BANKS, read, "gate", local, i, turn)
                pe.wait_ge(wk_ctx_set, b + 1)
                nc.tensor.matmul(banks[6 + A_BANKS.bank("gate", local, turn)][:, 0:KS], ones[:, :], wk_ctx[:, :],
                                 start=True, stop=True).then_inc(made["gate"], 1)

            def project(kind, i, local, turn, m, b):
                bank_free(pe, A_BANKS, read, kind, local, i, turn)
                pe.wait_ge(hT_set, b + 1)
                bank = banks[6 + A_BANKS.bank(kind, local, turn)]
                for k in range(2):
                    dst = bank[:, 256 * k:256 * (k + 1)]
                    if kind == "q":
                        ins = nc.tensor.matmul(dst, wq[:, P * (2 * m + k):P * (2 * m + k + 1)], hT[:, :], start=True, stop=True)
                    elif kind == "k":
                        ins = nc.tensor.matmul(dst, wk2[:, 2 * m + k, :, :], hT[:, :], start=True, stop=True)
                    else:
                        ins = nc.tensor.matmul(dst, hT[:, P * k:P * (k + 1)], wv[:, :], start=True, stop=True)
                ins.then_inc(made[kind], 1)

            def pre():
                pe.wait_ge(weights_in, 16 * N_WEIGHTS)
                pe.wait_ge(consts_set, N_CONSTS)
                transpose_x(0, 0, "pre", 0)
                gate_matmul(0, 0, "pre", 0)
                for kind, local in A_BANKS.pre[2:]:
                    project(kind, 0, local, "pre", local, 0)

            def body(i, turn):
                for s, slot, p, tile, g in steps(i, turn):
                    late = exists(turn, s, PV_LAG)
                    if late:
                        n = A_STEPS * i + s - PV_LAG
                        e = E[(s - PV_LAG) % E_RING]
                        pe.wait_ge(normed, n + 1)
                        for hp in range(2):
                            wait(pe, wT_read, 2 * (n - 1) + hp + 1)
                            for kb in range(TILES):
                                for hh in range(2):
                                    ins = nc.tensor.transpose(banks[4 + hp][:, P * (2 * kb + hh):P * (2 * kb + hh + 1)],
                                                              e[:, 2 * hh + hp, 2 * kb:2 * kb + 2, :], ident[:, :])
                            ins.then_inc(wT_made, 1)
                    if exists(turn, s):
                        n = A_STEPS * i + s
                        if g == 0:
                            b = PAIR * i + p
                            pe.wait_ge(read["q"], 4 * b + 4)
                            pe.wait_ge(read["k"], 2 * b + 2)
                        wait(pe, sub_done, n - 1)
                        for h in range(A_REP):
                            lo = A_HD * (h % 2)
                            ins = nc.tensor.matmul(
                                banks[2 * (s % 2) + h % 2][:, SEQ * (h // 2):SEQ * (h // 2 + 1)],
                                qT[p][lo:lo + A_HD, 2 * g + h // 2, P * tile:P * (tile + 1)],
                                kT[p][lo:lo + A_HD, g, :], start=True, stop=True)
                        ins.then_inc(scored, 1)
                    if prepares(turn, p):
                        b = PAIR * i + p + 1
                        if tile == 0 and g == 0:
                            transpose_x(i, p + 1, turn, b)
                        if tile == 0 and g == 2:
                            gate_matmul(i, p + 1, turn, b)
                        if tile == 1:
                            for kind, per, m in A_PROJECTIONS[g]:
                                project(kind, i, per * (p + 1) + m, turn, m, b)
                    if late:
                        n = A_STEPS * i + s - PV_LAG
                        at, og = divmod(s - PV_LAG, A_KV)
                        ap = (at // TILES) % PAIR
                        bank = banks[6 + A_BANKS.bank("o", s - PV_LAG, "middle")]
                        bank_free(pe, A_BANKS, read, "o", s - PV_LAG, i, turn)
                        if og == 0:
                            pe.wait_ge(read["v"], PAIR * i + at // TILES + 1)
                        for hp in range(2):
                            pe.wait_ge(wT_read, 2 * n + hp + 1)
                            for kb in range(TILES):
                                for hh in range(2):
                                    ins = nc.tensor.matmul(
                                        bank[A_HD * hh:A_HD * (hh + 1), P * hp:P * (hp + 1)],
                                        v[ap][:, kb, A_HD * og:A_HD * (og + 1)], wT[hp][:, kb, hh, :],
                                        start=(kb == 0), stop=(kb == TILES - 1))
                            ins.then_inc(pv_done, 1)
                    if g == OUT_LAG % A_KV and exists(turn, s, OUT_LAG):
                        at = (s - OUT_LAG) // A_KV
                        j = A_SLOTS * i + at
                        bank_free(pe, A_BANKS, read, "out", at, i, turn)
                        pe.wait_ge(read["o"], A_KV * j + A_KV)
                        for m in range(A_HEADS // 2):
                            ins = nc.tensor.matmul(banks[6 + A_BANKS.bank("out", at, "middle")][:, 0:DIM], oT[at % 2][:, m, :], wo[:, m, :],
                                                   start=(m == 0), stop=(m == A_HEADS // 2 - 1))
                        ins.then_inc(made["out"], 1)

            stage_a(pe, body, pre)

            def attention(layer):
                free = lambda kind, local, it, turn: bank_free(pe, F_BANKS, f_read, kind, local, it, turn)

                def prepare(it, kind, local, m, batch, turn):
                    par = (local // (F_BANKS.stride[kind] // PAIR)) % PAIR
                    bank = banks[6 + F_BANKS.bank(kind, local, turn)]
                    free(kind, local, it, turn)
                    if kind == "hT":
                        pe.wait_ge(hn_in[par], 64 * (TURNS * layer + it + local // PAIR + 1))
                        for tt in range(TILES):
                            ins = nc.tensor.transpose(bank[:, P * tt:P * (tt + 1)], hn[par][:, tt, :], ident[:, :])
                    elif kind in ("qk", "v"):
                        tile, k = divmod(m, 2) if kind == "qk" else (m, 2)
                        pe.wait_ge(f_read["hT"], batch + 1)
                        ins = nc.tensor.matmul(bank[:, :], fhT[:, P * tile:P * (tile + 1)], wqkv[layer][:, INNER * k:INNER * (k + 1)],
                                               start=True, stop=True)
                    else:
                        pe.wait_ge(qk_normed, F_BANKS.stride[kind] * it + local + 1)
                        flat = qk[m][:, :, :].rearrange("p h d -> p (h d)")
                        for block_of in range(4):
                            ins = nc.tensor.transpose(bank[:, P * block_of:P * (block_of + 1)],
                                                      flat[:, P * block_of:P * (block_of + 1)], ident[:, :])
                    ins.then_inc(f_made[kind], 1)

                def pre():
                    if layer == 0:
                        pe.wait_ge(f_consts, N_F_CONSTS)
                        pe.wait_ge(read["out"], BATCH * TILES)
                    else:
                        pe.wait_ge(down_read, BATCH * layer)
                        pe.wait_ge(u_done, 3 * BATCH * layer)
                    for kind, local in F_BANKS.pre:
                        per = F_BANKS.stride[kind] // PAIR
                        prepare(TURNS * layer, kind, local, local % per, PAIR * TURNS * layer + local // per, "pre")

                def body(i, it, turn):
                    for s, slot, p, tile, g in f_steps(turn):
                        n = F_STEPS * it + s
                        late = exists(turn, s, F_PV_LAG)
                        late_slot, late_g = divmod(s - F_PV_LAG, F_GROUPS)
                        late_p, late_tile = (late_slot // TILES) % PAIR, late_slot % TILES
                        if late:
                            pe.wait_ge(f_exp, n - F_PV_LAG + 1)
                            wait(pe, eT_read, n - F_PV_LAG)
                            e = fE[(s - F_PV_LAG) % F_RING]
                            own = keys(late_tile)[0] - P
                            if late_tile == 1:
                                wait(pe, f_o_read, n - F_PV_LAG)
                                wait(pe, back_read, F_GROUPS * (PAIR * it + late_slot // TILES) + late_g)
                            for h in range(F_GH):
                                ins = nc.tensor.transpose(banks[4][:, P * h:P * (h + 1)], e[:, h % 2, h // 2, own:own + P], ident[:, :])
                            if late_tile == 1:
                                for h in range(F_GH):
                                    ins = nc.tensor.transpose(banks[5][0:WINDOW, P * h:P * (h + 1)], e[:, h % 2, h // 2, 0:own], ident[:, :])
                            ins.then_inc(eT_made, 1)
                        if exists(turn, s):
                            n_keys, first_key = keys(tile)
                            if g == 0:
                                pe.wait_ge(f_read["qkT"], 4 * (PAIR * it + p) + 2 * tile + 2)
                            wait(pe, f_sub, n - 1)
                            m0 = 2 * P * tile
                            for k in range(2):
                                nc.tensor.matmul(banks[2 * (s % 2) + k][:, 0:2 * n_keys], ident16[:, :], mask[:, m0:m0 + 2 * n_keys],
                                                 start=True, stop=False)
                            for h in range(F_GH):
                                head = F_GH * g + h
                                lo = F_HD * (h % 2)
                                ins = nc.tensor.matmul(
                                    banks[2 * (s % 2) + h % 2][:, n_keys * (h // 2):n_keys * (h // 2 + 1)],
                                    qkT[p][lo:lo + F_HD, head // 2, P * tile:P * (tile + 1)],
                                    qkT[p][lo:lo + F_HD, 4 + head // 2, first_key:first_key + n_keys],
                                    start=False, stop=(h >= 2))
                            ins.then_inc(f_scored, 1)
                        if late:
                            bank = banks[5]
                            wait(pe, f_o_read, n - F_PV_LAG)
                            if late_g == 0:
                                pe.wait_ge(f_read["v"], 2 * (PAIR * it + late_slot // TILES) + late_tile + 1)
                            pe.wait_ge(eT_read, n - F_PV_LAG + 1)
                            if late_tile == 1:
                                pe.wait_ge(back_read, F_GROUPS * (PAIR * it + late_slot // TILES) + late_g + 1)
                            for h in range(F_GH):
                                dst = bank[:, (F_HD + 1) * h:(F_HD + 1) * (h + 1)]
                                ins = nc.tensor.matmul(dst, eT[:, h, :], v1s[late_p][:, late_tile, F_GH * late_g + h, :],
                                                       start=True, stop=(late_tile == 0))
                                if late_tile == 1:
                                    ins = nc.tensor.matmul(dst, eT_back[:, h, :], v1s[late_p][:, 0, F_GH * late_g + h, :],
                                                           start=False, stop=True)
                            ins.then_inc(f_o_made, 1)
                        for kind, local, m, ahead in f_fills(turn, s):
                            if kind not in ("oT", "out"):
                                prepare(it, kind, local, m, PAIR * it + p + ahead, turn)
                                continue
                            j = F_SLOTS * it + local
                            free(kind, local, it, turn)
                            bank = banks[6 + F_BANKS.bank(kind, local, "middle")]
                            if kind == "oT":
                                pe.wait_ge(f_o_read, F_GROUPS * j + F_GROUPS)
                                flat = o_nat[local % 2][:, :, :].rearrange("p h d -> p (h d)")
                                for m in range(INNER // P):
                                    ins = nc.tensor.transpose(bank[:, P * m:P * (m + 1)], flat[:, P * m:P * (m + 1)], ident[:, :])
                            else:
                                pe.wait_ge(f_read["oT"], j + 1)
                                for m in range(INNER // P):
                                    ins = nc.tensor.matmul(bank[:, 0:DIM], foT[:, m, :], wof[layer][:, m, :],
                                                           start=(m == 0), stop=(m == INNER // P - 1))
                            ins.then_inc(f_made[kind], 1)

                over_turns(pe, layer, body, pre)

            def mlp(layer):
                def transpose_h(par, bb):
                    pe.wait_ge(hc_set, bb + 1)
                    wait(pe, hT2_read, bb)
                    for tile in range(TILES):
                        ins = nc.tensor.transpose(banks[6][:, P * tile:P * (tile + 1)], hc[par][:, tile, :], ident[:, :])
                    ins.then_inc(hT2_made, 1)

                def pre():
                    pe.wait_ge(f_read["out"], BATCH * TILES * (layer + 1))
                    transpose_h(0, PAIR * TURNS * layer)

                def body(i, it, turn):
                    for p in range(PAIR):
                        b, bb = PAIR * i + p, PAIR * it + p
                        if turn != "drain":
                            pe.wait_ge(hT2_read, bb + 1)
                            for c, rows in enumerate(F_ROWS):
                                wait(pe, u_done, 3 * (bb - 2) + c + 1)
                                for a in range(2):
                                    at = F_HID * a + P * c
                                    ins = nc.tensor.matmul(banks[3 * p + c][0:rows, SEQ * a:SEQ * (a + 1)],
                                                           w1[layer][:, at:at + rows], hT2[p][:, :], start=True, stop=True)
                                ins.then_inc(up_made, 1)
                        if prepares(turn, p):
                            transpose_h(1 - p, bb + 1)
                        if not (turn == "first" and p == 0) and not (turn == "drain" and p >= 1):
                            other = 1 - p
                            pe.wait_ge(u_done, 3 * bb)
                            wait(pe, down_read, bb - 1)
                            for tile in range(TILES):
                                for c, rows in enumerate(F_ROWS):
                                    ins = nc.tensor.matmul(banks[7][:, DIM * tile:DIM * (tile + 1)],
                                                           uT[other][0:rows, c, P * tile:P * (tile + 1)], w2[layer][0:rows, c, :],
                                                           start=(c == 0), stop=(c == F_CHUNKS - 1))
                            ins.then_inc(down_made, 1)

                over_turns(pe, layer, body, pre)

            for layer in range(LAYERS):
                attention(layer)
                mlp(layer)


def rotary_tables():
    f32 = np.float32
    half = np.arange(0, F_HD, 2, dtype=f32)
    inv_freq = f32(1.0) / np.power(f32(10000.0), half / f32(F_HD)).astype(f32)
    tok = np.arange(SEQ, dtype=f32)
    freqs = tok[:, None] * inv_freq[None, :]
    freqs = np.concatenate([freqs, freqs], axis=-1)
    base = (half + f32(0.4 * F_HD)) / f32(1.4 * F_HD)
    power = (tok - SEQ // 2) / f32(WINDOW // 2)
    scale = np.power(base[None, :].astype(np.float64), power[:, None].astype(np.float64))
    scale = np.concatenate([scale, scale], axis=-1)
    cos, sin = np.cos(freqs.astype(np.float64)), np.sin(freqs.astype(np.float64))
    sin = sin * np.where(np.arange(F_HD) < F_HD // 2, -1.0, 1.0)
    tabs = np.stack([cos * scale * QK_SCALE, sin * scale * QK_SCALE, cos / scale, sin / scale], axis=1)
    return tabs.astype(f32)


def score_mask():
    q, own = np.arange(P)[:, None], np.arange(P)[None, :]
    first = (own <= q) & (own >= q - WINDOW)
    key = np.arange(F_KEYS)[None, :] - WINDOW
    second = (key <= q) & (key >= q - WINDOW)
    return np.where(np.concatenate([first, first, second, second], axis=1), 0.0, MASKED).astype(np.float32)


def kernel(**inputs):
    import concourse.bacc as bacc
    from concourse.bass_utils import run_bass_kernel_spmd

    nc = bacc.Bacc("TRN2", target_bir_lowering=False, num_devices=1)
    f = {k: np.asarray(a) for k, a in inputs.items()}
    arrays = {
        "x": f["L0_attn_hidden_states"],
        "wqT": f["L0_attn_w_q"].T, "wkT": f["L0_attn_w_k"].T, "wvT": f["L0_attn_w_v"].T, "woT": f["L0_attn_w_o"].T,
        "wkgenT": f["L0_attn_w_kgen"].T, "bkgen": f["L0_attn_b_kgen"],
        "wconv": f["L0_attn_w_conv"].reshape(DIM, KS), "bconv": f["L0_attn_b_conv"],
        "wqkv": f["L0_ffn_wqkv"], "q_scale": f["L0_ffn_q_scale"], "k_scale": f["L0_ffn_k_scale"], "wof": f["L0_ffn_wo"],
        "ln_g": f["L0_ffn_ln_g"], "ln_b": f["L0_ffn_ln_b"], "w1": f["L0_ffn_w1"], "b1": f["L0_ffn_b1"],
        "w2": f["L0_ffn_w2"], "b2": f["L0_ffn_b2"],
        "eye": np.eye(P, dtype=np.float32), "rotary": rotary_tables(), "mask": score_mask(),
    }
    arrays = {f"in_{k}": np.ascontiguousarray(a) for k, a in arrays.items()}
    t = {k[3:]: nc.dram_tensor(k, a.shape, mybir.dt.from_np(a.dtype), kind="ExternalInput").ap() for k, a in arrays.items()}
    for name in ("x1", "x2", "x3", "x4"):
        t[name] = nc.dram_tensor(f"stage_{name}", (BATCH, SEQ, DIM), FP32, kind="Internal").ap()
    t["out"] = nc.dram_tensor("out_x", (BATCH, SEQ, DIM), FP32, kind="ExternalOutput").ap()
    build(nc, t)
    r = run_bass_kernel_spmd(nc, [arrays], core_ids=[0])
    return r.results[0]["out_x"]
```

```python
import concourse.bass as bass
from concourse import mybir
from contextlib import ExitStack
import math

import numpy as np

FP32 = mybir.dt.float32
BF16 = mybir.dt.bfloat16
ALU = mybir.AluOpType
ACT = mybir.ActivationFunctionType
AX = mybir.AxisListType

BATCH, SEQ, DIM = 16, 256, 128
P = 128
TILES = SEQ // P
A_HEADS, A_KV, A_HD = 16, 4, 64
A_REP = A_HEADS // A_KV
CHUNK = 64
CHUNKS = SEQ // CHUNK
KS = 3
LAYERS, F_HEADS, F_HD, WINDOW = 2, 8, 64, 64
INNER = F_HEADS * F_HD
F_HID = int(DIM * 4 * 2 / 3)
LN_EPS = 1e-5

PAIR = 2
TURNS = BATCH // PAIR
A_SLOTS = PAIR * TILES
A_STEPS = A_SLOTS * A_KV
E_RING = 8
EXP_LAG, SUM_LAG, NORM_LAG, PV_LAG, OUT_LAG, LN_LAG = 1, 2, 5, 7, 11, 14
F_GROUPS = 2
F_GH = F_HEADS // F_GROUPS
F_SLOTS = PAIR * TILES
F_STEPS = F_SLOTS * F_GROUPS
F_BATCH = TILES * F_GROUPS
F_EXP_LAG, F_SUM_LAG, F_NORM_LAG, F_PV_LAG = 1, 2, 2, 4
F_LATE = {
    "out": (6, F_GROUPS),
    "stats": (10, F_BATCH), "norm": (11, F_BATCH), "mT": (13, F_BATCH),
    "gates": (14, F_BATCH), "mix": (14, F_BATCH), "residual": (14, F_BATCH), "values": (16, F_BATCH),
    "down": (17, F_BATCH), "z": (18, F_BATCH),
}
F_KEYS = P + WINDOW
F_RING = 4
F_CHUNKS = -(-F_HID // P)
F_ROWS = [min(P, F_HID - P * c) for c in range(F_CHUNKS)]
QK_SCALE = 8.0
MASKED = -1e30


def wait(engine, sem, value):
    if isinstance(value, int) and value <= 0:
        return
    engine.wait_ge(sem, value)


class SharedBanks:

    BEFORE = {"drain2": "drain", "drain": "last", "last": "middle", "middle": "middle", "second": "first", "first": "pre"}

    def __init__(self, order, pre, stride, late):
        assert len(order) % 2 == 0
        self.order, self.pre, self.stride, self.late = order, pre, stride, late

    def bank(self, kind, local, turn):
        if turn == "pre":
            return (self.pre.index((kind, local)) + len(self.pre)) % 2
        return self.order.index((kind, local)) % 2

    def left_out(self, turn, kind, local):
        if kind in self.late:
            if turn in ("first", "second"):
                return self.stride[kind] * (turn == "second") + local < 0
            return turn in ("drain", "drain2") and self.stride[kind] * (turn == "drain2") + local >= 0
        return turn in ("drain", "drain2") or turn == "last" and local // (self.stride[kind] // PAIR) >= PAIR

    def before(self, kind, local, turn):
        if turn == "pre":
            at = self.pre.index((kind, local)) - 2
            return (*self.pre[at], 0) if at >= 0 else None
        back, shift, at = self.order.index((kind, local)) - 2, 0, turn
        while True:
            if back < 0:
                at, shift, back = self.BEFORE[at], shift - 1, back + len(self.order)
                if at == "pre":
                    same = [f for f in self.pre if self.bank(*f, "pre") == back % 2]
                    return (*same[-1], 0)
            if not self.left_out(at, *self.order[back]):
                return (*self.order[back], shift)
            back -= 2


def stage_a_banks():
    order = []
    for s in range(A_STEPS):
        slot, g = divmod(s, A_KV)
        p, tile = divmod(slot, TILES)
        if tile == 0 and g == 0:
            order.append(("xT", p + 1))
        if tile == 0 and g == 2:
            order.append(("gate", p + 1))
        if tile == 1:
            order += [(k, per * (p + 1) + m) for k, per, m in A_PROJECTIONS[g]]
        order.append(("o", s - PV_LAG))
        if g == OUT_LAG % A_KV:
            order.append(("out", (s - OUT_LAG) // A_KV))
    pre = [("xT", 0), ("gate", 0)] + [(k, m) for g in range(A_KV) for k, per, m in A_PROJECTIONS[g]]
    stride = {"xT": PAIR, "gate": PAIR, "k": 2 * PAIR, "q": 4 * PAIR, "v": PAIR, "o": A_STEPS, "out": A_SLOTS}
    return SharedBanks(order, pre, stride, ("o", "out"))


A_PROJECTIONS = {0: [], 1: [("k", 2, 0), ("k", 2, 1), ("q", 4, 0)], 2: [("q", 4, 1), ("q", 4, 2)], 3: [("q", 4, 3), ("v", 1, 0)]}


F_FILLS = {
    0: ["out", "values", ("qk", 4, 0, 1)],
    1: [("qk", 4, 1, 1), "down", ("qkT", 4, 2, 0), ("qkT", 4, 3, 0), "mT"],
    2: ["out", ("qk", 4, 2, 1), "gates", "mix"],
    3: [("qkT", 4, 0, 1), ("v", 2, 0, 1), ("qkT", 4, 1, 1), ("v", 2, 1, 1), ("qk", 4, 3, 1), ("hT", 1, 0, 2)],
}


def stage_f_banks():
    order = []
    for s in range(F_STEPS):
        p, at = divmod(s, F_BATCH)
        for fill in F_FILLS[at]:
            if isinstance(fill, str):
                lag, every = F_LATE[fill]
                order.append((fill, (s - lag) // every))
            else:
                kind, per, m, ahead = fill
                order.append((kind, per * (p + ahead) + m))
    prepared = [f for at in range(F_BATCH) for f in F_FILLS[at] if not isinstance(f, str) and f[3] == 1]
    pre = [("hT", 0)] + [(k, m) for kind in ("qk", "v", "qkT") for k, per, m, _ in prepared if k == kind] + [("hT", 1)]
    late = ("out", "mT", "gates", "mix", "values", "down")
    stride = {"hT": PAIR, "qk": 4 * PAIR, "v": 2 * PAIR, "qkT": 4 * PAIR, **{k: F_STEPS // F_LATE[k][1] for k in late}}
    return SharedBanks(order, pre, stride, late)


A_BANKS, F_BANKS = stage_a_banks(), stage_f_banks()


def build(nc, t):
    ctx = ExitStack()
    with ctx:
        def sb(name, shape, dt=FP32):
            return ctx.enter_context(nc.sbuf_tensor(name, shape, dt))

        def sem(name):
            return ctx.enter_context(nc.semaphore(name))

        banks = [ctx.enter_context(nc.psum_tensor(f"bank{i}", [P, 512], FP32)) for i in range(8)]
        x_in = t["x"].rearrange("b (t p) d -> p b t d", p=P)
        x1, x2, x3, x4, x_out = (t[k].rearrange("b (t p) d -> p b t d", p=P) for k in ("x1", "x2", "x3", "x4", "out"))

        ident = sb("ident", [P, P])
        ones = sb("ones", [P, P])
        halves = sb("halves", [P, 32])
        eps = sb("eps", [P, TILES])
        wq = sb("wq", [P, A_HEADS * A_HD])
        wk2 = sb("wk2", [P, A_KV, 2, A_HD])
        wv = sb("wv", [P, A_KV * A_HD])
        wo = sb("wo", [P, A_HEADS // 2, DIM])
        wkgen = sb("wkgen", [P, KS])
        bkgen = sb("bkgen", [P, KS])
        wconv = sb("wconv", [P, KS])
        bconv = sb("bconv", [P, 1])

        xn = [sb(f"xn{p}", [P, TILES, DIM]) for p in range(PAIR)]
        xr = [sb(f"xr{p}", [P, TILES, DIM]) for p in range(PAIR)]
        xT = sb("xT", [P, SEQ + 2])
        ctx_sum = sb("ctx_sum", [P, 1])
        wk_ctx = sb("wk_ctx", [P, KS])
        gate = sb("gate", [P, 4, KS])
        gate_sum = sb("gate_sum", [P, 1])
        conv = sb("conv", [P, 3, SEQ])
        hT = sb("hT", [P, SEQ])
        qT = [sb(f"qT{p}", [P, A_HEADS // 2, SEQ]) for p in range(PAIR)]
        kT = [sb(f"kT{p}", [P, A_KV, SEQ]) for p in range(PAIR)]
        v = [sb(f"v{p}", [P, TILES, A_KV * A_HD]) for p in range(PAIR)]
        probs = sb("probs", [P, E_RING, A_REP * SEQ])
        E = [probs[:, r, :].rearrange("p (h c k) -> p h c k", h=A_REP, c=CHUNKS) for r in range(E_RING)]
        mx = [sb(f"mx{r}", [P, A_REP, CHUNKS]) for r in range(2)]
        sums = [sb(f"sums{r}", [P, A_HEADS, CHUNKS]) for r in range(2)]
        coef = [sb(f"coef{r}", [P, 3, A_HEADS, CHUNKS]) for r in range(2)]
        total = [sb(f"total{r}", [P, 3, A_HEADS]) for r in range(2)]
        wT = [sb(f"wT{r}", [P, TILES, 2, P]) for r in range(2)]
        oT = [sb(f"oT{r}", [P, A_HEADS // 2, P]) for r in range(2)]
        y = [sb(f"y{r}", [P, DIM]) for r in range(2)]
        stat = [sb(f"stat{r}", [P, 6]) for r in range(2)]
        mv = [sb(f"mv{r}", [P, 2]) for r in range(2)]
        rstd = [sb(f"rstd{r}", [P, 2]) for r in range(2)]
        xo = [sb(f"xo{r}", [P, DIM]) for r in range(2)]

        wqkv = [sb(f"wqkv{l}", [P, 3 * INNER]) for l in range(LAYERS)]
        wof = [sb(f"wof{l}", [P, INNER // P, DIM]) for l in range(LAYERS)]
        w1 = [sb(f"w1_{l}", [P, 2 * F_HID]) for l in range(LAYERS)]
        w2 = [sb(f"w2_{l}", [P, F_CHUNKS, DIM]) for l in range(LAYERS)]
        b1 = [sb(f"b1_{l}", [P, 2, F_CHUNKS]) for l in range(LAYERS)]
        b2 = [sb(f"b2_{l}", [P, DIM]) for l in range(LAYERS)]
        ln_g = [sb(f"ln_g{l}", [P, 1]) for l in range(LAYERS)]
        ln_b = [sb(f"ln_b{l}", [P, 1]) for l in range(LAYERS)]
        rotary = sb("rotary", [P, TILES, 4, F_HD])
        qk_scale = [sb(f"qk_scale{l}", [P, 4, F_HD]) for l in range(LAYERS)]
        table = [sb(f"table{l}", [P, TILES, 4, F_HD]) for l in range(LAYERS)]
        mask = sb("mask", [P, 2 * (P + F_KEYS)], BF16)
        ident16 = sb("ident16", [P, P], BF16)

        hn = [sb(f"hn{p}", [P, TILES, DIM]) for p in range(PAIR)]
        fhT = sb("fhT", [P, SEQ])
        raw = [sb(f"raw{r}", [P, F_HEADS, F_HD]) for r in range(2)]
        sq = [sb(f"sq{r}", [P, INNER]) for r in range(2)]
        on_self = [sb(f"on_self{r}", [P, F_HEADS, F_HD]) for r in range(2)]
        on_partner = [sb(f"on_partner{r}", [P, F_HEADS, F_HD]) for r in range(2)]
        qk = [sb(f"qk{m}", [P, F_HEADS, F_HD]) for m in range(4)]
        norm2 = sb("norm2", [P, 2, 4 * F_HEADS])
        rnorm = sb("rnorm", [P, 4 * F_HEADS])
        qkT = [probs[:, 2 * p:2 * p + 2, :].rearrange("p r (m q) -> p (r m) q", q=SEQ) for p in range(PAIR)]
        f_v = [sb(f"f_v{p}", [P, TILES, F_HEADS, F_HD]) for p in range(PAIR)]
        fE = [probs[:, 4 + r, 0:F_GH * F_KEYS].rearrange("p (k a n) -> p k a n", k=2, a=2) for r in range(F_RING)]
        fmx = [sb(f"fmx{r}", [P, 2, 2]) for r in range(2)]
        eT = sb("eT", [P, F_GH, P])
        eT_back = sb("eT_back", [P, F_GH, P])
        f_sum = [sb(f"f_sum{r}", [P, 2, 2]) for r in range(2)]
        f_rsum = [sb(f"f_rsum{r}", [P, 2, 2]) for r in range(2)]
        foT = [sb(f"foT{r}", [P, INNER // P, P]) for r in range(2)]

        hc = [sb(f"hc{p}", [P, TILES, DIM]) for p in range(PAIR)]
        hT2 = [sb(f"hT2_{p}", [P, SEQ]) for p in range(PAIR)]
        ge = [sb(f"ge{c}", [P, SEQ]) for c in range(F_CHUNKS)]
        uT = [sb(f"uT{p}", [P, F_CHUNKS, SEQ]) for p in range(PAIR)]
        mask32 = uT[1][:, :, :].rearrange("p c n -> p (c n)")[:, 0:2 * (P + F_KEYS)]
        mn = [sb(f"mn{p}", [P, TILES, DIM]) for p in range(PAIR)]
        res = [sb(f"res{p}", [P, TILES, DIM]) for p in range(PAIR)]
        m_res = [sb(f"m_res{p}", [P, TILES, DIM]) for p in range(PAIR)]
        res1 = [sb(f"res1_{p}", [P, TILES, DIM]) for p in range(PAIR)]
        resb = [sb(f"resb{p}", [P, 2, TILES, DIM]) for p in range(PAIR)]
        yo = [sb(f"yo{p}", [P, TILES, DIM]) for p in range(PAIR)]
        zo = [sb(f"zo{p}", [P, TILES, DIM]) for p in range(PAIR)]
        mstat = [sb(f"mstat{p}", [P, TILES, 6]) for p in range(PAIR)]
        mmv = [sb(f"mmv{p}", [P, TILES, 2]) for p in range(PAIR)]
        mrstd = [sb(f"mrstd{p}", [P, 2, TILES]) for p in range(PAIR)]
        zstat = [sb(f"zstat{p}", [P, TILES, 6]) for p in range(PAIR)]
        zmv = [sb(f"zmv{p}", [P, TILES, 2]) for p in range(PAIR)]
        zrstd = [sb(f"zrstd{p}", [P, 2, TILES]) for p in range(PAIR)]

        gate_weights_in, a_weights_in, weights_in = sem("gate_weights_in"), sem("a_weights_in"), sem("weights_in")
        ident_step, consts_set, pool_const = sem("ident_step"), sem("consts_set"), sem("pool_const")
        xn_in = [sem(f"xn{p}_in") for p in range(PAIR)]
        xr_in = [sem(f"xr{p}_in") for p in range(PAIR)]
        xo_out = [sem(f"xo{r}_out") for r in range(2)]
        made = {k: sem(f"{k}_made") for k in A_BANKS.stride}
        read = {k: sem(f"{k}_read") for k in A_BANKS.stride}
        wk_ctx_set, gate_exp, gate_step, conv_step, hT_set = (
            sem(n) for n in ("wk_ctx_set", "gate_exp", "gate_step", "conv_step", "hT_set"))
        scored, max_set, sub_done, exp_done, sum_done, coef_step, normed = (
            sem(n) for n in ("scored", "max_set", "sub_done", "exp_done", "sum_done", "coef_step", "normed"))
        wT_made, wT_read, pv_done = sem("wT_made"), sem("wT_read"), sem("pv_done")
        stats_waited, y_step, eps_added, rstd_set, xo_set = sem("stats_waited"), sem("y_step"), sem("eps_added"), sem("rstd_set"), sem("xo_set")

        f_made = {k: sem(f"f_{k}_made") for k in F_BANKS.stride}
        f_read = {k: sem(f"f_{k}_read") for k in F_BANKS.stride if k not in ("gates", "mix", "values")}
        gelu_done, u_done = sem("gelu_done"), sem("u_done")
        f_read.update(gates=gelu_done, mix=u_done, values=u_done)
        READ_COUNTS = {"gates": (F_CHUNKS, 2), "mix": (F_CHUNKS, 1), "values": (F_CHUNKS, F_CHUNKS)}
        f_o_made, f_o_read = sem("f_o_made"), sem("f_o_read")
        hn_in = [sem(f"hn{p}_in") for p in range(PAIR)]
        res_in = [sem(f"res{p}_in") for p in range(PAIR)]
        mn_in = [sem(f"mn{p}_in") for p in range(PAIR)]
        m_res_in = [sem(f"m_res{p}_in") for p in range(PAIR)]
        res1_in = [sem(f"res1_{p}_in") for p in range(PAIR)]
        f_out = [sem(f"f_out{r}") for r in range(2)]
        m_out = [sem(f"m_out{p}") for p in range(PAIR)]
        tables_set, f_consts = sem("tables_set"), sem("f_consts")
        squared, rotated, norm_step, guarded, added, rnorm_set, qk_normed = (
            sem(n) for n in ("squared", "rotated", "norm_step", "guarded", "added", "rnorm_set", "qk_normed"))
        f_scored, f_max, f_sub, f_exp, f_sum_set, f_rsum_set, f_normed, eT_made, eT_read, back_read = (
            sem(n) for n in ("f_scored", "f_max", "f_sub", "f_exp", "f_sum_set", "f_rsum_set", "f_normed", "eT_made", "eT_read", "back_read"))
        m_bn, m_stats, m_eps, m_rstd, hc_set, resb_step = (
            sem(n) for n in ("m_bn", "m_stats", "m_eps", "m_rstd", "hc_set", "resb_step"))
        z_bn, z_stats, z_eps, z_rstd, z_set = (sem(n) for n in ("z_bn", "z_stats", "z_eps", "z_rstd", "z_set"))

        block = ctx.enter_context(nc.Block())
        COEF_STEPS = 7
        N_GATE_WEIGHTS, N_A_WEIGHTS, N_WEIGHTS = 5, 5, 2 + LAYERS * (6 + 3 * F_CHUNKS + 6)
        N_CONSTS, N_F_CONSTS = 5, 7
        GATE_STEPS = 3

        def stage_a(engine, body, pre=None):
            if pre:
                pre()
            body(0, "first")
            with engine.Fori(1, TURNS - 1) as i:
                body(i, "middle")
            body(TURNS - 1, "last")
            body(TURNS, "drain")

        def f_steps(turn):
            for s in range(F_STEPS):
                slot, g = divmod(s, F_GROUPS)
                yield (s, slot, *divmod(slot, TILES), g)

        def f_fills(turn, s):
            p, at = divmod(s, F_BATCH)
            for fill in F_FILLS[at]:
                if isinstance(fill, str):
                    index = f_late(turn, s, fill)
                    if index is not None:
                        yield fill, index, 0, 0
                elif prepares(turn, p, fill[3]):
                    kind, per, m, ahead = fill
                    yield kind, per * (p + ahead) + m, m, ahead

        def f_late(turn, s, kind):
            lag, every = F_LATE[kind]
            if (s - lag) % every or not f_exists(turn, s, lag):
                return None
            return (s - lag) // every

        def f_exists(turn, s, lag=0):
            if turn in ("first", "second"):
                return F_STEPS * (turn == "second") + s >= lag
            return turn not in ("drain", "drain2") or F_STEPS * (turn == "drain2") + s < lag

        def over_turns(engine, layer, body, pre=None):
            if pre:
                pre()
            first = TURNS * layer
            body(0, first, "first")
            body(1, first + 1, "second")
            with engine.Fori(2, TURNS - 1) as i:
                body(i, first + i, "middle")
            body(TURNS - 1, first + TURNS - 1, "last")
            body(TURNS, first + TURNS, "drain")
            body(TURNS + 1, first + TURNS + 1, "drain2")

        def keys(tile):
            return (P, 0) if tile == 0 else (F_KEYS, P - WINDOW)

        def steps(i, turn):
            for s in range(A_STEPS if turn != "drain" else LN_LAG):
                slot, g = divmod(s, A_KV)
                p, tile = divmod(slot, TILES)
                yield s, slot, p, tile, g

        def exists(turn, s, lag=0):
            return not (turn == "first" and s < lag) and not (turn == "drain" and s >= lag)

        def prepares(turn, p, ahead=1):
            return turn not in ("drain", "drain2") and not (turn == "last" and p + ahead >= PAIR)

        def bank_free(pe, shared, read, kind, local, i, turn):
            last = shared.before(kind, local, turn)
            if last:
                kind_before, index, turns_back = last
                step, offset = READ_COUNTS.get(kind_before, (1, 1))
                wait(pe, read[kind_before], step * (shared.stride[kind_before] * (i + turns_back) + index) + offset)

        def layer_weights(l):
            half = F_HD // 2
            yield wqkv[l][:, :], t["wqkv"][l]
            yield wof[l][:, :, :], t["wof"][l].rearrange("(m p) n -> p m n", p=P)
            yield w1[l][:, :], t["w1"][l]
            yield b2[l][:, :], t["b2"][l].partition_broadcast(P)
            yield ln_g[l][:, :], t["ln_g"][l].rearrange("(p a) -> p a", a=1)
            yield ln_b[l][:, :], t["ln_b"][l].rearrange("(p a) -> p a", a=1)
            for c, rows in enumerate(F_ROWS):
                yield w2[l][0:rows, c, :], t["w2"][l, P * c:P * c + rows, :]
                for a in range(2):
                    at = F_HID * a + P * c
                    yield b1[l][0:rows, a, c:c + 1], t["b1"][l, at:at + rows].rearrange("(p a) -> p a", a=1)
            for a, name in enumerate(("q_scale", "k_scale")):
                yield qk_scale[l][:, 2 * a, :], t[name][l].partition_broadcast(P)
                yield qk_scale[l][:, 2 * a + 1, 0:half], t[name][l, half:].partition_broadcast(P)
                yield qk_scale[l][:, 2 * a + 1, half:], t[name][l, 0:half].partition_broadcast(P)

        @block.sync
        def _(sp):
            def load(dst, b, done, x_in=x_in):
                sp.dma_start(dst[:, :, :], x_in[:, bass.ds(b, 1), :, :]).then_inc(done, 16)

            def pre():
                load(xn[0], 0, xn_in[0])
                for dst, src in (
                    (ident[:, :], t["eye"]), (wkgen[:, :], t["wkgenT"]), (bkgen[:, :], t["bkgen"].partition_broadcast(P)),
                    (wconv[:, :], t["wconv"]), (bconv[:, :], t["bconv"].rearrange("(p a) -> p a", a=1)),
                ):
                    sp.dma_start(dst, src).then_inc(gate_weights_in, 16)
                for dst, src in (
                    (wk2[:, :, 0, :], t["wkT"].rearrange("c (g d) -> c g d", g=A_KV)),
                    (wk2[:, :, 1, :], t["wkT"].rearrange("c (g d) -> c g d", g=A_KV)),
                    (wq[:, :], t["wqT"]), (wv[:, :], t["wvT"]),
                    (wo[:, :, :], t["woT"].rearrange("(m p) n -> p m n", p=P)),
                ):
                    sp.dma_start(dst, src).then_inc(a_weights_in, 16)
                load(xn[1], 1, xn_in[1])
                load(xr[0], 0, xr_in[0])
                load(xr[1], 1, xr_in[1])
                for dst, src in (
                    (rotary[:, :, :, :], t["rotary"].rearrange("(t p) a d -> p t a d", p=P)), (mask32, t["mask"]),
                    *[pair for l in range(LAYERS) for pair in layer_weights(l)],
                ):
                    sp.dma_start(dst, src).then_inc(weights_in, 16)

            def body(i, turn):
                for p in range(PAIR):
                    b = PAIR * i + p
                    if turn in ("first", "middle"):
                        wait(sp, made["xT"], b + 1)
                        load(xn[p], b + 2, xn_in[p])
                    if turn in ("middle", "last"):
                        wait(sp, read["out"], TILES * (b - 1))
                        load(xr[p], b, xr_in[p])
                    for tile in range(TILES):
                        at = TILES * p + tile - 3
                        j = A_SLOTS * i + at
                        if (turn == "first" and at < 0) or (turn == "drain" and at >= 0):
                            continue
                        wait(sp, xo_set, j + 1)
                        r = at % 2
                        jb, jt = (at // TILES), at % TILES
                        sp.dma_start(x1[:, bass.ds(PAIR * i + jb, 1), jt, :], xo[r][:, :]).then_inc(xo_out[r], 16)

            stage_a(sp, body, pre)
            for r in range(2):
                sp.wait_ge(xo_out[r], 16 * BATCH * TILES // 2)

            HALF = DIM // 2

            def load_shifted(dst, b, done, src):
                x = src[:, bass.ds(b, 1), :, :]
                sp.dma_start(dst[:, :, 0:HALF], x[:, :, :, 0:HALF]).then_inc(done, 16)
                sp.dma_start(dst[1:P, 0, HALF:DIM], x[0:P - 1, :, 0, HALF:DIM]).then_inc(done, 16)
                sp.dma_start(dst[0:1, 1, HALF:DIM], x[P - 1:P, :, 0, HALF:DIM]).then_inc(done, 16)
                sp.dma_start(dst[1:P, 1, HALF:DIM], x[0:P - 1, :, 1, HALF:DIM]).then_inc(done, 16)

            def layer_program(layer):
                src, mid, dst = (x1, x2, x3) if layer == 0 else (x3, x4, x_out)
                last_layer = layer == LAYERS - 1

                def pre():
                    for p in range(PAIR):
                        load_shifted(hn[p], p, hn_in[p], src)

                def body(i, it, turn):
                    for p in range(PAIR):
                        b, bb = PAIR * i + p, PAIR * it + p
                        if prepares(turn, p, 2):
                            wait(sp, f_made["hT"], bb + 1)
                            load_shifted(hn[p], b + 2, hn_in[p], src)
                        if f_exists(turn, F_BATCH * p, 2 * F_BATCH):
                            for tile in range(TILES):
                                at = TILES * (p - 2) + tile
                                wait(sp, f_read["out"], F_SLOTS * it + at + 1)
                                sp.dma_start(mid[:, bass.ds(b - 2, 1), tile, :], xo[tile][:, :]).then_inc(f_out[tile], 16)
                        if prepares(turn, p, 0):
                            wait(sp, f_read["out"], TILES * (bb - 1))
                            load(res[p], b, res_in[p], src)
                        if f_exists(turn, F_BATCH * p, 2 * F_BATCH):
                            for tile in range(TILES):
                                sp.wait_ge(f_out[tile], 16 * (bb - 1))
                            load_shifted(mn[p], b - 2, mn_in[p], mid)
                        if f_exists(turn, F_BATCH * p, 4 * F_BATCH):
                            if last_layer:
                                wait(sp, z_set, b - 3)
                            else:
                                wait(sp, f_read["down"], bb - 3)
                            sp.dma_start(dst[:, bass.ds(b - 4, 1), :, :], (zo if last_layer else yo)[p][:, :, :]).then_inc(m_out[p], 16)
                        if f_exists(turn, F_BATCH * p, 2 * F_BATCH):
                            wait(sp, f_read["down"], bb - 3)
                            load(m_res[p], b - 2, m_res_in[p], mid)
                            if last_layer:
                                load(res1[p], b - 2, res1_in[p], x1)

                over_turns(sp, layer, body, pre)
                for p in range(PAIR):
                    sp.wait_ge(m_out[p], 16 * (layer + 1) * TURNS)

            for layer in range(LAYERS):
                layer_program(layer)

        @block.gpsimd
        def _(pool):
            pool.memset(ones[:, :], 1.0).then_inc(consts_set, 1)
            pool.memset(halves[:, :], -0.5).then_inc(consts_set, 1)
            pool.memset(eps[:, :], LN_EPS).then_inc(consts_set, 1)
            pool.memset(xT[:, 0:1], 0.0).then_inc(consts_set, 1)
            pool.memset(xT[:, SEQ + 1:SEQ + 2], 0.0).then_inc(consts_set, 1)
            for p in range(PAIR):
                pool.memset(hn[p][0:1, 0, DIM // 2:DIM], 0.0).then_inc(f_consts, 1)
                pool.memset(mn[p][0:1, 0, DIM // 2:DIM], 0.0).then_inc(f_consts, 1)
            pool.memset(eT_back[0:WINDOW, :, :], 0.0).then_inc(f_consts, 1)
            pool.wait_ge(consts_set, N_CONSTS)
            pool.wait_ge(weights_in, 16 * N_WEIGHTS)
            for l in range(LAYERS):
                for tile in range(TILES):
                    nc.gpsimd.tensor_tensor(out=table[l][:, tile, :, :], in0=rotary[:, tile, :, :], in1=qk_scale[l][:, :, :],
                                            op=ALU.mult).then_inc(tables_set, 1)

            def body(i, turn):
                for s, slot, p, tile, g in steps(i, turn):
                    if exists(turn, s, NORM_LAG):
                        at, ng = divmod(s - NORM_LAG, A_KV)
                        r = at % 2
                        wait(pool, coef_step, COEF_STEPS * (A_SLOTS * i + at + 1))
                        e = E[(s - NORM_LAG) % E_RING]
                        nc.gpsimd.tensor_tensor(
                            out=e[:, :, :, :], in0=e[:, :, :, :],
                            in1=coef[r][:, 2, A_REP * ng:A_REP * (ng + 1), :].unsqueeze(3).broadcast_to([P, A_REP, CHUNKS, CHUNK]),
                            op=ALU.mult).then_inc(normed, 1)
                    if g == (OUT_LAG + 1) % A_KV and exists(turn, s, OUT_LAG + 1):
                        at = (s - OUT_LAG - 1) // A_KV
                        j = A_SLOTS * i + at
                        r = at % 2
                        wait(pool, y_step, 2 * j + 2)
                        nc.gpsimd.tensor_tensor(out=rstd[r][:, 0:1], in0=mv[r][:, 1:2], in1=eps[:, 0:1], op=ALU.add).then_inc(eps_added, 1)
                        wait(pool, eps_added, j + 1)
                        wait(pool, xo_set, j - 1)
                        nc.gpsimd.tensor_tensor(out=rstd[r][:, 1:2], in0=rstd[r][:, 0:1], in1=halves[:, 0:1],
                                                op=ALU.pow).then_inc(rstd_set, 1)

            stage_a(pool, body)

            def layer_program(layer):
                last_layer = layer == LAYERS - 1

                def sums(it, local, m):
                    index = F_BANKS.stride["qk"] * it + local
                    pool.wait_ge(rotated, index + 1)
                    wait(pool, f_made["qkT"], index - 3)
                    nc.gpsimd.tensor_tensor(out=qk[m][:, :, :], in0=on_self[m % 2][:, :, :], in1=on_partner[m % 2][:, :, :],
                                            op=ALU.add).then_inc(added, 1)

                def inverse_norms(bb, tile):
                    pool.wait_ge(guarded, TILES * bb + tile + 1)
                    wait(pool, qk_normed, 4 * (bb - 1) + 2 * tile + 2)
                    at = slice(2 * F_HEADS * tile, 2 * F_HEADS * (tile + 1))
                    nc.gpsimd.tensor_tensor(out=rnorm[:, at], in0=norm2[:, 1, at], in1=halves[:, 0:2 * F_HEADS],
                                            op=ALU.pow).then_inc(rnorm_set, 1)
                    pool.wait_ge(rnorm_set, TILES * bb + tile + 1)

                def normalise(bb, m):
                    wait(pool, added, 4 * bb + m + 1)
                    nc.gpsimd.tensor_tensor(
                        out=qk[m][:, :, :], in0=qk[m][:, :, :],
                        in1=rnorm[:, F_HEADS * m:F_HEADS * (m + 1)].unsqueeze(2).broadcast_to([P, F_HEADS, F_HD]),
                        op=ALU.mult).then_inc(qk_normed, 1)

                def normalise_tile(bb, tile):
                    for m in (2 * tile, 2 * tile + 1):
                        normalise(bb, m)

                def prepare(bb, it, m, ahead_local):
                    sums(it, ahead_local + m, m)
                    if m % 2 == 1:
                        inverse_norms(bb, m // 2)

                def pre():
                    for m in range(4):
                        prepare(PAIR * TURNS * layer, TURNS * layer, m, 0)
                        if m == 1:
                            normalise_tile(PAIR * TURNS * layer, 0)

                def rstd_of(mv2, out, step, done, stats, count):
                    pool.wait_ge(stats, TILES * (count + 1))
                    nc.gpsimd.tensor_tensor(out=out[:, 0, :], in0=mv2[:, :, 1], in1=eps[:, 0:TILES], op=ALU.add).then_inc(step, 1)
                    pool.wait_ge(step, count + 1)
                    nc.gpsimd.tensor_tensor(out=out[:, 1, :], in0=out[:, 0, :], in1=halves[:, 0:TILES], op=ALU.pow).then_inc(done, 1)

                def residual(i, it, local):
                    p, b, bb, turn_of = local % PAIR, PAIR * i + local, PAIR * it + local, local // PAIR
                    pool.wait_ge(m_res_in[p], 16 * (it + turn_of + 1))
                    wait(pool, f_read["down"], bb - 1)
                    nc.gpsimd.tensor_tensor(out=resb[p][:, 0, :, :], in0=m_res[p][:, :, :],
                                            in1=b2[layer][:, :].unsqueeze(1).broadcast_to([P, TILES, DIM]),
                                            op=ALU.add).then_inc(resb_step, 1)
                    if last_layer:
                        pool.wait_ge(res1_in[p], 16 * (i + turn_of + 1))
                        wait(pool, resb_step, BATCH * layer + 2 * b + 1)
                        nc.gpsimd.tensor_tensor(out=resb[p][:, 1, :, :], in0=resb[p][:, 0, :, :], in1=res1[p][:, :, :],
                                                op=ALU.add).then_inc(resb_step, 1)

                def body(i, it, turn):
                    for s, slot, p, tile, g in f_steps(turn):
                        if f_exists(turn, s, F_NORM_LAG):
                            n = F_STEPS * it + s - F_NORM_LAG
                            n_keys, _ = keys((s - F_NORM_LAG) // F_GROUPS % TILES)
                            e = fE[(s - F_NORM_LAG) % F_RING][:, :, :, 0:n_keys]
                            pool.wait_ge(f_rsum_set, n + 1)
                            nc.gpsimd.tensor_tensor(out=e, in0=e,
                                                    in1=f_rsum[(s - F_NORM_LAG) % 2][:, :, :].unsqueeze(3).broadcast_to([P, 2, 2, n_keys]),
                                                    op=ALU.mult).then_inc(f_normed, 1)
                        if tile == 0 and g == 0 and prepares(turn, p, 0):
                            normalise_tile(PAIR * it + p, 1)
                        if tile == 1 and g == 0 and prepares(turn, p):
                            normalise_tile(PAIR * it + p + 1, 0)
                        if prepares(turn, p):
                            prepare(PAIR * it + p + 1, it, F_GROUPS * tile + g, 4 * (p + 1))
                        local = f_late(turn, s, "residual")
                        if local is not None:
                            residual(i, it, local)
                        local = f_late(turn, s, "stats")
                        if local is not None:
                            rstd_of(mmv[local % PAIR], mrstd[local % PAIR], m_eps, m_rstd, m_stats, PAIR * it + local)
                        local = f_late(turn, s, "down")
                        if local is not None and last_layer:
                            rstd_of(zmv[local % PAIR], zrstd[local % PAIR], z_eps, z_rstd, z_stats, PAIR * i + local)

                over_turns(pool, layer, body, pre)

            for layer in range(LAYERS):
                layer_program(layer)

        @block.scalar
        def _(act):
            def x_transposed(i, local, turn, b):
                act.wait_ge(made["xT"], b + 1)
                wait(act, hT_set, b)
                wait(act, wk_ctx_set, b)
                nc.scalar.activation(xT[:, 1:SEQ + 1], banks[6 + A_BANKS.bank("xT", local, turn)][:, 0:SEQ], ACT.Copy,
                                     accum_out=ctx_sum[:, :]).then_inc(read["xT"], 1)

            def gate_exponential(b):
                act.wait_ge(read["gate"], b + 1)
                nc.scalar.activation(gate[:, 1, :], gate[:, 0, :], ACT.Exp, scale=-1.0).then_inc(gate_exp, 1)

            def projected(kind, i, local, turn, m, pb):
                index = A_BANKS.stride[kind] * i + local
                act.wait_ge(made[kind], index + 1)
                bank = banks[6 + A_BANKS.bank(kind, local, turn)]
                if kind == "q":
                    nc.scalar.activation(qT[pb][:, 2 * m:2 * m + 2, :], bank[:, :], ACT.Copy, scale=A_HD ** -0.5).then_inc(read[kind], 1)
                elif kind == "k":
                    nc.scalar.activation(kT[pb][:, 2 * m:2 * m + 2, :], bank[:, :], ACT.Copy).then_inc(read[kind], 1)
                else:
                    nc.scalar.activation(v[pb][:, :, :], bank[:, :], ACT.Copy).then_inc(read[kind], 1)

            def pre():
                act.wait_ge(consts_set, N_CONSTS)
                x_transposed(0, 0, "pre", 0)
                gate_exponential(0)
                for kind, local in A_BANKS.pre[2:]:
                    projected(kind, 0, local, "pre", local, 0)

            def body(i, turn):
                for s, slot, p, tile, g in steps(i, turn):
                    if exists(turn, s, PV_LAG):
                        n = A_STEPS * i + s - PV_LAG
                        for hp in range(2):
                            act.wait_ge(wT_made, 2 * n + hp + 1)
                            wait(act, pv_done, 2 * (n - 1) + hp + 1)
                            nc.scalar.activation(wT[hp][:, :, :, :], banks[4 + hp][:, :], ACT.Copy).then_inc(wT_read, 1)
                    if exists(turn, s, EXP_LAG):
                        n = A_STEPS * i + s - EXP_LAG
                        act.wait_ge(sub_done, n + 1)
                        e = E[(s - EXP_LAG) % E_RING]
                        nc.scalar.activation(e[:, :, :, :], e[:, :, :, :], ACT.Exp).then_inc(exp_done, 1)
                    if prepares(turn, p) and tile == 0:
                        if g == 0:
                            x_transposed(i, p + 1, turn, PAIR * i + p + 1)
                        if g == 3:
                            gate_exponential(PAIR * i + p + 1)
                    if prepares(turn, p) and tile == 1:
                        for kind, per, m in A_PROJECTIONS[g]:
                            projected(kind, i, per * (p + 1) + m, turn, m, (p + 1) % 2)
                    if exists(turn, s, PV_LAG):
                        n = A_STEPS * i + s - PV_LAG
                        at, og = divmod(s - PV_LAG, A_KV)
                        act.wait_ge(pv_done, 2 * n + 2)
                        wait(act, made["out"], A_SLOTS * i + at - 1)
                        nc.scalar.activation(oT[at % 2][:, 2 * og:2 * og + 2, :],
                                             banks[6 + A_BANKS.bank("o", s - PV_LAG, "middle")][:, 0:2 * P], ACT.Copy).then_inc(read["o"], 1)

            stage_a(act, body, pre)

            def layer_program(layer):
                def prepare(it, kind, local, m, batch, turn):
                    act.wait_ge(f_made[kind], F_BANKS.stride[kind] * it + local + 1)
                    bank = banks[6 + F_BANKS.bank(kind, local, turn)]
                    par = (local // (F_BANKS.stride[kind] // PAIR)) % PAIR
                    if kind == "hT":
                        nc.scalar.activation(fhT[:, :], bank[:, 0:SEQ], ACT.Copy).then_inc(f_read[kind], 1)
                    elif kind == "qk":
                        wait(act, norm_step, 4 * batch + m - 1)
                        nc.scalar.activation(raw[m % 2][:, :, :], bank[:, :].rearrange("p (h d) -> p h d", h=F_HEADS), ACT.Copy).then_inc(f_read[kind], 1)
                        act.wait_ge(f_read[kind], F_BANKS.stride[kind] * it + local + 1)
                        nc.scalar.activation(sq[m % 2][:, :], raw[m % 2][:, :, :].rearrange("p h d -> p (h d)"), ACT.Square).then_inc(squared, 1)
                    elif kind == "v":
                        wait(act, f_o_made, 4 * (batch - 1))
                        nc.scalar.activation(f_v[par][:, m, :, :], bank[:, :].rearrange("p (h d) -> p h d", h=F_HEADS),
                                             ACT.Copy).then_inc(f_read[kind], 1)
                    else:
                        tile, half = divmod(m, 2)
                        nc.scalar.activation(qkT[par][:, 4 * half:4 * half + 4, P * tile:P * (tile + 1)],
                                             bank[:, :].rearrange("p (m q) -> p m q", m=4), ACT.Copy).then_inc(f_read[kind], 1)

                def pre():
                    if layer == 0:
                        act.wait_ge(f_consts, N_F_CONSTS)
                    for kind, local in F_BANKS.pre:
                        per = F_BANKS.stride[kind] // PAIR
                        prepare(TURNS * layer, kind, local, local % per, PAIR * TURNS * layer + local // per, "pre")

                def body(i, it, turn):
                    for s, slot, p, tile, g in f_steps(turn):
                        n = F_STEPS * it + s
                        if f_exists(turn, s, F_PV_LAG):
                            act.wait_ge(eT_made, n - F_PV_LAG + 1)
                            wait(act, f_o_made, n - F_PV_LAG)
                            nc.scalar.activation(eT[:, :, :], banks[4][:, :], ACT.Copy).then_inc(eT_read, 1)
                            if (s - F_PV_LAG) // F_GROUPS % TILES == 1:
                                nc.scalar.activation(eT_back[WINDOW:P, :, :], banks[5][0:WINDOW, :], ACT.Copy).then_inc(back_read, 1)
                        if f_exists(turn, s, F_EXP_LAG):
                            n_keys, _ = keys((s - F_EXP_LAG) // F_GROUPS % TILES)
                            e = fE[(s - F_EXP_LAG) % F_RING]
                            act.wait_ge(f_sub, n - F_EXP_LAG + 1)
                            nc.scalar.activation(e[:, :, :, 0:n_keys], e[:, :, :, 0:n_keys], ACT.Exp).then_inc(f_exp, 1)

                        if f_exists(turn, s, F_PV_LAG):
                            at, og = divmod(s - F_PV_LAG, F_GROUPS)
                            act.wait_ge(f_o_made, n - F_PV_LAG + 1)
                            wait(act, f_made["out"], F_SLOTS * it + at - 1)
                            nc.scalar.activation(foT[at % 2][:, 2 * og:2 * og + 2, :], banks[5][:, 0:2 * P], ACT.Copy).then_inc(f_o_read, 1)
                        for kind, local, m, ahead in f_fills(turn, s):
                            if kind == "mix":
                                par, bb = local % PAIR, PAIR * it + local
                                wait(act, u_done, F_CHUNKS * bb)
                                for c, rows in enumerate(F_ROWS):
                                    name, col = ("gates", SEQ * c) if c < F_CHUNKS - 1 else ("mix", SEQ)
                                    act.wait_ge(f_made[name], bb + 1)
                                    nc.scalar.activation(ge[c][0:rows, :], banks[6 + F_BANKS.bank(name, local, "middle")][0:rows, col:col + SEQ],
                                                         ACT.Gelu, bias=b1[layer][0:rows, 1, c:c + 1]).then_inc(gelu_done, 1)
                            elif kind in ("hT", "qk", "v", "qkT"):
                                prepare(it, kind, local, m, PAIR * it + p + ahead, turn)

                over_turns(act, layer, body, pre)

            for layer in range(LAYERS):
                layer_program(layer)

        @block.vector
        def _(dve):
            def gate_weights(b):
                dve.wait_ge(read["xT"], b + 1)
                wait(dve, made["gate"], b)
                nc.vector.tensor_scalar(wk_ctx[:, :], wkgen[:, :], ctx_sum[:, 0:1], None, ALU.mult).then_inc(wk_ctx_set, 1)

            def gate_logit(b, local, turn):
                dve.wait_ge(made["gate"], b + 1)
                wait(dve, gate_step, GATE_STEPS * b)
                wait(dve, gate_exp, b)
                nc.vector.scalar_tensor_tensor(gate[:, 0, :], banks[6 + A_BANKS.bank("gate", local, turn)][:, 0:KS], 1.0 / SEQ,
                                               bkgen[:, :], ALU.mult, ALU.add).then_inc(read["gate"], 1)

            def convolution(b):
                nc.vector.tensor_scalar(conv[:, 0, :], xT[:, 1:SEQ + 1], wconv[:, 1:2], bconv[:, 0:1],
                                        ALU.mult, ALU.add).then_inc(conv_step, 1)
                dve.wait_ge(conv_step, 3 * b + 1)
                nc.vector.scalar_tensor_tensor(conv[:, 1, :], xT[:, 0:SEQ], wconv[:, 0:1], conv[:, 0, :],
                                               ALU.mult, ALU.add).then_inc(conv_step, 1)
                dve.wait_ge(conv_step, 3 * b + 2)
                nc.vector.scalar_tensor_tensor(conv[:, 2, :], xT[:, 2:SEQ + 2], wconv[:, 2:3], conv[:, 1, :],
                                               ALU.mult, ALU.add).then_inc(conv_step, 1)

            def gated(b):
                dve.wait_ge(gate_exp, b + 1)
                nc.vector.tensor_scalar_add(gate[:, 2, :], gate[:, 1, :], 1.0).then_inc(gate_step, 1)
                dve.wait_ge(gate_step, GATE_STEPS * b + 1)
                nc.vector.reciprocal(gate[:, 3, :], gate[:, 2, :]).then_inc(gate_step, 1)
                dve.wait_ge(gate_step, GATE_STEPS * b + 2)
                nc.vector.tensor_reduce(gate_sum[:, :], gate[:, 3, :], AX.X, ALU.add).then_inc(gate_step, 1)
                dve.wait_ge(gate_step, GATE_STEPS * b + 3)
                dve.wait_ge(conv_step, 3 * b + 3)
                wait(dve, made["v"], b)
                nc.vector.tensor_scalar(hT[:, :], conv[:, 2, :], gate_sum[:, 0:1], 1.0 / KS,
                                        ALU.mult, ALU.mult).then_inc(hT_set, 1)

            def pre():
                dve.wait_ge(gate_weights_in, 16 * N_GATE_WEIGHTS)
                dve.wait_ge(consts_set, N_CONSTS)
                gate_weights(0)
                gate_logit(0, 0, "pre")
                convolution(0)
                gated(0)

            def factors(j, r):
                c, tt = coef[r], total[r]
                k = COEF_STEPS * j

                def link(ins, at):
                    ins.then_inc(coef_step, 1)
                    if at < COEF_STEPS:
                        dve.wait_ge(coef_step, k + at)
                dve.wait_ge(sum_done, A_KV * (j + 1))
                wait(dve, normed, A_KV * (j - 1))
                link(nc.vector.reciprocal(c[:, 0, :, :], sums[r][:, :, :]), 1)
                link(nc.vector.tensor_tensor(c[:, 1, :, :], sums[r][:, :, :], c[:, 0, :, :], ALU.mult), 2)
                link(nc.vector.tensor_reduce(tt[:, 0, :], c[:, 1, :, :], AX.X, ALU.add), 3)
                link(nc.vector.tensor_scalar_add(tt[:, 1, :], tt[:, 0, :], 1e-9), 4)
                link(nc.vector.reciprocal(tt[:, 2, :], tt[:, 1, :]), 5)
                link(nc.vector.tensor_tensor(c[:, 1, :, :], c[:, 1, :, :],
                                             tt[:, 2, :].unsqueeze(2).broadcast_to([P, A_HEADS, CHUNKS]), ALU.mult), 6)
                link(nc.vector.tensor_tensor(c[:, 2, :, :], c[:, 0, :, :], c[:, 1, :, :], ALU.mult), 7)

            def summed(i, turn, s):
                if exists(turn, s, SUM_LAG):
                    n = A_STEPS * i + s - SUM_LAG
                    at, gg = divmod(s - SUM_LAG, A_KV)
                    dve.wait_ge(exp_done, n + 1)
                    nc.vector.tensor_reduce(sums[at % 2][:, A_REP * gg:A_REP * (gg + 1), :], E[(s - SUM_LAG) % E_RING][:, :, :, :],
                                            AX.X, ALU.add).then_inc(sum_done, 1)
                    if gg == A_KV - 1:
                        factors(A_SLOTS * i + at, at % 2)

            def body(i, turn):
                for s, slot, p, tile, g in steps(i, turn):
                    if tile == 0 and g == 1 and prepares(turn, p):
                        gate_weights(PAIR * i + p + 1)
                    if tile == 1 and g == 0 and prepares(turn, p):
                        gated(PAIR * i + p + 1)
                    if g == 1:
                        summed(i, turn, s)
                    if exists(turn, s):
                        n = A_STEPS * i + s
                        e, m = E[s % E_RING], mx[s % 2]
                        both = [banks[2 * (s % 2) + k] for k in range(2)]
                        dve.wait_ge(scored, n + 1)
                        for k in range(2):
                            ins = nc.vector.tensor_reduce(m[:, 2 * k:2 * k + 2, :], both[k][:, :].rearrange("p (h c k) -> p h c k", h=2, c=CHUNKS),
                                                          AX.X, ALU.max)
                            ins.then_inc(max_set, 1)
                        wait(dve, wT_made, 2 * (n - E_RING) + 2)
                        for k in range(2):
                            dve.wait_ge(max_set, 2 * n + k + 1)
                            ins = nc.vector.tensor_tensor(
                                e[:, 2 * k:2 * k + 2, :, :], both[k][:, :].rearrange("p (h c k) -> p h c k", h=2, c=CHUNKS),
                                m[:, 2 * k:2 * k + 2, :].unsqueeze(3).broadcast_to([P, 2, CHUNKS, CHUNK]), ALU.subtract)
                        ins.then_inc(sub_done, 1)
                    if tile == 0 and g == 2 and prepares(turn, p):
                        gate_logit(PAIR * i + p + 1, p + 1, turn)
                    if g != 1:
                        summed(i, turn, s)
                    if prepares(turn, p):
                        b = PAIR * i + p + 1
                        if tile == 0 and g == 2:
                            convolution(b)
                    if g == OUT_LAG % A_KV and exists(turn, s, OUT_LAG):
                        at = (s - OUT_LAG) // A_KV
                        j, r = A_SLOTS * i + at, at % 2
                        dve.wait_ge(made["out"], j + 1)
                        dve.wait_ge(xr_in[(at // TILES) % 2], 16 * (i + at // TILES // PAIR + 1))
                        nc.vector.tensor_tensor(y[r][:, :], banks[6 + A_BANKS.bank("out", at, "middle")][:, 0:DIM],
                                                xr[(at // TILES) % 2][:, at % TILES, :], ALU.add).then_inc(read["out"], 1)
                        dve.wait_ge(read["out"], j + 1)
                        nc.vector.bn_stats(stat[r][:, :], y[r][:, :]).then_inc(y_step, 1)
                        dve.wait_ge(y_step, 2 * j + 1)
                        dve.sem_inc(stats_waited, 1)
                        nc.vector.bn_aggr(mv[r][:, :], stat[r][:, :]).then_inc(y_step, 1)
                    if g == LN_LAG % A_KV and exists(turn, s, LN_LAG):
                        at = (s - LN_LAG) // A_KV
                        j, r = A_SLOTS * i + at, at % 2
                        dve.wait_ge(rstd_set, j + 1)
                        wait(dve, xo_out[r], 16 * (2 * i + at // 2))
                        nc.vector.tensor_scalar(xo[r][:, :], y[r][:, :], mv[r][:, 0:1], rstd[r][:, 1:2],
                                                ALU.subtract, ALU.mult).then_inc(xo_set, 1)

            stage_a(dve, body, pre)

            dve.wait_ge(tables_set, LAYERS * TILES)
            nc.vector.tensor_copy(mask[:, :], mask32).then_inc(f_consts, 1)
            nc.vector.tensor_copy(ident16[:, :], ident[:, :]).then_inc(f_consts, 1)

            def layer_program(layer):
                last_layer = layer == LAYERS - 1
                HALF = F_HD // 2

                def rotate(it, local, m, turn):
                    index = F_BANKS.stride["qk"] * it + local
                    tile, kind = divmod(m, 2)
                    x = raw[m % 2]

                    def tab(k, lo, hi):
                        return table[layer][:, tile, 2 * kind + k, lo:hi].unsqueeze(1).broadcast_to([P, F_HEADS, hi - lo])

                    dve.wait_ge(f_read["qk"], index + 1)
                    wait(dve, added, index - 1)
                    nc.vector.tensor_tensor(on_self[m % 2][:, :, :], x[:, :, :], tab(0, 0, F_HD), ALU.mult)
                    nc.vector.tensor_tensor(on_partner[m % 2][:, :, 0:HALF], x[:, :, HALF:F_HD], tab(1, 0, HALF), ALU.mult)
                    nc.vector.tensor_tensor(on_partner[m % 2][:, :, HALF:F_HD], x[:, :, 0:HALF], tab(1, HALF, F_HD),
                                            ALU.mult).then_inc(rotated, 1)
                    dve.wait_ge(squared, index + 1)
                    nc.vector.tensor_reduce(norm2[:, 0, F_HEADS * m:F_HEADS * (m + 1)],
                                            sq[m % 2][:, :].rearrange("p (h d) -> p h d", h=F_HEADS), AX.X, ALU.add).then_inc(norm_step, 1)
                    if m % 2 == 1:
                        dve.wait_ge(norm_step, index + 1)
                        wait(dve, rnorm_set, TILES * (PAIR * it + local // 4 - 1) + tile + 1)
                        at = slice(F_HEADS * (m - 1), F_HEADS * (m + 1))
                        nc.vector.tensor_scalar_max(norm2[:, 1, at], norm2[:, 0, at], 1e-24).then_inc(guarded, 1)

                def stats(x, st, out, bn, done, count):
                    for tile in range(TILES):
                        nc.vector.bn_stats(st[:, tile, :], x[:, tile, :]).then_inc(bn, 1)
                    dve.wait_ge(bn, TILES * (count + 1))
                    dve.sem_inc(stats_waited, 1)
                    for tile in range(TILES):
                        nc.vector.bn_aggr(out[:, tile, :], st[:, tile, :]).then_inc(done, 1)

                def normalised(par, bb):
                    dve.wait_ge(m_rstd, bb + 1)
                    for tile in range(TILES):
                        ins = nc.vector.tensor_scalar(hc[par][:, tile, :], mn[par][:, tile, :], mmv[par][:, tile, 0:1],
                                                      mrstd[par][:, 1, tile:tile + 1], ALU.subtract, ALU.mult)
                    ins.then_inc(hc_set, 1)

                def gated_product(c, bank, col, par, bb):
                    rows = F_ROWS[c]
                    dve.wait_ge(gelu_done, F_CHUNKS * bb + c + 1)
                    ins = nc.vector.scalar_tensor_tensor(uT[par][0:rows, c, :], bank[0:rows, col:col + SEQ],
                                                         b1[layer][0:rows, 0, c:c + 1], ge[c][0:rows, :], ALU.add, ALU.mult)
                    return ins.then_inc(u_done, 1)

                def mlp_fill(kind, i, it, local):
                    par, b, bb, turn_of = local % PAIR, PAIR * i + local, PAIR * it + local, local // PAIR
                    bank = banks[6 + F_BANKS.bank(kind, local, "middle")]
                    dve.wait_ge(f_made[kind], bb + 1)
                    if kind == "mT":
                        nc.vector.tensor_scalar(hT2[par][:, :], bank[:, 0:SEQ], ln_g[layer][:, 0:1], ln_b[layer][:, 0:1],
                                                ALU.mult, ALU.add).then_inc(f_read["mT"], 1)
                    if kind == "mix":
                        gated_product(F_CHUNKS - 1, bank, 0, par, bb)
                    if kind == "values":
                        for c in range(F_CHUNKS - 1):
                            gated_product(c, bank, SEQ * c, par, bb)
                    if kind == "down":
                        dve.wait_ge(resb_step, BATCH * layer + 2 * b + 2 if last_layer else bb + 1)
                        if not last_layer:
                            wait(dve, m_out[par], 16 * (it + turn_of))
                        nc.vector.tensor_tensor(yo[par][:, :, :], bank[:, 0:TILES * DIM].rearrange("p (t d) -> p t d", t=TILES),
                                                resb[par][:, 1 if last_layer else 0, :, :], ALU.add).then_inc(f_read["down"], 1)
                        if last_layer:
                            dve.wait_ge(f_read["down"], bb + 1)
                            stats(yo[par], zstat[par], zmv[par], z_bn, z_stats, b)

                def shared_fill(kind, local, m, i, it, turn):
                    if kind == "qk":
                        rotate(it, local, m, turn)
                    if kind == "out":
                        at = local
                        j, r = F_SLOTS * it + at, at % 2
                        dve.wait_ge(f_made["out"], j + 1)
                        dve.wait_ge(res_in[(at // TILES) % PAIR], 16 * (it + at // TILES // PAIR + 1))
                        wait(dve, f_out[r], 16 * (2 * it + at // 2))
                        nc.vector.tensor_tensor(xo[r][:, :], banks[6 + F_BANKS.bank("out", at, "middle")][:, 0:DIM],
                                                res[(at // TILES) % PAIR][:, at % TILES, :], ALU.add).then_inc(f_read["out"], 1)
                    if kind in ("mT", "mix", "values", "down"):
                        mlp_fill(kind, i, it, local)

                def sums_of_exponentials(s, n, turn):
                    if f_exists(turn, s, F_SUM_LAG):
                        nn, r = n - F_SUM_LAG, (s - F_SUM_LAG) % 2
                        n_keys, _ = keys((s - F_SUM_LAG) // F_GROUPS % TILES)
                        dve.wait_ge(f_exp, nn + 1)
                        nc.vector.tensor_reduce(f_sum[r][:, :, :], fE[(s - F_SUM_LAG) % F_RING][:, :, :, 0:n_keys], AX.X, ALU.add).then_inc(f_sum_set, 1)
                        dve.wait_ge(f_sum_set, nn + 1)
                        wait(dve, f_normed, nn - 1)
                        nc.vector.reciprocal(f_rsum[r][:, :, :], f_sum[r][:, :, :]).then_inc(f_rsum_set, 1)

                def pre():
                    for m in range(4):
                        rotate(TURNS * layer, m, m, "pre")

                def body(i, it, turn):
                    for s, slot, p, tile, g in f_steps(turn):
                        n = F_STEPS * it + s
                        if f_exists(turn, s):
                            n_keys, _ = keys(tile)
                            e, m = fE[s % F_RING], fmx[s % 2]
                            both = [banks[2 * (s % 2) + k][:, 0:2 * n_keys].rearrange("p (a k) -> p a k", a=2) for k in range(2)]
                            dve.wait_ge(f_scored, n + 1)
                            for k in range(2):
                                nc.vector.tensor_reduce(m[:, k, :], both[k], AX.X, ALU.max).then_inc(f_max, 1)
                            wait(dve, eT_made, n - F_RING + 1)
                            for k in range(2):
                                dve.wait_ge(f_max, 2 * n + k + 1)
                                ins = nc.vector.tensor_tensor(e[:, k, :, 0:n_keys], both[k],
                                                              m[:, k, :].unsqueeze(2).broadcast_to([P, 2, n_keys]), ALU.subtract)
                            ins.then_inc(f_sub, 1)
                        awaited = ("out", "down")
                        for summing in (False, True):
                            if summing:
                                sums_of_exponentials(s, n, turn)
                            for kind, local, m, ahead in f_fills(turn, s):
                                if summing != (kind in awaited):
                                    shared_fill(kind, local, m, i, it, turn)
                        local = f_late(turn, s, "stats")
                        if local is not None:
                            par = local % PAIR
                            dve.wait_ge(mn_in[par], 64 * (it + local // PAIR + 1))
                            stats(mn[par], mstat[par], mmv[par], m_bn, m_stats, PAIR * it + local)
                        local = f_late(turn, s, "norm")
                        if local is not None:
                            normalised(local % PAIR, PAIR * it + local)
                        local = f_late(turn, s, "z")
                        if local is not None and last_layer:
                            par = local % PAIR
                            dve.wait_ge(z_rstd, PAIR * i + local + 1)
                            wait(dve, m_out[par], 16 * (it + local // PAIR))
                            for t2 in range(TILES):
                                ins = nc.vector.tensor_scalar(zo[par][:, t2, :], yo[par][:, t2, :], zmv[par][:, t2, 0:1],
                                                              zrstd[par][:, 1, t2:t2 + 1], ALU.subtract, ALU.mult)
                            ins.then_inc(z_set, 1)

                over_turns(dve, layer, body, pre)

            for layer in range(LAYERS):
                layer_program(layer)

        @block.tensor
        def _(pe):
            def transpose_x(i, local, turn, b):
                bank_free(pe, A_BANKS, read, "xT", local, i, turn)
                pe.wait_ge(xn_in[local % 2], 16 * (i + local // 2 + 1))
                bank = banks[6 + A_BANKS.bank("xT", local, turn)]
                for tt in range(TILES):
                    ins = nc.tensor.transpose(bank[:, P * tt:P * (tt + 1)], xn[local % 2][:, tt, :], ident[:, :])
                ins.then_inc(made["xT"], 1)

            def gate_matmul(i, local, turn, b):
                bank_free(pe, A_BANKS, read, "gate", local, i, turn)
                pe.wait_ge(wk_ctx_set, b + 1)
                nc.tensor.matmul(banks[6 + A_BANKS.bank("gate", local, turn)][:, 0:KS], ones[:, :], wk_ctx[:, :],
                                 start=True, stop=True).then_inc(made["gate"], 1)

            def project(kind, i, local, turn, m, b):
                bank_free(pe, A_BANKS, read, kind, local, i, turn)
                pe.wait_ge(hT_set, b + 1)
                bank = banks[6 + A_BANKS.bank(kind, local, turn)]
                for k in range(2):
                    dst = bank[:, 256 * k:256 * (k + 1)]
                    if kind == "q":
                        ins = nc.tensor.matmul(dst, wq[:, P * (2 * m + k):P * (2 * m + k + 1)], hT[:, :], start=True, stop=True)
                    elif kind == "k":
                        ins = nc.tensor.matmul(dst, wk2[:, 2 * m + k, :, :], hT[:, :], start=True, stop=True)
                    else:
                        ins = nc.tensor.matmul(dst, hT[:, P * k:P * (k + 1)], wv[:, :], start=True, stop=True)
                ins.then_inc(made[kind], 1)

            def pre():
                pe.wait_ge(gate_weights_in, 16 * N_GATE_WEIGHTS)
                pe.wait_ge(consts_set, N_CONSTS)
                transpose_x(0, 0, "pre", 0)
                gate_matmul(0, 0, "pre", 0)
                pe.wait_ge(a_weights_in, 16 * N_A_WEIGHTS)
                for kind, local in A_BANKS.pre[2:]:
                    project(kind, 0, local, "pre", local, 0)

            def body(i, turn):
                for s, slot, p, tile, g in steps(i, turn):
                    late = exists(turn, s, PV_LAG)
                    if late:
                        n = A_STEPS * i + s - PV_LAG
                        e = E[(s - PV_LAG) % E_RING]
                        pe.wait_ge(normed, n + 1)
                        for hp in range(2):
                            wait(pe, wT_read, 2 * (n - 1) + hp + 1)
                            for kb in range(TILES):
                                for hh in range(2):
                                    ins = nc.tensor.transpose(banks[4 + hp][:, P * (2 * kb + hh):P * (2 * kb + hh + 1)],
                                                              e[:, 2 * hh + hp, 2 * kb:2 * kb + 2, :], ident[:, :])
                            ins.then_inc(wT_made, 1)
                    if exists(turn, s):
                        n = A_STEPS * i + s
                        if g == 0:
                            b = PAIR * i + p
                            pe.wait_ge(read["q"], 4 * b + 4)
                            pe.wait_ge(read["k"], 2 * b + 2)
                        wait(pe, sub_done, n - 1)
                        for h in range(A_REP):
                            lo = A_HD * (h % 2)
                            ins = nc.tensor.matmul(
                                banks[2 * (s % 2) + h % 2][:, SEQ * (h // 2):SEQ * (h // 2 + 1)],
                                qT[p][lo:lo + A_HD, 2 * g + h // 2, P * tile:P * (tile + 1)],
                                kT[p][lo:lo + A_HD, g, :], start=True, stop=True)
                        ins.then_inc(scored, 1)
                    if prepares(turn, p):
                        b = PAIR * i + p + 1
                        if tile == 0 and g == 0:
                            transpose_x(i, p + 1, turn, b)
                        if tile == 0 and g == 2:
                            gate_matmul(i, p + 1, turn, b)
                        if tile == 1:
                            for kind, per, m in A_PROJECTIONS[g]:
                                project(kind, i, per * (p + 1) + m, turn, m, b)
                    if late:
                        n = A_STEPS * i + s - PV_LAG
                        at, og = divmod(s - PV_LAG, A_KV)
                        ap = (at // TILES) % PAIR
                        bank = banks[6 + A_BANKS.bank("o", s - PV_LAG, "middle")]
                        bank_free(pe, A_BANKS, read, "o", s - PV_LAG, i, turn)
                        if og == 0:
                            pe.wait_ge(read["v"], PAIR * i + at // TILES + 1)
                        for hp in range(2):
                            pe.wait_ge(wT_read, 2 * n + hp + 1)
                            for kb in range(TILES):
                                for hh in range(2):
                                    ins = nc.tensor.matmul(
                                        bank[A_HD * hh:A_HD * (hh + 1), P * hp:P * (hp + 1)],
                                        v[ap][:, kb, A_HD * og:A_HD * (og + 1)], wT[hp][:, kb, hh, :],
                                        start=(kb == 0), stop=(kb == TILES - 1))
                            ins.then_inc(pv_done, 1)
                    if g == OUT_LAG % A_KV and exists(turn, s, OUT_LAG):
                        at = (s - OUT_LAG) // A_KV
                        j = A_SLOTS * i + at
                        bank_free(pe, A_BANKS, read, "out", at, i, turn)
                        pe.wait_ge(read["o"], A_KV * j + A_KV)
                        for m in range(A_HEADS // 2):
                            ins = nc.tensor.matmul(banks[6 + A_BANKS.bank("out", at, "middle")][:, 0:DIM], oT[at % 2][:, m, :], wo[:, m, :],
                                                   start=(m == 0), stop=(m == A_HEADS // 2 - 1))
                        ins.then_inc(made["out"], 1)

            stage_a(pe, body, pre)

            def layer_program(layer):
                free = lambda kind, local, it, turn: bank_free(pe, F_BANKS, f_read, kind, local, it, turn)

                def prepare(it, kind, local, m, batch, turn):
                    par = (local // (F_BANKS.stride[kind] // PAIR)) % PAIR
                    bank = banks[6 + F_BANKS.bank(kind, local, turn)]
                    free(kind, local, it, turn)
                    if kind == "hT":
                        pe.wait_ge(hn_in[par], 64 * (it + local // PAIR + 1))
                        for tt in range(TILES):
                            ins = nc.tensor.transpose(bank[:, P * tt:P * (tt + 1)], hn[par][:, tt, :], ident[:, :])
                    elif kind in ("qk", "v"):
                        tile, k = divmod(m, 2) if kind == "qk" else (m, 2)
                        pe.wait_ge(f_read["hT"], batch + 1)
                        ins = nc.tensor.matmul(bank[:, :], fhT[:, P * tile:P * (tile + 1)], wqkv[layer][:, INNER * k:INNER * (k + 1)],
                                               start=True, stop=True)
                    else:
                        pe.wait_ge(qk_normed, F_BANKS.stride[kind] * it + local + 1)
                        flat = qk[m][:, :, :].rearrange("p h d -> p (h d)")
                        for block_of in range(4):
                            ins = nc.tensor.transpose(bank[:, P * block_of:P * (block_of + 1)],
                                                      flat[:, P * block_of:P * (block_of + 1)], ident[:, :])
                    ins.then_inc(f_made[kind], 1)

                def mlp_fill(kind, it, local):
                    par, bb = local % PAIR, PAIR * it + local
                    bank = banks[6 + F_BANKS.bank(kind, local, "middle")]

                    def hidden(a, c, col):
                        at, rows = F_HID * a + P * c, F_ROWS[c]
                        return nc.tensor.matmul(bank[0:rows, col:col + SEQ], w1[layer][:, at:at + rows], hT2[par][:, :], start=True, stop=True)

                    if kind == "mT":
                        pe.wait_ge(hc_set, bb + 1)
                        for tile in range(TILES):
                            ins = nc.tensor.transpose(bank[:, P * tile:P * (tile + 1)], hc[par][:, tile, :], ident[:, :])
                    if kind == "gates":
                        pe.wait_ge(f_read["mT"], bb + 1)
                        for c in range(F_CHUNKS - 1):
                            ins = hidden(1, c, SEQ * c)
                    if kind == "mix":
                        for a in range(2):
                            ins = hidden(a, F_CHUNKS - 1, SEQ * a)
                    if kind == "values":
                        for c in range(F_CHUNKS - 1):
                            ins = hidden(0, c, SEQ * c)
                    if kind == "down":
                        pe.wait_ge(u_done, F_CHUNKS * (bb + 1))
                        for tile in range(TILES):
                            for c, rows in enumerate(F_ROWS):
                                ins = nc.tensor.matmul(bank[:, DIM * tile:DIM * (tile + 1)],
                                                       uT[par][0:rows, c, P * tile:P * (tile + 1)], w2[layer][0:rows, c, :],
                                                       start=(c == 0), stop=(c == F_CHUNKS - 1))
                    ins.then_inc(f_made[kind], 1)

                def pre():
                    if layer == 0:
                        pe.wait_ge(weights_in, 16 * N_WEIGHTS)
                        pe.wait_ge(f_consts, N_F_CONSTS)
                        pe.wait_ge(read["out"], BATCH * TILES)
                    else:
                        pe.wait_ge(f_read["down"], BATCH * layer)
                    for kind, local in F_BANKS.pre:
                        per = F_BANKS.stride[kind] // PAIR
                        prepare(TURNS * layer, kind, local, local % per, PAIR * TURNS * layer + local // per, "pre")

                def body(i, it, turn):
                    for s, slot, p, tile, g in f_steps(turn):
                        n = F_STEPS * it + s
                        late = f_exists(turn, s, F_PV_LAG)
                        late_slot, late_g = divmod(s - F_PV_LAG, F_GROUPS)
                        late_p, late_tile = (late_slot // TILES) % PAIR, late_slot % TILES
                        if late:
                            pe.wait_ge(f_normed, n - F_PV_LAG + 1)
                            wait(pe, eT_read, n - F_PV_LAG)
                            e = fE[(s - F_PV_LAG) % F_RING]
                            own = keys(late_tile)[0] - P
                            if late_tile == 1:
                                wait(pe, f_o_read, n - F_PV_LAG)
                                wait(pe, back_read, F_GROUPS * (PAIR * it + late_slot // TILES) + late_g)
                            for h in range(F_GH):
                                ins = nc.tensor.transpose(banks[4][:, P * h:P * (h + 1)], e[:, h % 2, h // 2, own:own + P], ident[:, :])
                            if late_tile == 1:
                                for h in range(F_GH):
                                    ins = nc.tensor.transpose(banks[5][0:WINDOW, P * h:P * (h + 1)], e[:, h % 2, h // 2, 0:own], ident[:, :])
                            ins.then_inc(eT_made, 1)
                        if f_exists(turn, s):
                            n_keys, first_key = keys(tile)
                            if g == 0:
                                pe.wait_ge(f_read["qkT"], 4 * (PAIR * it + p) + 2 * tile + 2)
                            wait(pe, f_sub, n - 1)
                            m0 = 2 * P * tile
                            for k in range(2):
                                nc.tensor.matmul(banks[2 * (s % 2) + k][:, 0:2 * n_keys], ident16[:, :], mask[:, m0:m0 + 2 * n_keys],
                                                 start=True, stop=False)
                            for h in range(F_GH):
                                head = F_GH * g + h
                                lo = F_HD * (h % 2)
                                ins = nc.tensor.matmul(
                                    banks[2 * (s % 2) + h % 2][:, n_keys * (h // 2):n_keys * (h // 2 + 1)],
                                    qkT[p][lo:lo + F_HD, head // 2, P * tile:P * (tile + 1)],
                                    qkT[p][lo:lo + F_HD, 4 + head // 2, first_key:first_key + n_keys],
                                    start=False, stop=(h >= 2))
                            ins.then_inc(f_scored, 1)
                        if late:
                            bank = banks[5]
                            wait(pe, f_o_read, n - F_PV_LAG)
                            if late_g == 0:
                                pe.wait_ge(f_read["v"], 2 * (PAIR * it + late_slot // TILES) + late_tile + 1)
                            pe.wait_ge(eT_read, n - F_PV_LAG + 1)
                            if late_tile == 1:
                                pe.wait_ge(back_read, F_GROUPS * (PAIR * it + late_slot // TILES) + late_g + 1)
                            for pair in range(F_GH // 2):
                                for back in range(late_tile + 1):
                                    for hh in range(2):
                                        h = 2 * pair + hh
                                        ins = nc.tensor.matmul(bank[F_HD * hh:F_HD * (hh + 1), P * pair:P * (pair + 1)],
                                                               f_v[late_p][:, late_tile - back, F_GH * late_g + h, :],
                                                               (eT_back if back else eT)[:, h, :], start=(back == 0), stop=(back == late_tile))
                            ins.then_inc(f_o_made, 1)
                        for kind, local, m, ahead in f_fills(turn, s):
                            if kind in ("hT", "qk", "v", "qkT"):
                                prepare(it, kind, local, m, PAIR * it + p + ahead, turn)
                                continue
                            free(kind, local, it, turn)
                            if kind != "out":
                                mlp_fill(kind, it, local)
                                continue
                            j = F_SLOTS * it + local
                            bank = banks[6 + F_BANKS.bank(kind, local, "middle")]
                            pe.wait_ge(f_o_read, F_GROUPS * j + F_GROUPS)
                            for m in range(INNER // P):
                                ins = nc.tensor.matmul(bank[:, 0:DIM], foT[local % 2][:, m, :], wof[layer][:, m, :],
                                                       start=(m == 0), stop=(m == INNER // P - 1))
                            ins.then_inc(f_made[kind], 1)

                over_turns(pe, layer, body, pre)

            for layer in range(LAYERS):
                layer_program(layer)


def rotary_tables():
    f32 = np.float32
    half = np.arange(0, F_HD, 2, dtype=f32)
    inv_freq = f32(1.0) / np.power(f32(10000.0), half / f32(F_HD)).astype(f32)
    tok = np.arange(SEQ, dtype=f32)
    freqs = tok[:, None] * inv_freq[None, :]
    freqs = np.concatenate([freqs, freqs], axis=-1)
    base = (half + f32(0.4 * F_HD)) / f32(1.4 * F_HD)
    power = (tok - SEQ // 2) / f32(WINDOW // 2)
    scale = np.power(base[None, :].astype(np.float64), power[:, None].astype(np.float64))
    scale = np.concatenate([scale, scale], axis=-1)
    cos, sin = np.cos(freqs.astype(np.float64)), np.sin(freqs.astype(np.float64))
    sin = sin * np.where(np.arange(F_HD) < F_HD // 2, -1.0, 1.0)
    tabs = np.stack([cos * scale * QK_SCALE, sin * scale * QK_SCALE, cos / scale, sin / scale], axis=1)
    return tabs.astype(f32)


def score_mask():
    q, own = np.arange(P)[:, None], np.arange(P)[None, :]
    first = (own <= q) & (own >= q - WINDOW)
    key = np.arange(F_KEYS)[None, :] - WINDOW
    second = (key <= q) & (key >= q - WINDOW)
    return np.where(np.concatenate([first, first, second, second], axis=1), 0.0, MASKED).astype(np.float32)


def kernel(**inputs):
    import concourse.bacc as bacc
    from concourse.bass_utils import run_bass_kernel_spmd

    nc = bacc.Bacc("TRN2", target_bir_lowering=False, num_devices=1)
    f = {k: np.asarray(a) for k, a in inputs.items()}
    arrays = {
        "x": f["L0_attn_hidden_states"],
        "wqT": f["L0_attn_w_q"].T, "wkT": f["L0_attn_w_k"].T, "wvT": f["L0_attn_w_v"].T, "woT": f["L0_attn_w_o"].T,
        "wkgenT": f["L0_attn_w_kgen"].T, "bkgen": f["L0_attn_b_kgen"],
        "wconv": f["L0_attn_w_conv"].reshape(DIM, KS), "bconv": f["L0_attn_b_conv"],
        "wqkv": f["L0_ffn_wqkv"], "q_scale": f["L0_ffn_q_scale"], "k_scale": f["L0_ffn_k_scale"], "wof": f["L0_ffn_wo"],
        "ln_g": f["L0_ffn_ln_g"], "ln_b": f["L0_ffn_ln_b"], "w1": f["L0_ffn_w1"], "b1": f["L0_ffn_b1"],
        "w2": f["L0_ffn_w2"], "b2": f["L0_ffn_b2"],
        "eye": np.eye(P, dtype=np.float32), "rotary": rotary_tables(), "mask": score_mask(),
    }
    arrays = {f"in_{k}": np.ascontiguousarray(a) for k, a in arrays.items()}
    t = {k[3:]: nc.dram_tensor(k, a.shape, mybir.dt.from_np(a.dtype), kind="ExternalInput").ap() for k, a in arrays.items()}
    for name in ("x1", "x2", "x3", "x4"):
        t[name] = nc.dram_tensor(f"stage_{name}", (BATCH, SEQ, DIM), FP32, kind="Internal").ap()
    t["out"] = nc.dram_tensor("out_x", (BATCH, SEQ, DIM), FP32, kind="ExternalOutput").ap()
    build(nc, t)
    r = run_bass_kernel_spmd(nc, [arrays], core_ids=[0])
    return r.results[0]["out_x"]
```

```python
import concourse.bass as bass
from concourse import mybir
from contextlib import ExitStack
import numpy as np

FP32 = mybir.dt.float32
BF16 = mybir.dt.bfloat16
FP32R = mybir.dt.float32r
ALU = mybir.AluOpType
ACT = mybir.ActivationFunctionType
AX = mybir.AxisListType

BATCH, SEQ, DIM = 16, 256, 128
P = 128
TILES = SEQ // P
A_HEADS, A_KV, A_HD = 16, 4, 64
A_REP = A_HEADS // A_KV
CHUNK = 64
CHUNKS = SEQ // CHUNK
KS = 3
LAYERS, F_HEADS, F_HD, WINDOW = 2, 8, 64, 64
INNER = F_HEADS * F_HD
F_HID = int(DIM * 4 * 2 / 3)
LN_EPS = 1e-5

PAIR = 2
TURNS = BATCH // PAIR
A_SLOTS = PAIR * TILES
A_STEPS = A_SLOTS * A_KV
E_RING = 8
EXP_LAG, SUM_LAG, NORM_LAG, PV_LAG, OUT_LAG, LN_LAG = 1, 2, 5, 7, 11, 14
F_GROUPS = 2
F_GH = F_HEADS // F_GROUPS
F_SLOTS = PAIR * TILES
F_STEPS = F_SLOTS * F_GROUPS
F_BATCH = TILES * F_GROUPS
F_EXP_LAG, F_SUM_LAG, F_NORM_LAG, F_PV_LAG = 1, 2, 2, 4
F_LATE = {
    "out": (6, F_GROUPS),
    "stats": (10, F_BATCH), "norm": (11, F_BATCH), "mT": (13, F_BATCH),
    "gates": (14, F_BATCH), "mix": (14, F_BATCH), "residual": (14, F_BATCH), "values": (16, F_BATCH),
    "down": (17, F_BATCH), "z": (18, F_BATCH),
}
F_KEYS = P + WINDOW
F_RING = 4
F_CHUNKS = -(-F_HID // P)
F_ROWS = [min(P, F_HID - P * c) for c in range(F_CHUNKS)]
QK_SCALE = 8.0
MASKED = -1e30


def wait(engine, sem, value):
    if isinstance(value, int) and value <= 0:
        return
    engine.wait_ge(sem, value)


class SharedBanks:

    BEFORE = {"drain2": "drain", "drain": "last", "last": "middle", "middle": "middle", "second": "first", "first": "pre"}

    def __init__(self, order, pre, stride, late):
        assert len(order) % 2 == 0
        self.order, self.pre, self.stride, self.late = order, pre, stride, late

    def bank(self, kind, local, turn):
        if turn == "pre":
            return (self.pre.index((kind, local)) + len(self.pre)) % 2
        return self.order.index((kind, local)) % 2

    def left_out(self, turn, kind, local):
        if kind in self.late:
            if turn in ("first", "second"):
                return self.stride[kind] * (turn == "second") + local < 0
            return turn in ("drain", "drain2") and self.stride[kind] * (turn == "drain2") + local >= 0
        return turn in ("drain", "drain2") or turn == "last" and local // (self.stride[kind] // PAIR) >= PAIR

    def before(self, kind, local, turn):
        if turn == "pre":
            at = self.pre.index((kind, local)) - 2
            return (*self.pre[at], 0) if at >= 0 else None
        back, shift, at = self.order.index((kind, local)) - 2, 0, turn
        while True:
            if back < 0:
                at, shift, back = self.BEFORE[at], shift - 1, back + len(self.order)
                if at == "pre":
                    same = [f for f in self.pre if self.bank(*f, "pre") == back % 2]
                    return (*same[-1], 0)
            if not self.left_out(at, *self.order[back]):
                return (*self.order[back], shift)
            back -= 2


def stage_a_banks():
    order = []
    for s in range(A_STEPS):
        slot, g = divmod(s, A_KV)
        p, tile = divmod(slot, TILES)
        if tile == 0 and g == 0:
            order.append(("xT", p + 1))
        if tile == 0 and g == 2:
            order.append(("gate", p + 1))
        if tile == 1:
            order += [(k, per * (p + 1) + m) for k, per, m in A_PROJECTIONS[g]]
        order.append(("o", s - PV_LAG))
        if g == OUT_LAG % A_KV:
            order.append(("out", (s - OUT_LAG) // A_KV))
    pre = [("xT", 0), ("gate", 0)] + [(k, m) for g in range(A_KV) for k, per, m in A_PROJECTIONS[g]]
    stride = {"xT": PAIR, "gate": PAIR, "k": PAIR, "q": 4 * PAIR, "v": PAIR, "o": A_STEPS, "out": A_SLOTS}
    return SharedBanks(order, pre, stride, ("o", "out"))


A_PROJECTIONS = {0: [], 1: [("q", 4, 0), ("q", 4, 1)], 2: [("q", 4, 2), ("k", 1, 0)], 3: [("q", 4, 3), ("v", 1, 0)]}


F_FILLS = {
    0: ["out", "values", ("qk", 4, 0, 1)],
    1: [("qk", 4, 1, 1), "down", ("qkT", 4, 2, 0), ("qkT", 4, 3, 0), "mT"],
    2: [("qk", 4, 2, 1), "out", "gates", "mix"],
    3: [("qk", 4, 3, 1), ("qkT", 4, 0, 1), ("v", 2, 0, 1), ("qkT", 4, 1, 1), ("v", 2, 1, 1), ("hT", 1, 0, 2)],
}


def stage_f_banks():
    order = []
    for s in range(F_STEPS):
        p, at = divmod(s, F_BATCH)
        for fill in F_FILLS[at]:
            if isinstance(fill, str):
                lag, every = F_LATE[fill]
                order.append((fill, (s - lag) // every))
            else:
                kind, per, m, ahead = fill
                order.append((kind, per * (p + ahead) + m))
    prepared = [f for at in range(F_BATCH) for f in F_FILLS[at] if not isinstance(f, str) and f[3] == 1]
    pre = [("hT", 0)] + [(k, m) for kind in ("qk", "v", "qkT") for k, per, m, _ in prepared if k == kind] + [("hT", 1)]
    late = ("out", "mT", "gates", "mix", "values", "down")
    stride = {"hT": PAIR, "qk": 4 * PAIR, "v": 2 * PAIR, "qkT": 4 * PAIR, **{k: F_STEPS // F_LATE[k][1] for k in late}}
    return SharedBanks(order, pre, stride, late)


A_BANKS, F_BANKS = stage_a_banks(), stage_f_banks()


def build(nc, t):
    ctx = ExitStack()
    with ctx:
        def sb(name, shape, dt=FP32):
            return ctx.enter_context(nc.sbuf_tensor(name, shape, dt))

        def sem(name):
            return ctx.enter_context(nc.semaphore(name))

        banks = [ctx.enter_context(nc.psum_tensor(f"bank{i}", [P, 512], FP32)) for i in range(8)]
        x_in = t["x"].rearrange("b (t p) d -> p b t d", p=P)
        x1, x2, x3, x4, x_out = (t[k].rearrange("b (t p) d -> p b t d", p=P) for k in ("x1", "x2", "x3", "x4", "out"))

        ident = sb("ident", [P, P])
        ones = sb("ones", [P, P])
        halves = sb("halves", [P, 32])
        eps = sb("eps", [P, TILES])
        wq = sb("wq", [P, A_HEADS * A_HD])
        wk = sb("wk", [P, A_KV * A_HD])
        wv = sb("wv", [P, A_KV * A_HD])
        wo = sb("wo", [P, A_HEADS // 2, DIM])
        wkgen = sb("wkgen", [P, KS])
        bkgen = sb("bkgen", [P, KS])
        wconv = sb("wconv", [P, KS])
        bconv = sb("bconv", [P, 1])

        xn = [sb(f"xn{p}", [P, TILES, DIM]) for p in range(PAIR)]
        xr = [sb(f"xr{p}", [P, TILES, DIM]) for p in range(PAIR)]
        xT = sb("xT", [P, SEQ + 2])
        ctx_sum = sb("ctx_sum", [P, 1])
        wk_ctx = sb("wk_ctx", [P, KS])
        gate = sb("gate", [P, 4, KS])
        gate_sum = sb("gate_sum", [P, 1])
        conv = sb("conv", [P, 3, SEQ])
        hT = sb("hT", [P, SEQ])
        qT = [sb(f"qT{p}", [P, A_HEADS // 2, SEQ]) for p in range(PAIR)]
        kT = [sb(f"kT{p}", [P, A_KV, SEQ]) for p in range(PAIR)]
        v = [sb(f"v{p}", [P, TILES, A_KV * A_HD]) for p in range(PAIR)]
        probs = sb("probs", [P, E_RING, A_REP * SEQ])
        E = [probs[:, r, :].rearrange("p (h c k) -> p h c k", h=A_REP, c=CHUNKS) for r in range(E_RING)]
        mx = [sb(f"mx{r}", [P, A_REP, CHUNKS]) for r in range(2)]
        sums = [sb(f"sums{r}", [P, A_HEADS, CHUNKS]) for r in range(2)]
        coef = [sb(f"coef{r}", [P, 3, A_HEADS, CHUNKS]) for r in range(2)]
        total = [sb(f"total{r}", [P, 3, A_HEADS]) for r in range(2)]
        wT = [sb(f"wT{r}", [P, TILES, 2, P]) for r in range(2)]
        oT = [sb(f"oT{r}", [P, A_HEADS // 2, P]) for r in range(2)]
        y = [sb(f"y{r}", [P, DIM]) for r in range(2)]
        stat = [sb(f"stat{r}", [P, 6]) for r in range(2)]
        mv = [sb(f"mv{r}", [P, 2]) for r in range(2)]
        rstd = [sb(f"rstd{r}", [P, 2]) for r in range(2)]
        xo = [sb(f"xo{r}", [P, DIM]) for r in range(2)]

        wqkv = [sb(f"wqkv{l}", [P, 3 * INNER]) for l in range(LAYERS)]
        wqkv_low = [sb(f"wqkv_low{l}", [P, 3 * INNER], FP32R) for l in range(LAYERS)]
        wqkv_high = [sb(f"wqkv_high{l}", [P, 3 * INNER], FP32R) for l in range(LAYERS)]
        wof = [sb(f"wof{l}", [P, INNER // P, DIM]) for l in range(LAYERS)]
        w1 = [sb(f"w1_{l}", [P, 2 * F_HID]) for l in range(LAYERS)]
        w2 = [sb(f"w2_{l}", [P, F_CHUNKS, DIM]) for l in range(LAYERS)]
        b1 = [sb(f"b1_{l}", [P, 2, F_CHUNKS]) for l in range(LAYERS)]
        b2 = [sb(f"b2_{l}", [P, DIM]) for l in range(LAYERS)]
        ln_g = [sb(f"ln_g{l}", [P, 1]) for l in range(LAYERS)]
        ln_b = [sb(f"ln_b{l}", [P, 1]) for l in range(LAYERS)]
        rotary = sb("rotary", [P, TILES, 4, F_HD])
        qk_scale = [sb(f"qk_scale{l}", [P, 4, F_HD]) for l in range(LAYERS)]
        table = [sb(f"table{l}", [P, TILES, 4, F_HD]) for l in range(LAYERS)]
        mask = sb("mask", [P, 2 * (P + F_KEYS)], BF16)
        ident16 = sb("ident16", [P, P], BF16)

        hn = [sb(f"hn{p}", [P, TILES, DIM]) for p in range(PAIR)]
        fhT_high, fhT_low = sb("fhT_high", [P, SEQ], FP32R), sb("fhT_low", [P, SEQ], FP32R)

        def in_queries(p, at):
            return qT[p][:, 2 * at:2 * at + 2, :].rearrange("p a b -> p (a b)")

        raw = [in_queries(0, r).rearrange("p (h d) -> p h d", h=F_HEADS) for r in range(2)]
        sq = [in_queries(0, 2 + r) for r in range(2)]
        on_self = [in_queries(1, r).rearrange("p (h d) -> p h d", h=F_HEADS) for r in range(2)]
        on_partner = [in_queries(1, 2 + r).rearrange("p (h d) -> p h d", h=F_HEADS) for r in range(2)]
        qk = [kT[m // 2][:, 2 * (m % 2):2 * (m % 2) + 2, :].rearrange("p a b -> p (a b)").rearrange("p (h d) -> p h d", h=F_HEADS)
              for m in range(4)]
        norm2 = sb("norm2", [P, 2, 4 * F_HEADS])
        rnorm = sb("rnorm", [P, 4 * F_HEADS])
        qkT = [probs[:, 2 * p:2 * p + 2, :].rearrange("p r (m q) -> p (r m) q", q=SEQ) for p in range(PAIR)]
        f_v = [sb(f"f_v{p}", [P, TILES, F_HEADS, F_HD]) for p in range(PAIR)]
        fE = [probs[:, 4 + r, 0:F_GH * F_KEYS].rearrange("p (k a n) -> p k a n", k=2, a=2) for r in range(F_RING)]
        fmx = [sb(f"fmx{r}", [P, 2, 2]) for r in range(2)]
        eT = sb("eT", [P, F_GH, P])
        eT_back = sb("eT_back", [P, F_GH, P])
        f_sum = [sb(f"f_sum{r}", [P, 2, 2]) for r in range(2)]
        f_rsum = [sb(f"f_rsum{r}", [P, 2, 2]) for r in range(2)]
        foT = [sb(f"foT{r}", [P, INNER // P, P]) for r in range(2)]

        hc = [sb(f"hc{p}", [P, TILES, DIM]) for p in range(PAIR)]
        hT2 = [sb(f"hT2_{p}", [P, SEQ]) for p in range(PAIR)]
        ge = [sb(f"ge{c}", [P, SEQ]) for c in range(F_CHUNKS)]
        uT = [sb(f"uT{p}", [P, F_CHUNKS, SEQ]) for p in range(PAIR)]
        mask32 = uT[1][:, :, :].rearrange("p c n -> p (c n)")[:, 0:2 * (P + F_KEYS)]
        mn = [sb(f"mn{p}", [P, TILES, DIM]) for p in range(PAIR)]
        res = [sb(f"res{p}", [P, TILES, DIM]) for p in range(PAIR)]
        m_res = [sb(f"m_res{p}", [P, TILES, DIM]) for p in range(PAIR)]
        res1 = [sb(f"res1_{p}", [P, TILES, DIM]) for p in range(PAIR)]
        resb = [sb(f"resb{p}", [P, 2, TILES, DIM]) for p in range(PAIR)]
        yo = [sb(f"yo{p}", [P, TILES, DIM]) for p in range(PAIR)]
        zo = [sb(f"zo{p}", [P, TILES, DIM]) for p in range(PAIR)]
        mstat = [sb(f"mstat{p}", [P, TILES, 6]) for p in range(PAIR)]
        mmv = [sb(f"mmv{p}", [P, TILES, 2]) for p in range(PAIR)]
        mrstd = [sb(f"mrstd{p}", [P, 2, TILES]) for p in range(PAIR)]
        zstat = [sb(f"zstat{p}", [P, TILES, 6]) for p in range(PAIR)]
        zmv = [sb(f"zmv{p}", [P, TILES, 2]) for p in range(PAIR)]
        zrstd = [sb(f"zrstd{p}", [P, 2, TILES]) for p in range(PAIR)]

        gate_weights_in, a_weights_in, weights_in = sem("gate_weights_in"), sem("a_weights_in"), sem("weights_in")
        consts_set = sem("consts_set")
        xn_in = [sem(f"xn{p}_in") for p in range(PAIR)]
        xr_in = [sem(f"xr{p}_in") for p in range(PAIR)]
        xo_out = [sem(f"xo{r}_out") for r in range(2)]
        made = {k: sem(f"{k}_made") for k in A_BANKS.stride}
        read = {k: sem(f"{k}_read") for k in A_BANKS.stride}
        wk_ctx_set, gate_exp, gate_step, conv_step, hT_set = (
            sem(n) for n in ("wk_ctx_set", "gate_exp", "gate_step", "conv_step", "hT_set"))
        scored, max_set, sub_done, exp_done, sum_done, coef_step, normed = (
            sem(n) for n in ("scored", "max_set", "sub_done", "exp_done", "sum_done", "coef_step", "normed"))
        wT_made, wT_read, pv_done = sem("wT_made"), sem("wT_read"), sem("pv_done")
        stats_waited, y_step, eps_added, rstd_set, xo_set = sem("stats_waited"), sem("y_step"), sem("eps_added"), sem("rstd_set"), sem("xo_set")

        f_made = {k: sem(f"f_{k}_made") for k in F_BANKS.stride}
        f_read = {k: sem(f"f_{k}_read") for k in F_BANKS.stride if k not in ("gates", "mix", "values")}
        gelu_done, u_done = sem("gelu_done"), sem("u_done")
        f_read.update(gates=gelu_done, mix=u_done, values=u_done)
        READ_COUNTS = {"gates": (F_CHUNKS, 2), "mix": (F_CHUNKS, 1), "values": (F_CHUNKS, F_CHUNKS)}
        f_o_made, f_o_read = sem("f_o_made"), sem("f_o_read")
        hn_in = [sem(f"hn{p}_in") for p in range(PAIR)]
        res_in = [sem(f"res{p}_in") for p in range(PAIR)]
        mn_in = [sem(f"mn{p}_in") for p in range(PAIR)]
        m_res_in = [sem(f"m_res{p}_in") for p in range(PAIR)]
        res1_in = [sem(f"res1_{p}_in") for p in range(PAIR)]
        f_out = [sem(f"f_out{r}") for r in range(2)]
        m_out = [sem(f"m_out{p}") for p in range(PAIR)]
        tables_set, f_consts = sem("tables_set"), sem("f_consts")
        weights_rounded, weights_split, hT_rounded = sem("weights_rounded"), sem("weights_split"), sem("hT_rounded")
        squared, rotated, norm_step, guarded, added, rnorm_set, qk_normed = (
            sem(n) for n in ("squared", "rotated", "norm_step", "guarded", "added", "rnorm_set", "qk_normed"))
        f_scored, f_max, f_sub, f_exp, f_sum_set, f_rsum_set, f_normed, eT_made, eT_read, back_read = (
            sem(n) for n in ("f_scored", "f_max", "f_sub", "f_exp", "f_sum_set", "f_rsum_set", "f_normed", "eT_made", "eT_read", "back_read"))
        m_bn, m_stats, m_eps, m_rstd, hc_set, resb_step = (
            sem(n) for n in ("m_bn", "m_stats", "m_eps", "m_rstd", "hc_set", "resb_step"))
        z_bn, z_stats, z_eps, z_rstd, z_set = (sem(n) for n in ("z_bn", "z_stats", "z_eps", "z_rstd", "z_set"))

        block = ctx.enter_context(nc.Block())
        COEF_STEPS = 7
        N_GATE_WEIGHTS, N_A_WEIGHTS, N_WEIGHTS = 5, 4, 2 + LAYERS * (6 + 3 * F_CHUNKS + 6)
        N_CONSTS, N_F_CONSTS = 5, 7
        GATE_STEPS = 3

        def stage_a(engine, body, pre=None):
            if pre:
                pre()
            body(0, "first")
            body(1, "middle")
            with engine.Fori(2, TURNS - 1) as i:
                body(i, "middle")
            body(TURNS - 1, "last")

        def first_fill(s):
            return F_BANKS.pre[s - 1] if 1 <= s <= len(F_BANKS.pre) else None

        def f_bank(kind, local, turn):
            if turn == "pre":
                return banks[F_BANKS.pre.index((kind, local)) % 4]
            return banks[6 + F_BANKS.bank(kind, local, turn)]

        def f_steps(turn):
            for s in range(F_STEPS):
                slot, g = divmod(s, F_GROUPS)
                yield (s, slot, *divmod(slot, TILES), g)

        def f_fills(turn, s):
            p, at = divmod(s, F_BATCH)
            for fill in F_FILLS[at]:
                if isinstance(fill, str):
                    index = f_late(turn, s, fill)
                    if index is not None:
                        yield fill, index, 0, 0
                elif prepares(turn, p, fill[3]):
                    kind, per, m, ahead = fill
                    yield kind, per * (p + ahead) + m, m, ahead

        def f_late(turn, s, kind):
            lag, every = F_LATE[kind]
            if (s - lag) % every or not f_exists(turn, s, lag):
                return None
            return (s - lag) // every

        def f_exists(turn, s, lag=0):
            if turn in ("first", "second"):
                return F_STEPS * (turn == "second") + s >= lag
            return turn not in ("drain", "drain2") or F_STEPS * (turn == "drain2") + s < lag

        def both_layers(engine, body, pre=None):
            if pre:
                pre()
            body(0, "first", layer_at(0))
            body(1, "second", layer_at(1))
            body(2, "middle", layer_at(2))
            for layer in range(LAYERS):
                start, end = TURNS * layer + (2 if layer else 3), TURNS * (layer + 1) - 1
                with engine.Fori(start, end) as it:
                    body(it, "middle", lambda local, layer=layer: layer)
                if layer < LAYERS - 1:
                    for it in range(end, end + 3):
                        body(it, "middle", layer_at(it))
            for it, turn in zip(range(LAYERS * TURNS - 1, LAYERS * TURNS + 2), ("last", "drain", "drain2")):
                body(it, turn, layer_at(it))

        def layer_at(it):
            return lambda local: (PAIR * it + local) // BATCH

        def keys(tile):
            return (P, 0) if tile == 0 else (F_KEYS, P - WINDOW)

        def steps(i, turn, beside=None):
            for s in range(A_STEPS if turn != "drain" else LN_LAG):
                slot, g = divmod(s, A_KV)
                p, tile = divmod(slot, TILES)
                yield s, slot, p, tile, g
                if beside:
                    beside(s)

        def exists(turn, s, lag=0):
            return not (turn == "first" and s < lag) and not (turn == "drain" and s >= lag)

        def prepares(turn, p, ahead=1):
            return turn not in ("drain", "drain2") and not (turn == "last" and p + ahead >= PAIR)

        def bank_free(pe, shared, read, kind, local, i, turn):
            last = shared.before(kind, local, turn)
            if last:
                kind_before, index, turns_back = last
                step, offset = READ_COUNTS.get(kind_before, (1, 1))
                wait(pe, read[kind_before], step * (shared.stride[kind_before] * (i + turns_back) + index) + offset)

        def layer_weights(l):
            half = F_HD // 2
            yield wqkv[l][:, :], t["wqkv"][l]
            yield wof[l][:, :, :], t["wof"][l].rearrange("(m p) n -> p m n", p=P)
            yield w1[l][:, :], t["w1"][l]
            yield b2[l][:, :], t["b2"][l].partition_broadcast(P)
            yield ln_g[l][:, :], t["ln_g"][l].rearrange("(p a) -> p a", a=1)
            yield ln_b[l][:, :], t["ln_b"][l].rearrange("(p a) -> p a", a=1)
            for c, rows in enumerate(F_ROWS):
                yield w2[l][0:rows, c, :], t["w2"][l, P * c:P * c + rows, :]
                for a in range(2):
                    at = F_HID * a + P * c
                    yield b1[l][0:rows, a, c:c + 1], t["b1"][l, at:at + rows].rearrange("(p a) -> p a", a=1)
            for a, name in enumerate(("q_scale", "k_scale")):
                yield qk_scale[l][:, 2 * a, :], t[name][l].partition_broadcast(P)
                yield qk_scale[l][:, 2 * a + 1, 0:half], t[name][l, half:].partition_broadcast(P)
                yield qk_scale[l][:, 2 * a + 1, half:], t[name][l, 0:half].partition_broadcast(P)

        @block.sync
        def _(sp):
            def load(dst, b, done, x_in=x_in):
                sp.dma_start(dst[:, :, :], x_in[:, bass.ds(b, 1), :, :]).then_inc(done, 16)

            def pre():
                load(xn[0], 0, xn_in[0])
                for dst, src in (
                    (ident[:, :], t["eye"]), (wkgen[:, :], t["wkgenT"]), (bkgen[:, :], t["bkgen"].partition_broadcast(P)),
                    (wconv[:, :], t["wconv"]), (bconv[:, :], t["bconv"].rearrange("(p a) -> p a", a=1)),
                ):
                    sp.dma_start(dst, src).then_inc(gate_weights_in, 16)
                for dst, src in (
                    (wk[:, :], t["wkT"]), (wq[:, :], t["wqT"]), (wv[:, :], t["wvT"]),
                    (wo[:, :, :], t["woT"].rearrange("(m p) n -> p m n", p=P)),
                ):
                    sp.dma_start(dst, src).then_inc(a_weights_in, 16)
                load(xn[1], 1, xn_in[1])
                load(xr[0], 0, xr_in[0])
                load(xr[1], 1, xr_in[1])
                for dst, src in (
                    (rotary[:, :, :, :], t["rotary"].rearrange("(t p) a d -> p t a d", p=P)), (mask32, t["mask"]),
                    *[pair for l in range(LAYERS) for pair in layer_weights(l)],
                ):
                    sp.dma_start(dst, src).then_inc(weights_in, 16)

            def body(i, turn):
                for p in range(PAIR):
                    b = PAIR * i + p
                    if turn in ("first", "middle"):
                        wait(sp, made["xT"], b + 1)
                        load(xn[p], b + 2, xn_in[p])
                    if turn in ("middle", "last"):
                        wait(sp, read["out"], TILES * (b - 1))
                        load(xr[p], b, xr_in[p])
                    for tile in range(TILES):
                        at = TILES * p + tile - 3
                        j = A_SLOTS * i + at
                        if (turn == "first" and at < 0) or (turn == "drain" and at >= 0):
                            continue
                        wait(sp, xo_set, j + 1)
                        r = at % 2
                        jb, jt = (at // TILES), at % TILES
                        sp.dma_start(x1[:, bass.ds(PAIR * i + jb, 1), jt, :], xo[r][:, :]).then_inc(xo_out[r], 16)

            stage_a(sp, body, pre)
            a_drain = body

            HALF = DIM // 2

            def load_shifted(dst, b, done, src):
                x = src[:, bass.ds(b, 1), :, :]
                sp.dma_start(dst[:, :, 0:HALF], x[:, :, :, 0:HALF]).then_inc(done, 16)
                sp.dma_start(dst[1:P, 0, HALF:DIM], x[0:P - 1, :, 0, HALF:DIM]).then_inc(done, 16)
                sp.dma_start(dst[0:1, 1, HALF:DIM], x[P - 1:P, :, 0, HALF:DIM]).then_inc(done, 16)
                sp.dma_start(dst[1:P, 1, HALF:DIM], x[0:P - 1, :, 1, HALF:DIM]).then_inc(done, 16)

            def layers_program():
                sources, middles, results = (x1, x3), (x2, x4), (x3, x_out)

                def pre():
                    for p in range(PAIR):
                        sp.wait_ge(xo_out[p], 16 * PAIR)
                    for p in range(PAIR):
                        load_shifted(hn[p], p, hn_in[p], sources[0])
                    a_drain(TURNS, "drain")
                    for r in range(2):
                        sp.wait_ge(xo_out[r], 16 * BATCH * TILES // 2)

                def body(it, turn, layer_of):
                    for p in range(PAIR):
                        bb = PAIR * it + p

                        def at(local):
                            return layer_of(local), PAIR * it + local - BATCH * layer_of(local)

                        if prepares(turn, p, 2):
                            layer, b = at(p + 2)
                            wait(sp, f_made["hT"], bb + 1)
                            if layer > 0:
                                sp.wait_ge(m_out[p], 16 * (it + 2 - TURNS))
                            load_shifted(hn[p], b, hn_in[p], sources[layer])
                        if f_exists(turn, F_BATCH * p, 2 * F_BATCH):
                            layer, b = at(p - 2)
                            for tile in range(TILES):
                                wait(sp, f_read["out"], F_SLOTS * it + TILES * (p - 2) + tile + 1)
                                sp.dma_start(middles[layer][:, bass.ds(b, 1), tile, :], xo[tile][:, :]).then_inc(f_out[tile], 16)
                        if prepares(turn, p, 0):
                            layer, b = at(p)
                            wait(sp, f_read["out"], TILES * (bb - 1))
                            load(res[p], b, res_in[p], sources[layer])
                        if f_exists(turn, F_BATCH * p, 2 * F_BATCH):
                            layer, b = at(p - 2)
                            for tile in range(TILES):
                                sp.wait_ge(f_out[tile], 16 * (bb - 1))
                            load_shifted(mn[p], b, mn_in[p], middles[layer])
                        if f_exists(turn, F_BATCH * p, 4 * F_BATCH):
                            layer, b = at(p - 4)
                            if layer == LAYERS - 1:
                                wait(sp, z_set, b + 1)
                            else:
                                wait(sp, f_read["down"], bb - 3)
                            sp.dma_start(results[layer][:, bass.ds(b, 1), :, :],
                                         (zo if layer == LAYERS - 1 else yo)[p][:, :, :]).then_inc(m_out[p], 16)
                        if f_exists(turn, F_BATCH * p, 2 * F_BATCH):
                            layer, b = at(p - 2)
                            wait(sp, f_read["down"], bb - 3)
                            load(m_res[p], b, m_res_in[p], middles[layer])
                            if layer == LAYERS - 1:
                                load(res1[p], b, res1_in[p], x1)

                both_layers(sp, body, pre)
                for p in range(PAIR):
                    sp.wait_ge(f_out[p], 16 * LAYERS * BATCH)
                    sp.wait_ge(m_out[p], 16 * LAYERS * TURNS)

            layers_program()

        @block.gpsimd
        def _(pool):
            pool.memset(ones[:, :], 1.0).then_inc(consts_set, 1)
            pool.memset(halves[:, :], -0.5).then_inc(consts_set, 1)
            pool.memset(eps[:, :], LN_EPS).then_inc(consts_set, 1)
            pool.memset(xT[:, 0:1], 0.0).then_inc(consts_set, 1)
            pool.memset(xT[:, SEQ + 1:SEQ + 2], 0.0).then_inc(consts_set, 1)
            for p in range(PAIR):
                pool.memset(hn[p][0:1, 0, DIM // 2:DIM], 0.0).then_inc(f_consts, 1)
                pool.memset(mn[p][0:1, 0, DIM // 2:DIM], 0.0).then_inc(f_consts, 1)
            pool.memset(eT_back[0:WINDOW, :, :], 0.0).then_inc(f_consts, 1)
            pool.wait_ge(consts_set, N_CONSTS)
            pool.wait_ge(weights_in, 16 * N_WEIGHTS)
            for l in range(LAYERS):
                for tile in range(TILES):
                    nc.gpsimd.tensor_tensor(out=table[l][:, tile, :, :], in0=rotary[:, tile, :, :], in1=qk_scale[l][:, :, :],
                                            op=ALU.mult).then_inc(tables_set, 1)

            def split_weights(l, part):
                cols = slice(INNER * part, INNER * (part + 1))
                nc.gpsimd.tensor_copy(wqkv_high[l][:, cols], wqkv[l][:, cols]).then_inc(weights_rounded, 1)
                pool.wait_ge(weights_rounded, 3 * l + part + 1)
                nc.gpsimd.tensor_tensor(out=wqkv_low[l][:, cols], in0=wqkv[l][:, cols], in1=wqkv_high[l][:, cols].bitcast(FP32),
                                        op=ALU.subtract).then_inc(weights_split, 1)

            def a_body(i, turn, beside=None):
                for s, slot, p, tile, g in steps(i, turn, beside):
                    if exists(turn, s, NORM_LAG):
                        at, ng = divmod(s - NORM_LAG, A_KV)
                        r = at % 2
                        wait(pool, coef_step, COEF_STEPS * (A_SLOTS * i + at + 1))
                        e = E[(s - NORM_LAG) % E_RING]
                        nc.gpsimd.tensor_tensor(
                            out=e[:, :, :, :], in0=e[:, :, :, :],
                            in1=coef[r][:, 2, A_REP * ng:A_REP * (ng + 1), :].unsqueeze(3).broadcast_to([P, A_REP, CHUNKS, CHUNK]),
                            op=ALU.mult).then_inc(normed, 1)
                    if turn == "first" and s < 3 * LAYERS:
                        split_weights(*divmod(s, 3))
                    if g == (OUT_LAG + 1) % A_KV and exists(turn, s, OUT_LAG + 1):
                        at = (s - OUT_LAG - 1) // A_KV
                        j = A_SLOTS * i + at
                        r = at % 2
                        wait(pool, y_step, 2 * j + 2)
                        nc.gpsimd.tensor_tensor(out=rstd[r][:, 0:1], in0=mv[r][:, 1:2], in1=eps[:, 0:1], op=ALU.add).then_inc(eps_added, 1)
                        wait(pool, eps_added, j + 1)
                        wait(pool, xo_set, j - 1)
                        nc.gpsimd.tensor_tensor(out=rstd[r][:, 1:2], in0=rstd[r][:, 0:1], in1=halves[:, 0:1],
                                                op=ALU.pow).then_inc(rstd_set, 1)

            stage_a(pool, a_body)

            def layers_program():
                def sums(it, local, m):
                    index = F_BANKS.stride["qk"] * it + local
                    pool.wait_ge(rotated, index + 1)
                    wait(pool, f_made["qkT"], index - 3)
                    nc.gpsimd.tensor_tensor(out=qk[m][:, :, :], in0=on_self[m % 2][:, :, :], in1=on_partner[m % 2][:, :, :],
                                            op=ALU.add).then_inc(added, 1)

                def inverse_norms(bb, tile):
                    pool.wait_ge(guarded, TILES * bb + tile + 1)
                    wait(pool, qk_normed, 4 * (bb - 1) + 2 * tile + 2)
                    at = slice(2 * F_HEADS * tile, 2 * F_HEADS * (tile + 1))
                    nc.gpsimd.tensor_tensor(out=rnorm[:, at], in0=norm2[:, 1, at], in1=halves[:, 0:2 * F_HEADS],
                                            op=ALU.pow).then_inc(rnorm_set, 1)
                    pool.wait_ge(rnorm_set, TILES * bb + tile + 1)

                def normalise(bb, m):
                    wait(pool, added, 4 * bb + m + 1)
                    nc.gpsimd.tensor_tensor(
                        out=qk[m][:, :, :], in0=qk[m][:, :, :],
                        in1=rnorm[:, F_HEADS * m:F_HEADS * (m + 1)].unsqueeze(2).broadcast_to([P, F_HEADS, F_HD]),
                        op=ALU.mult).then_inc(qk_normed, 1)

                def normalise_tile(bb, tile):
                    for m in (2 * tile, 2 * tile + 1):
                        normalise(bb, m)

                def prepare(bb, it, m, ahead_local):
                    sums(it, ahead_local + m, m)
                    if m % 2 == 1:
                        inverse_norms(bb, m // 2)

                def pre():
                    def beside(s):
                        fill = first_fill(s)
                        if fill and fill[0] == "qk":
                            prepare(0, 0, fill[1], 0)
                            if fill[1] == 1:
                                normalise_tile(0, 0)

                    a_body(TURNS, "drain", beside)

                def rstd_of(mv2, out, step, done, stats, count):
                    pool.wait_ge(stats, TILES * (count + 1))
                    nc.gpsimd.tensor_tensor(out=out[:, 0, :], in0=mv2[:, :, 1], in1=eps[:, 0:TILES], op=ALU.add).then_inc(step, 1)
                    pool.wait_ge(step, count + 1)
                    nc.gpsimd.tensor_tensor(out=out[:, 1, :], in0=out[:, 0, :], in1=halves[:, 0:TILES], op=ALU.pow).then_inc(done, 1)

                def residual(it, local, layer):
                    p, bb, turn_of = local % PAIR, PAIR * it + local, local // PAIR
                    b = bb - BATCH * layer
                    pool.wait_ge(m_res_in[p], 16 * (it + turn_of + 1))
                    wait(pool, f_read["down"], bb - 1)
                    nc.gpsimd.tensor_tensor(out=resb[p][:, 0, :, :], in0=m_res[p][:, :, :],
                                            in1=b2[layer][:, :].unsqueeze(1).broadcast_to([P, TILES, DIM]),
                                            op=ALU.add).then_inc(resb_step, 1)
                    if layer == LAYERS - 1:
                        pool.wait_ge(res1_in[p], 16 * (it + turn_of + 1 - TURNS * layer))
                        wait(pool, resb_step, BATCH * layer + 2 * b + 1)
                        nc.gpsimd.tensor_tensor(out=resb[p][:, 1, :, :], in0=resb[p][:, 0, :, :], in1=res1[p][:, :, :],
                                                op=ALU.add).then_inc(resb_step, 1)

                def body(it, turn, layer_of):
                    for s, slot, p, tile, g in f_steps(turn):
                        if f_exists(turn, s, F_NORM_LAG):
                            n = F_STEPS * it + s - F_NORM_LAG
                            n_keys, _ = keys((s - F_NORM_LAG) // F_GROUPS % TILES)
                            e = fE[(s - F_NORM_LAG) % F_RING][:, :, :, 0:n_keys]
                            pool.wait_ge(f_rsum_set, n + 1)
                            nc.gpsimd.tensor_tensor(out=e, in0=e,
                                                    in1=f_rsum[(s - F_NORM_LAG) % 2][:, :, :].unsqueeze(3).broadcast_to([P, 2, 2, n_keys]),
                                                    op=ALU.mult).then_inc(f_normed, 1)
                        if tile == 0 and g == 0 and prepares(turn, p, 0):
                            normalise_tile(PAIR * it + p, 1)
                        if tile == 1 and g == 0 and prepares(turn, p):
                            normalise_tile(PAIR * it + p + 1, 0)
                        if prepares(turn, p):
                            prepare(PAIR * it + p + 1, it, F_GROUPS * tile + g, 4 * (p + 1))
                        local = f_late(turn, s, "residual")
                        if local is not None:
                            residual(it, local, layer_of(local))
                        local = f_late(turn, s, "stats")
                        if local is not None:
                            rstd_of(mmv[local % PAIR], mrstd[local % PAIR], m_eps, m_rstd, m_stats, PAIR * it + local)
                        local = f_late(turn, s, "down")
                        if local is not None and layer_of(local) == LAYERS - 1:
                            rstd_of(zmv[local % PAIR], zrstd[local % PAIR], z_eps, z_rstd, z_stats, PAIR * it + local - BATCH * (LAYERS - 1))

                both_layers(pool, body, pre)

            layers_program()

        @block.scalar
        def _(act):
            def x_transposed(i, local, turn, b):
                act.wait_ge(made["xT"], b + 1)
                wait(act, hT_set, b)
                wait(act, wk_ctx_set, b)
                nc.scalar.activation(xT[:, 1:SEQ + 1], banks[6 + A_BANKS.bank("xT", local, turn)][:, 0:SEQ], ACT.Copy,
                                     accum_out=ctx_sum[:, :]).then_inc(read["xT"], 1)

            def gate_exponential(b):
                act.wait_ge(read["gate"], b + 1)
                nc.scalar.activation(gate[:, 1, :], gate[:, 0, :], ACT.Exp, scale=-1.0).then_inc(gate_exp, 1)

            def projected(kind, i, local, turn, m, pb):
                index = A_BANKS.stride[kind] * i + local
                act.wait_ge(made[kind], index + 1)
                bank = banks[6 + A_BANKS.bank(kind, local, turn)]
                if kind == "q":
                    nc.scalar.activation(qT[pb][:, 2 * m:2 * m + 2, :], bank[:, :], ACT.Copy, scale=A_HD ** -0.5).then_inc(read[kind], 1)
                elif kind == "k":
                    for a in range(2):
                        for half in range(2):
                            ins = nc.scalar.activation(
                                kT[pb][A_HD * half:A_HD * (half + 1), :, :].rearrange("p (k a) n -> p k a n", a=2)[:, :, a, :],
                                bank[A_HD * a:A_HD * (a + 1), :].rearrange("p (k n) -> p k n", k=2), ACT.Copy)
                    ins.then_inc(read[kind], 1)
                else:
                    nc.scalar.activation(v[pb][:, :, :], bank[:, :], ACT.Copy).then_inc(read[kind], 1)

            def pre():
                act.wait_ge(consts_set, N_CONSTS)
                x_transposed(0, 0, "pre", 0)
                gate_exponential(0)
                for kind, local in A_BANKS.pre[2:]:
                    projected(kind, 0, local, "pre", local, 0)

            def a_body(i, turn, beside=None):
                for s, slot, p, tile, g in steps(i, turn, beside):
                    if exists(turn, s, PV_LAG):
                        n = A_STEPS * i + s - PV_LAG
                        for hp in range(2):
                            act.wait_ge(wT_made, 2 * n + hp + 1)
                            wait(act, pv_done, 2 * (n - 1) + hp + 1)
                            nc.scalar.activation(wT[hp][:, :, :, :], banks[4 + hp][:, :], ACT.Copy).then_inc(wT_read, 1)
                    if prepares(turn, p) and tile == 0:
                        if g == 0:
                            x_transposed(i, p + 1, turn, PAIR * i + p + 1)
                        if g == 3:
                            gate_exponential(PAIR * i + p + 1)
                    if prepares(turn, p) and tile == 1:
                        for kind, per, m in A_PROJECTIONS[g]:
                            projected(kind, i, per * (p + 1) + m, turn, m, (p + 1) % 2)
                    if exists(turn, s, EXP_LAG):
                        n = A_STEPS * i + s - EXP_LAG
                        act.wait_ge(sub_done, n + 1)
                        e = E[(s - EXP_LAG) % E_RING]
                        nc.scalar.activation(e[:, :, :, :], e[:, :, :, :], ACT.Exp).then_inc(exp_done, 1)
                    if exists(turn, s, PV_LAG):
                        n = A_STEPS * i + s - PV_LAG
                        at, og = divmod(s - PV_LAG, A_KV)
                        act.wait_ge(pv_done, 2 * n + 2)
                        wait(act, made["out"], A_SLOTS * i + at - 1)
                        nc.scalar.activation(oT[at % 2][:, 2 * og:2 * og + 2, :],
                                             banks[6 + A_BANKS.bank("o", s - PV_LAG, "middle")][:, 0:2 * P], ACT.Copy).then_inc(read["o"], 1)

            stage_a(act, a_body, pre)

            def layers_program():
                def prepare(it, kind, local, m, batch, turn):
                    act.wait_ge(f_made[kind], F_BANKS.stride[kind] * it + local + 1)
                    bank = f_bank(kind, local, turn)
                    par = (local // (F_BANKS.stride[kind] // PAIR)) % PAIR
                    if kind == "hT":
                        nc.scalar.activation(fhT_high[:, :], bank[:, 0:SEQ], ACT.Copy).then_inc(hT_rounded, 1)
                    elif kind == "qk":
                        wait(act, norm_step, 4 * batch + m - 1)
                        nc.scalar.activation(raw[m % 2][:, :, :], bank[:, :].rearrange("p (h d) -> p h d", h=F_HEADS), ACT.Copy).then_inc(f_read[kind], 1)
                        act.wait_ge(f_read[kind], F_BANKS.stride[kind] * it + local + 1)
                        nc.scalar.activation(sq[m % 2][:, :], raw[m % 2][:, :, :].rearrange("p h d -> p (h d)"), ACT.Square).then_inc(squared, 1)
                    elif kind == "v":
                        wait(act, f_o_made, 4 * (batch - 1))
                        nc.scalar.activation(f_v[par][:, m, :, :], bank[:, :].rearrange("p (h d) -> p h d", h=F_HEADS),
                                             ACT.Copy).then_inc(f_read[kind], 1)
                    else:
                        tile, half = divmod(m, 2)
                        nc.scalar.activation(qkT[par][:, 4 * half:4 * half + 4, P * tile:P * (tile + 1)],
                                             bank[:, :].rearrange("p (m q) -> p m q", m=4), ACT.Copy).then_inc(f_read[kind], 1)

                def pre():
                    def beside(s):
                        fill = first_fill(s)
                        if fill:
                            kind, local = fill
                            per = F_BANKS.stride[kind] // PAIR
                            prepare(0, kind, local, local % per, local // per, "pre")

                    a_body(TURNS, "drain", beside)
                    act.wait_ge(f_consts, N_F_CONSTS)

                def shared_fill(kind, local, m, batch, it, turn, layer_of):
                    if kind == "mix":
                        par, bb = local % PAIR, PAIR * it + local
                        wait(act, u_done, F_CHUNKS * bb)
                        for c, rows in enumerate(F_ROWS):
                            name, col = ("gates", SEQ * c) if c < F_CHUNKS - 1 else ("mix", SEQ)
                            act.wait_ge(f_made[name], bb + 1)
                            nc.scalar.activation(ge[c][0:rows, :], banks[6 + F_BANKS.bank(name, local, "middle")][0:rows, col:col + SEQ],
                                                 ACT.Gelu, bias=b1[layer_of(local)][0:rows, 1, c:c + 1]).then_inc(gelu_done, 1)
                    elif kind in ("hT", "qk", "v", "qkT"):
                        prepare(it, kind, local, m, batch, turn)

                def body(it, turn, layer_of):
                    for s, slot, p, tile, g in f_steps(turn):
                        n = F_STEPS * it + s
                        if f_exists(turn, s, F_PV_LAG):
                            act.wait_ge(eT_made, n - F_PV_LAG + 1)
                            wait(act, f_o_made, n - F_PV_LAG)
                            nc.scalar.activation(eT[:, :, :], banks[4][:, :], ACT.Copy).then_inc(eT_read, 1)
                            if (s - F_PV_LAG) // F_GROUPS % TILES == 1:
                                nc.scalar.activation(eT_back[WINDOW:P, :, :], banks[5][0:WINDOW, :], ACT.Copy).then_inc(back_read, 1)
                        if f_exists(turn, s, F_EXP_LAG):
                            n_keys, _ = keys((s - F_EXP_LAG) // F_GROUPS % TILES)
                            e = fE[(s - F_EXP_LAG) % F_RING]
                            act.wait_ge(f_sub, n - F_EXP_LAG + 1)
                            nc.scalar.activation(e[:, :, :, 0:n_keys], e[:, :, :, 0:n_keys], ACT.Exp).then_inc(f_exp, 1)

                        def shared_fills(fills):
                            for kind, local, m, ahead in fills:
                                shared_fill(kind, local, m, PAIR * it + p + ahead, it, turn, layer_of)

                        fills = list(f_fills(turn, s))
                        shared_fills(fills[:1])
                        if f_exists(turn, s, F_PV_LAG):
                            at, og = divmod(s - F_PV_LAG, F_GROUPS)
                            act.wait_ge(f_o_made, n - F_PV_LAG + 1)
                            wait(act, f_made["out"], F_SLOTS * it + at - 1)
                            nc.scalar.activation(foT[at % 2][:, 2 * og:2 * og + 2, :], banks[5][:, 0:2 * P], ACT.Copy).then_inc(f_o_read, 1)
                        shared_fills(fills[1:])

                both_layers(act, body, pre)

            layers_program()

        @block.vector
        def _(dve):
            def gate_weights(b):
                dve.wait_ge(read["xT"], b + 1)
                wait(dve, made["gate"], b)
                nc.vector.tensor_scalar(wk_ctx[:, :], wkgen[:, :], ctx_sum[:, 0:1], None, ALU.mult).then_inc(wk_ctx_set, 1)

            def gate_logit(b, local, turn):
                dve.wait_ge(made["gate"], b + 1)
                wait(dve, gate_step, GATE_STEPS * b)
                wait(dve, gate_exp, b)
                nc.vector.scalar_tensor_tensor(gate[:, 0, :], banks[6 + A_BANKS.bank("gate", local, turn)][:, 0:KS], 1.0 / SEQ,
                                               bkgen[:, :], ALU.mult, ALU.add).then_inc(read["gate"], 1)

            def convolution(b):
                nc.vector.tensor_scalar(conv[:, 0, :], xT[:, 1:SEQ + 1], wconv[:, 1:2], bconv[:, 0:1],
                                        ALU.mult, ALU.add).then_inc(conv_step, 1)
                dve.wait_ge(conv_step, 3 * b + 1)
                nc.vector.scalar_tensor_tensor(conv[:, 1, :], xT[:, 0:SEQ], wconv[:, 0:1], conv[:, 0, :],
                                               ALU.mult, ALU.add).then_inc(conv_step, 1)
                dve.wait_ge(conv_step, 3 * b + 2)
                nc.vector.scalar_tensor_tensor(conv[:, 2, :], xT[:, 2:SEQ + 2], wconv[:, 2:3], conv[:, 1, :],
                                               ALU.mult, ALU.add).then_inc(conv_step, 1)

            def gated(b):
                dve.wait_ge(gate_exp, b + 1)
                nc.vector.tensor_scalar_add(gate[:, 2, :], gate[:, 1, :], 1.0).then_inc(gate_step, 1)
                dve.wait_ge(gate_step, GATE_STEPS * b + 1)
                nc.vector.reciprocal(gate[:, 3, :], gate[:, 2, :]).then_inc(gate_step, 1)
                dve.wait_ge(gate_step, GATE_STEPS * b + 2)
                nc.vector.tensor_reduce(gate_sum[:, :], gate[:, 3, :], AX.X, ALU.add).then_inc(gate_step, 1)
                dve.wait_ge(gate_step, GATE_STEPS * b + 3)
                dve.wait_ge(conv_step, 3 * b + 3)
                wait(dve, made["v"], b)
                nc.vector.tensor_scalar(hT[:, :], conv[:, 2, :], gate_sum[:, 0:1], 1.0 / KS,
                                        ALU.mult, ALU.mult).then_inc(hT_set, 1)

            def pre():
                dve.wait_ge(gate_weights_in, 16 * N_GATE_WEIGHTS)
                dve.wait_ge(consts_set, N_CONSTS)
                gate_weights(0)
                gate_logit(0, 0, "pre")
                convolution(0)
                gated(0)

            def factors(j, r):
                c, tt = coef[r], total[r]
                k = COEF_STEPS * j

                def link(ins, at):
                    ins.then_inc(coef_step, 1)
                    if at < COEF_STEPS:
                        dve.wait_ge(coef_step, k + at)
                dve.wait_ge(sum_done, A_KV * (j + 1))
                wait(dve, normed, A_KV * (j - 1))
                link(nc.vector.reciprocal(c[:, 0, :, :], sums[r][:, :, :]), 1)
                link(nc.vector.tensor_tensor(c[:, 1, :, :], sums[r][:, :, :], c[:, 0, :, :], ALU.mult), 2)
                link(nc.vector.tensor_reduce(tt[:, 0, :], c[:, 1, :, :], AX.X, ALU.add), 3)
                link(nc.vector.tensor_scalar_add(tt[:, 1, :], tt[:, 0, :], 1e-9), 4)
                link(nc.vector.reciprocal(tt[:, 2, :], tt[:, 1, :]), 5)
                link(nc.vector.tensor_tensor(c[:, 1, :, :], c[:, 1, :, :],
                                             tt[:, 2, :].unsqueeze(2).broadcast_to([P, A_HEADS, CHUNKS]), ALU.mult), 6)
                link(nc.vector.tensor_tensor(c[:, 2, :, :], c[:, 0, :, :], c[:, 1, :, :], ALU.mult), 7)

            def summed(i, turn, s):
                if exists(turn, s, SUM_LAG):
                    n = A_STEPS * i + s - SUM_LAG
                    at, gg = divmod(s - SUM_LAG, A_KV)
                    dve.wait_ge(exp_done, n + 1)
                    nc.vector.tensor_reduce(sums[at % 2][:, A_REP * gg:A_REP * (gg + 1), :], E[(s - SUM_LAG) % E_RING][:, :, :, :],
                                            AX.X, ALU.add).then_inc(sum_done, 1)
                    if gg == A_KV - 1:
                        factors(A_SLOTS * i + at, at % 2)

            def layer_constants(s):
                if s == A_STEPS - 1:
                    dve.wait_ge(tables_set, LAYERS * TILES)
                    nc.vector.tensor_copy(mask[:, :], mask32).then_inc(f_consts, 1)
                    nc.vector.tensor_copy(ident16[:, :], ident[:, :]).then_inc(f_consts, 1)

            def a_body(i, turn, beside=None):
                for s, slot, p, tile, g in steps(i, turn, layer_constants if turn == "first" else beside):
                    if tile == 0 and g == 1 and prepares(turn, p):
                        gate_weights(PAIR * i + p + 1)
                    if tile == 1 and g == 0 and prepares(turn, p):
                        gated(PAIR * i + p + 1)
                    if g == 1:
                        summed(i, turn, s)
                    if exists(turn, s):
                        n = A_STEPS * i + s
                        e, m = E[s % E_RING], mx[s % 2]
                        both = [banks[2 * (s % 2) + k] for k in range(2)]
                        dve.wait_ge(scored, n + 1)
                        for k in range(2):
                            ins = nc.vector.tensor_reduce(m[:, 2 * k:2 * k + 2, :], both[k][:, :].rearrange("p (h c k) -> p h c k", h=2, c=CHUNKS),
                                                          AX.X, ALU.max)
                            ins.then_inc(max_set, 1)
                        wait(dve, wT_made, 2 * (n - E_RING) + 2)
                        for k in range(2):
                            dve.wait_ge(max_set, 2 * n + k + 1)
                            ins = nc.vector.tensor_tensor(
                                e[:, 2 * k:2 * k + 2, :, :], both[k][:, :].rearrange("p (h c k) -> p h c k", h=2, c=CHUNKS),
                                m[:, 2 * k:2 * k + 2, :].unsqueeze(3).broadcast_to([P, 2, CHUNKS, CHUNK]), ALU.subtract)
                        ins.then_inc(sub_done, 1)
                    if tile == 0 and g == 2 and prepares(turn, p):
                        gate_logit(PAIR * i + p + 1, p + 1, turn)
                    if g != 1:
                        summed(i, turn, s)
                    if prepares(turn, p):
                        b = PAIR * i + p + 1
                        if tile == 0 and g == 2:
                            convolution(b)
                    if g == OUT_LAG % A_KV and exists(turn, s, OUT_LAG):
                        at = (s - OUT_LAG) // A_KV
                        j, r = A_SLOTS * i + at, at % 2
                        dve.wait_ge(made["out"], j + 1)
                        dve.wait_ge(xr_in[(at // TILES) % 2], 16 * (i + at // TILES // PAIR + 1))
                        nc.vector.tensor_tensor(y[r][:, :], banks[6 + A_BANKS.bank("out", at, "middle")][:, 0:DIM],
                                                xr[(at // TILES) % 2][:, at % TILES, :], ALU.add).then_inc(read["out"], 1)
                        dve.wait_ge(read["out"], j + 1)
                        nc.vector.bn_stats(stat[r][:, :], y[r][:, :]).then_inc(y_step, 1)
                        dve.wait_ge(y_step, 2 * j + 1)
                        dve.sem_inc(stats_waited, 1)
                        nc.vector.bn_aggr(mv[r][:, :], stat[r][:, :]).then_inc(y_step, 1)
                    if g == LN_LAG % A_KV and exists(turn, s, LN_LAG):
                        at = (s - LN_LAG) // A_KV
                        j, r = A_SLOTS * i + at, at % 2
                        dve.wait_ge(rstd_set, j + 1)
                        wait(dve, xo_out[r], 16 * (2 * i + at // 2))
                        nc.vector.tensor_scalar(xo[r][:, :], y[r][:, :], mv[r][:, 0:1], rstd[r][:, 1:2],
                                                ALU.subtract, ALU.mult).then_inc(xo_set, 1)

            stage_a(dve, a_body, pre)

            def layers_program():
                HALF = F_HD // 2

                def rotate(it, local, m, turn, layer):
                    index = F_BANKS.stride["qk"] * it + local
                    tile, kind = divmod(m, 2)
                    x = raw[m % 2]

                    def tab(k, lo, hi):
                        return table[layer][:, tile, 2 * kind + k, lo:hi].unsqueeze(1).broadcast_to([P, F_HEADS, hi - lo])

                    dve.wait_ge(f_read["qk"], index + 1)
                    wait(dve, added, index - 1)
                    nc.vector.tensor_tensor(on_self[m % 2][:, :, :], x[:, :, :], tab(0, 0, F_HD), ALU.mult)
                    nc.vector.tensor_tensor(on_partner[m % 2][:, :, 0:HALF], x[:, :, HALF:F_HD], tab(1, 0, HALF), ALU.mult)
                    nc.vector.tensor_tensor(on_partner[m % 2][:, :, HALF:F_HD], x[:, :, 0:HALF], tab(1, HALF, F_HD),
                                            ALU.mult).then_inc(rotated, 1)
                    dve.wait_ge(squared, index + 1)
                    nc.vector.tensor_reduce(norm2[:, 0, F_HEADS * m:F_HEADS * (m + 1)],
                                            sq[m % 2][:, :].rearrange("p (h d) -> p h d", h=F_HEADS), AX.X, ALU.add).then_inc(norm_step, 1)
                    if m % 2 == 1:
                        dve.wait_ge(norm_step, index + 1)
                        wait(dve, rnorm_set, TILES * (PAIR * it + local // 4 - 1) + tile + 1)
                        at = slice(F_HEADS * (m - 1), F_HEADS * (m + 1))
                        nc.vector.tensor_scalar_max(norm2[:, 1, at], norm2[:, 0, at], 1e-24).then_inc(guarded, 1)

                def stats(x, st, out, bn, done, count):
                    for tile in range(TILES):
                        nc.vector.bn_stats(st[:, tile, :], x[:, tile, :]).then_inc(bn, 1)
                    dve.wait_ge(bn, TILES * (count + 1))
                    dve.sem_inc(stats_waited, 1)
                    for tile in range(TILES):
                        nc.vector.bn_aggr(out[:, tile, :], st[:, tile, :]).then_inc(done, 1)

                def normalised(par, bb):
                    dve.wait_ge(m_rstd, bb + 1)
                    for tile in range(TILES):
                        ins = nc.vector.tensor_scalar(hc[par][:, tile, :], mn[par][:, tile, :], mmv[par][:, tile, 0:1],
                                                      mrstd[par][:, 1, tile:tile + 1], ALU.subtract, ALU.mult)
                    ins.then_inc(hc_set, 1)

                def gated_product(c, bank, col, par, bb, layer):
                    rows = F_ROWS[c]
                    dve.wait_ge(gelu_done, F_CHUNKS * bb + c + 1)
                    ins = nc.vector.scalar_tensor_tensor(uT[par][0:rows, c, :], bank[0:rows, col:col + SEQ],
                                                         b1[layer][0:rows, 0, c:c + 1], ge[c][0:rows, :], ALU.add, ALU.mult)
                    return ins.then_inc(u_done, 1)

                def mlp_fill(kind, it, local, layer):
                    par, bb, turn_of = local % PAIR, PAIR * it + local, local // PAIR
                    b, last_layer = bb - BATCH * layer, layer == LAYERS - 1
                    bank = banks[6 + F_BANKS.bank(kind, local, "middle")]
                    dve.wait_ge(f_made[kind], bb + 1)
                    if kind == "mT":
                        nc.vector.tensor_scalar(hT2[par][:, :], bank[:, 0:SEQ], ln_g[layer][:, 0:1], ln_b[layer][:, 0:1],
                                                ALU.mult, ALU.add).then_inc(f_read["mT"], 1)
                    if kind == "mix":
                        gated_product(F_CHUNKS - 1, bank, 0, par, bb, layer)
                    if kind == "values":
                        for c in range(F_CHUNKS - 1):
                            gated_product(c, bank, SEQ * c, par, bb, layer)
                    if kind == "down":
                        dve.wait_ge(resb_step, BATCH * layer + 2 * b + 2 if last_layer else bb + 1)
                        wait(dve, m_out[par], 16 * (it + turn_of))
                        nc.vector.tensor_tensor(yo[par][:, :, :], bank[:, 0:TILES * DIM].rearrange("p (t d) -> p t d", t=TILES),
                                                resb[par][:, 1 if last_layer else 0, :, :], ALU.add).then_inc(f_read["down"], 1)
                        if last_layer:
                            dve.wait_ge(f_read["down"], bb + 1)
                            stats(yo[par], zstat[par], zmv[par], z_bn, z_stats, b)

                def low_part(it, local, turn):
                    dve.wait_ge(hT_rounded, PAIR * it + local + 1)
                    nc.vector.tensor_tensor(fhT_low[:, :], f_bank("hT", local, turn)[:, 0:SEQ],
                                            fhT_high[:, :].bitcast(FP32), ALU.subtract).then_inc(f_read["hT"], 1)

                def shared_fill(kind, local, m, it, turn, layer):
                    if kind == "hT":
                        low_part(it, local, turn)
                    if kind == "qk":
                        rotate(it, local, m, turn, layer)
                    if kind == "out":
                        at = local
                        j, r = F_SLOTS * it + at, at % 2
                        dve.wait_ge(f_made["out"], j + 1)
                        dve.wait_ge(res_in[(at // TILES) % PAIR], 16 * (it + at // TILES // PAIR + 1))
                        wait(dve, f_out[r], 16 * (2 * it + at // 2))
                        nc.vector.tensor_tensor(xo[r][:, :], banks[6 + F_BANKS.bank("out", at, "middle")][:, 0:DIM],
                                                res[(at // TILES) % PAIR][:, at % TILES, :], ALU.add).then_inc(f_read["out"], 1)
                    if kind in ("mT", "mix", "values", "down"):
                        mlp_fill(kind, it, local, layer)

                def sums_of_exponentials(s, n, turn):
                    if f_exists(turn, s, F_SUM_LAG):
                        nn, r = n - F_SUM_LAG, (s - F_SUM_LAG) % 2
                        n_keys, _ = keys((s - F_SUM_LAG) // F_GROUPS % TILES)
                        dve.wait_ge(f_exp, nn + 1)
                        nc.vector.tensor_reduce(f_sum[r][:, :, :], fE[(s - F_SUM_LAG) % F_RING][:, :, :, 0:n_keys], AX.X, ALU.add).then_inc(f_sum_set, 1)
                        dve.wait_ge(f_sum_set, nn + 1)
                        wait(dve, f_normed, nn - 1)
                        nc.vector.reciprocal(f_rsum[r][:, :, :], f_sum[r][:, :, :]).then_inc(f_rsum_set, 1)

                def pre():
                    def beside(s):
                        fill = first_fill(s)
                        if fill and fill[0] == "hT":
                            low_part(0, fill[1], "pre")
                        if fill and fill[0] == "qk":
                            rotate(0, fill[1], fill[1], "pre", 0)

                    a_body(TURNS, "drain", beside)

                def body(it, turn, layer_of):
                    for s, slot, p, tile, g in f_steps(turn):
                        n = F_STEPS * it + s
                        if f_exists(turn, s):
                            n_keys, _ = keys(tile)
                            e, m = fE[s % F_RING], fmx[s % 2]
                            both = [banks[2 * (s % 2) + k][:, 0:2 * n_keys].rearrange("p (a k) -> p a k", a=2) for k in range(2)]
                            dve.wait_ge(f_scored, n + 1)
                            for k in range(2):
                                nc.vector.tensor_reduce(m[:, k, :], both[k], AX.X, ALU.max).then_inc(f_max, 1)
                            wait(dve, eT_made, n - F_RING + 1)
                            for k in range(2):
                                dve.wait_ge(f_max, 2 * n + k + 1)
                                ins = nc.vector.tensor_tensor(e[:, k, :, 0:n_keys], both[k],
                                                              m[:, k, :].unsqueeze(2).broadcast_to([P, 2, n_keys]), ALU.subtract)
                            ins.then_inc(f_sub, 1)
                        awaited = ("out", "down")
                        for summing in (False, True):
                            if summing:
                                sums_of_exponentials(s, n, turn)
                            for kind, local, m, ahead in f_fills(turn, s):
                                if summing != (kind in awaited):
                                    shared_fill(kind, local, m, it, turn, layer_of(local // (F_BANKS.stride[kind] // PAIR)))
                        local = f_late(turn, s, "stats")
                        if local is not None:
                            par = local % PAIR
                            dve.wait_ge(mn_in[par], 64 * (it + local // PAIR + 1))
                            stats(mn[par], mstat[par], mmv[par], m_bn, m_stats, PAIR * it + local)
                        local = f_late(turn, s, "norm")
                        if local is not None:
                            normalised(local % PAIR, PAIR * it + local)
                        local = f_late(turn, s, "z")
                        if local is not None and layer_of(local) == LAYERS - 1:
                            par = local % PAIR
                            dve.wait_ge(z_rstd, PAIR * it + local + 1 - BATCH * (LAYERS - 1))
                            wait(dve, m_out[par], 16 * (it + local // PAIR))
                            for t2 in range(TILES):
                                ins = nc.vector.tensor_scalar(zo[par][:, t2, :], yo[par][:, t2, :], zmv[par][:, t2, 0:1],
                                                              zrstd[par][:, 1, t2:t2 + 1], ALU.subtract, ALU.mult)
                            ins.then_inc(z_set, 1)

                both_layers(dve, body, pre)

            layers_program()

        @block.tensor
        def _(pe):
            def transpose_x(i, local, turn, b):
                bank_free(pe, A_BANKS, read, "xT", local, i, turn)
                pe.wait_ge(xn_in[local % 2], 16 * (i + local // 2 + 1))
                bank = banks[6 + A_BANKS.bank("xT", local, turn)]
                for tt in range(TILES):
                    ins = nc.tensor.transpose(bank[:, P * tt:P * (tt + 1)], xn[local % 2][:, tt, :], ident[:, :])
                ins.then_inc(made["xT"], 1)

            def gate_matmul(i, local, turn, b):
                bank_free(pe, A_BANKS, read, "gate", local, i, turn)
                pe.wait_ge(wk_ctx_set, b + 1)
                nc.tensor.matmul(banks[6 + A_BANKS.bank("gate", local, turn)][:, 0:KS], ones[:, :], wk_ctx[:, :],
                                 start=True, stop=True).then_inc(made["gate"], 1)

            def project(kind, i, local, turn, m, b):
                bank_free(pe, A_BANKS, read, kind, local, i, turn)
                pe.wait_ge(hT_set, b + 1)
                bank = banks[6 + A_BANKS.bank(kind, local, turn)]
                for k in range(2):
                    dst = bank[:, 256 * k:256 * (k + 1)]
                    if kind == "q":
                        ins = nc.tensor.matmul(dst, wq[:, P * (2 * m + k):P * (2 * m + k + 1)], hT[:, :], start=True, stop=True)
                    elif kind == "k":
                        ins = nc.tensor.matmul(dst, wk[:, P * k:P * (k + 1)], hT[:, :], start=True, stop=True)
                    else:
                        ins = nc.tensor.matmul(dst, hT[:, P * k:P * (k + 1)], wv[:, :], start=True, stop=True)
                ins.then_inc(made[kind], 1)

            def pre():
                pe.wait_ge(gate_weights_in, 16 * N_GATE_WEIGHTS)
                pe.wait_ge(consts_set, N_CONSTS)
                transpose_x(0, 0, "pre", 0)
                gate_matmul(0, 0, "pre", 0)
                pe.wait_ge(a_weights_in, 16 * N_A_WEIGHTS)
                for kind, local in A_BANKS.pre[2:]:
                    project(kind, 0, local, "pre", local, 0)

            def a_body(i, turn, beside=None):
                for s, slot, p, tile, g in steps(i, turn, beside):
                    late = exists(turn, s, PV_LAG)
                    if late:
                        n = A_STEPS * i + s - PV_LAG
                        e = E[(s - PV_LAG) % E_RING]
                        pe.wait_ge(normed, n + 1)
                        for hp in range(2):
                            wait(pe, wT_read, 2 * (n - 1) + hp + 1)
                            for kb in range(TILES):
                                for hh in range(2):
                                    ins = nc.tensor.transpose(banks[4 + hp][:, P * (2 * kb + hh):P * (2 * kb + hh + 1)],
                                                              e[:, 2 * hh + hp, 2 * kb:2 * kb + 2, :], ident[:, :])
                            ins.then_inc(wT_made, 1)
                    if exists(turn, s):
                        n = A_STEPS * i + s
                        if g == 0:
                            b = PAIR * i + p
                            pe.wait_ge(read["q"], 4 * b + 4)
                            pe.wait_ge(read["k"], b + 1)
                        wait(pe, sub_done, n - 1)
                        for h in range(A_REP):
                            lo = A_HD * (h % 2)
                            ins = nc.tensor.matmul(
                                banks[2 * (s % 2) + h % 2][:, SEQ * (h // 2):SEQ * (h // 2 + 1)],
                                qT[p][lo:lo + A_HD, 2 * g + h // 2, P * tile:P * (tile + 1)],
                                kT[p][lo:lo + A_HD, g, :], start=True, stop=True)
                        ins.then_inc(scored, 1)
                    if prepares(turn, p):
                        b = PAIR * i + p + 1
                        if tile == 0 and g == 0:
                            transpose_x(i, p + 1, turn, b)
                        if tile == 0 and g == 2:
                            gate_matmul(i, p + 1, turn, b)
                        if tile == 1:
                            for kind, per, m in A_PROJECTIONS[g]:
                                project(kind, i, per * (p + 1) + m, turn, m, b)
                    if late:
                        n = A_STEPS * i + s - PV_LAG
                        at, og = divmod(s - PV_LAG, A_KV)
                        ap = (at // TILES) % PAIR
                        bank = banks[6 + A_BANKS.bank("o", s - PV_LAG, "middle")]
                        bank_free(pe, A_BANKS, read, "o", s - PV_LAG, i, turn)
                        if og == 0:
                            pe.wait_ge(read["v"], PAIR * i + at // TILES + 1)
                        for hp in range(2):
                            pe.wait_ge(wT_read, 2 * n + hp + 1)
                            for kb in range(TILES):
                                for hh in range(2):
                                    ins = nc.tensor.matmul(
                                        bank[A_HD * hh:A_HD * (hh + 1), P * hp:P * (hp + 1)],
                                        v[ap][:, kb, A_HD * og:A_HD * (og + 1)], wT[hp][:, kb, hh, :],
                                        start=(kb == 0), stop=(kb == TILES - 1))
                            ins.then_inc(pv_done, 1)
                    if g == OUT_LAG % A_KV and exists(turn, s, OUT_LAG):
                        at = (s - OUT_LAG) // A_KV
                        j = A_SLOTS * i + at
                        bank_free(pe, A_BANKS, read, "out", at, i, turn)
                        pe.wait_ge(read["o"], A_KV * j + A_KV)
                        for m in range(A_HEADS // 2):
                            ins = nc.tensor.matmul(banks[6 + A_BANKS.bank("out", at, "middle")][:, 0:DIM], oT[at % 2][:, m, :], wo[:, m, :],
                                                   start=(m == 0), stop=(m == A_HEADS // 2 - 1))
                        ins.then_inc(made["out"], 1)

            stage_a(pe, a_body, pre)

            def layers_program():
                free = lambda kind, local, it, turn: bank_free(pe, F_BANKS, f_read, kind, local, it, turn)

                def prepare(it, kind, local, m, batch, turn, layer):
                    par = (local // (F_BANKS.stride[kind] // PAIR)) % PAIR
                    bank = f_bank(kind, local, turn)
                    if turn != "pre":
                        free(kind, local, it, turn)
                    elif (kind, local) in F_BANKS.pre[4:]:
                        before, index = F_BANKS.pre[F_BANKS.pre.index((kind, local)) - 4]
                        pe.wait_ge(f_read[before], index + 1)
                    if kind == "hT":
                        pe.wait_ge(hn_in[par], 64 * (it + local // PAIR + 1))
                        for tt in range(TILES):
                            ins = nc.tensor.transpose(bank[:, P * tt:P * (tt + 1)], hn[par][:, tt, :], ident[:, :])
                    elif kind in ("qk", "v"):
                        tile, k = divmod(m, 2) if kind == "qk" else (m, 2)
                        pe.wait_ge(f_read["hT"], batch + 1)
                        tokens, cols = slice(P * tile, P * (tile + 1)), slice(INNER * k, INNER * (k + 1))
                        parts = ((fhT_high, wqkv_high), (fhT_high, wqkv_low), (fhT_low, wqkv_high))
                        for at, (h_part, w_part) in enumerate(parts):
                            ins = nc.tensor.matmul(bank[:, :], h_part[:, tokens], w_part[layer][:, cols], start=(at == 0), stop=(at == 2))
                    else:
                        pe.wait_ge(qk_normed, F_BANKS.stride[kind] * it + local + 1)
                        flat = qk[m][:, :, :].rearrange("p h d -> p (h d)")
                        for block_of in range(4):
                            ins = nc.tensor.transpose(bank[:, P * block_of:P * (block_of + 1)],
                                                      flat[:, P * block_of:P * (block_of + 1)], ident[:, :])
                    ins.then_inc(f_made[kind], 1)

                def mlp_fill(kind, it, local, layer):
                    par, bb = local % PAIR, PAIR * it + local
                    bank = banks[6 + F_BANKS.bank(kind, local, "middle")]

                    def hidden(a, c, col):
                        at, rows = F_HID * a + P * c, F_ROWS[c]
                        return nc.tensor.matmul(bank[0:rows, col:col + SEQ], w1[layer][:, at:at + rows], hT2[par][:, :], start=True, stop=True)

                    if kind == "mT":
                        pe.wait_ge(hc_set, bb + 1)
                        for tile in range(TILES):
                            ins = nc.tensor.transpose(bank[:, P * tile:P * (tile + 1)], hc[par][:, tile, :], ident[:, :])
                    if kind == "gates":
                        pe.wait_ge(f_read["mT"], bb + 1)
                        for c in range(F_CHUNKS - 1):
                            ins = hidden(1, c, SEQ * c)
                    if kind == "mix":
                        for a in range(2):
                            ins = hidden(a, F_CHUNKS - 1, SEQ * a)
                    if kind == "values":
                        for c in range(F_CHUNKS - 1):
                            ins = hidden(0, c, SEQ * c)
                    if kind == "down":
                        pe.wait_ge(u_done, F_CHUNKS * (bb + 1))
                        for tile in range(TILES):
                            for c, rows in enumerate(F_ROWS):
                                ins = nc.tensor.matmul(bank[:, DIM * tile:DIM * (tile + 1)],
                                                       uT[par][0:rows, c, P * tile:P * (tile + 1)], w2[layer][0:rows, c, :],
                                                       start=(c == 0), stop=(c == F_CHUNKS - 1))
                    ins.then_inc(f_made[kind], 1)

                def pre():
                    def beside(s):
                        if s == 0:
                            pe.wait_ge(weights_in, 16 * N_WEIGHTS)
                            pe.wait_ge(weights_split, 3 * LAYERS)
                            pe.wait_ge(sub_done, A_STEPS * TURNS)
                        fill = first_fill(s)
                        if fill:
                            kind, local = fill
                            per = F_BANKS.stride[kind] // PAIR
                            prepare(0, kind, local, local % per, local // per, "pre", 0)

                    a_body(TURNS, "drain", beside)
                    pe.wait_ge(f_consts, N_F_CONSTS)
                    pe.wait_ge(read["out"], BATCH * TILES)
                    for kind in ("v", "qkT", "hT"):
                        pe.wait_ge(f_read[kind], 2)

                def shared_fill(kind, local, m, batch, it, turn, layer_of):
                    layer = layer_of(local // (F_BANKS.stride[kind] // PAIR))
                    if kind in ("hT", "qk", "v", "qkT"):
                        prepare(it, kind, local, m, batch, turn, layer)
                        return
                    free(kind, local, it, turn)
                    if kind != "out":
                        mlp_fill(kind, it, local, layer)
                        return
                    j = F_SLOTS * it + local
                    bank = banks[6 + F_BANKS.bank(kind, local, "middle")]
                    pe.wait_ge(f_o_read, F_GROUPS * j + F_GROUPS)
                    for m in range(INNER // P):
                        ins = nc.tensor.matmul(bank[:, 0:DIM], foT[local % 2][:, m, :], wof[layer][:, m, :],
                                               start=(m == 0), stop=(m == INNER // P - 1))
                    ins.then_inc(f_made[kind], 1)

                def body(it, turn, layer_of):
                    for s, slot, p, tile, g in f_steps(turn):
                        n = F_STEPS * it + s
                        late = f_exists(turn, s, F_PV_LAG)
                        late_slot, late_g = divmod(s - F_PV_LAG, F_GROUPS)
                        late_p, late_tile = (late_slot // TILES) % PAIR, late_slot % TILES
                        if late:
                            pe.wait_ge(f_normed, n - F_PV_LAG + 1)
                            wait(pe, eT_read, n - F_PV_LAG)
                            e = fE[(s - F_PV_LAG) % F_RING]
                            own = keys(late_tile)[0] - P
                            if late_tile == 1:
                                wait(pe, f_o_read, n - F_PV_LAG)
                                wait(pe, back_read, F_GROUPS * (PAIR * it + late_slot // TILES) + late_g)
                            for h in range(F_GH):
                                ins = nc.tensor.transpose(banks[4][:, P * h:P * (h + 1)], e[:, h % 2, h // 2, own:own + P], ident[:, :])
                            if late_tile == 1:
                                for h in range(F_GH):
                                    ins = nc.tensor.transpose(banks[5][0:WINDOW, P * h:P * (h + 1)], e[:, h % 2, h // 2, 0:own], ident[:, :])
                            ins.then_inc(eT_made, 1)
                        if f_exists(turn, s):
                            n_keys, first_key = keys(tile)
                            if g == 0:
                                pe.wait_ge(f_read["qkT"], 4 * (PAIR * it + p) + 2 * tile + 2)
                            wait(pe, f_sub, n - 1)
                            m0 = 2 * P * tile
                            for k in range(2):
                                nc.tensor.matmul(banks[2 * (s % 2) + k][:, 0:2 * n_keys], ident16[:, :], mask[:, m0:m0 + 2 * n_keys],
                                                 start=True, stop=False)
                            for h in range(F_GH):
                                head = F_GH * g + h
                                lo = F_HD * (h % 2)
                                ins = nc.tensor.matmul(
                                    banks[2 * (s % 2) + h % 2][:, n_keys * (h // 2):n_keys * (h // 2 + 1)],
                                    qkT[p][lo:lo + F_HD, head // 2, P * tile:P * (tile + 1)],
                                    qkT[p][lo:lo + F_HD, 4 + head // 2, first_key:first_key + n_keys],
                                    start=False, stop=(h >= 2))
                            ins.then_inc(f_scored, 1)
                        fills = list(f_fills(turn, s))
                        for kind, local, m, ahead in fills[:1]:
                            shared_fill(kind, local, m, PAIR * it + p + ahead, it, turn, layer_of)
                        if late:
                            bank = banks[5]
                            wait(pe, f_o_read, n - F_PV_LAG)
                            if late_g == 0:
                                pe.wait_ge(f_read["v"], 2 * (PAIR * it + late_slot // TILES) + late_tile + 1)
                            pe.wait_ge(eT_read, n - F_PV_LAG + 1)
                            if late_tile == 1:
                                pe.wait_ge(back_read, F_GROUPS * (PAIR * it + late_slot // TILES) + late_g + 1)
                            for pair in range(F_GH // 2):
                                for back in range(late_tile + 1):
                                    for hh in range(2):
                                        h = 2 * pair + hh
                                        ins = nc.tensor.matmul(bank[F_HD * hh:F_HD * (hh + 1), P * pair:P * (pair + 1)],
                                                               f_v[late_p][:, late_tile - back, F_GH * late_g + h, :],
                                                               (eT_back if back else eT)[:, h, :], start=(back == 0), stop=(back == late_tile))
                            ins.then_inc(f_o_made, 1)
                        for kind, local, m, ahead in fills[1:]:
                            shared_fill(kind, local, m, PAIR * it + p + ahead, it, turn, layer_of)

                both_layers(pe, body, pre)

            layers_program()


def rotary_tables():
    f32 = np.float32
    half = np.arange(0, F_HD, 2, dtype=f32)
    inv_freq = f32(1.0) / np.power(f32(10000.0), half / f32(F_HD)).astype(f32)
    tok = np.arange(SEQ, dtype=f32)
    freqs = tok[:, None] * inv_freq[None, :]
    freqs = np.concatenate([freqs, freqs], axis=-1)
    base = (half + f32(0.4 * F_HD)) / f32(1.4 * F_HD)
    power = (tok - SEQ // 2) / f32(WINDOW // 2)
    scale = np.power(base[None, :].astype(np.float64), power[:, None].astype(np.float64))
    scale = np.concatenate([scale, scale], axis=-1)
    cos, sin = np.cos(freqs.astype(np.float64)), np.sin(freqs.astype(np.float64))
    sin = sin * np.where(np.arange(F_HD) < F_HD // 2, -1.0, 1.0)
    tabs = np.stack([cos * scale * QK_SCALE, sin * scale * QK_SCALE, cos / scale, sin / scale], axis=1)
    return tabs.astype(f32)


def score_mask():
    q, own = np.arange(P)[:, None], np.arange(P)[None, :]
    first = (own <= q) & (own >= q - WINDOW)
    key = np.arange(F_KEYS)[None, :] - WINDOW
    second = (key <= q) & (key >= q - WINDOW)
    return np.where(np.concatenate([first, first, second, second], axis=1), 0.0, MASKED).astype(np.float32)


def kernel(**inputs):
    import concourse.bacc as bacc
    from concourse.bass_utils import run_bass_kernel_spmd

    nc = bacc.Bacc("TRN2", target_bir_lowering=False, num_devices=1)
    f = {k: np.asarray(a) for k, a in inputs.items()}
    arrays = {
        "x": f["L0_attn_hidden_states"],
        "wqT": f["L0_attn_w_q"].T, "wkT": f["L0_attn_w_k"].T, "wvT": f["L0_attn_w_v"].T, "woT": f["L0_attn_w_o"].T,
        "wkgenT": f["L0_attn_w_kgen"].T, "bkgen": f["L0_attn_b_kgen"],
        "wconv": f["L0_attn_w_conv"].reshape(DIM, KS), "bconv": f["L0_attn_b_conv"],
        "wqkv": f["L0_ffn_wqkv"], "q_scale": f["L0_ffn_q_scale"], "k_scale": f["L0_ffn_k_scale"], "wof": f["L0_ffn_wo"],
        "ln_g": f["L0_ffn_ln_g"], "ln_b": f["L0_ffn_ln_b"], "w1": f["L0_ffn_w1"], "b1": f["L0_ffn_b1"],
        "w2": f["L0_ffn_w2"], "b2": f["L0_ffn_b2"],
        "eye": np.eye(P, dtype=np.float32), "rotary": rotary_tables(), "mask": score_mask(),
    }
    arrays = {f"in_{k}": np.ascontiguousarray(a) for k, a in arrays.items()}
    t = {k[3:]: nc.dram_tensor(k, a.shape, mybir.dt.from_np(a.dtype), kind="ExternalInput").ap() for k, a in arrays.items()}
    for name in ("x1", "x2", "x3", "x4"):
        t[name] = nc.dram_tensor(f"stage_{name}", (BATCH, SEQ, DIM), FP32, kind="Internal").ap()
    t["out"] = nc.dram_tensor("out_x", (BATCH, SEQ, DIM), FP32, kind="ExternalOutput").ap()
    build(nc, t)
    r = run_bass_kernel_spmd(nc, [arrays], core_ids=[0])
    return r.results[0]["out_x"]
```
